# Optimizing a Trainium2 kernel written in Bass

```python
import numpy as np
import jax
import jax.numpy as jnp

def _softmax(x, axis=-1):
    return jax.nn.softmax(x, axis=axis)

def _gelu(x):
    return jax.nn.gelu(x, approximate=True)

def _silu(x):
    return jax.nn.silu(x)

def _sigmoid(x):
    return jax.nn.sigmoid(x)

def _layernorm(x, axis=-1, eps=1e-05):
    m = jnp.mean(x, axis=axis, keepdims=True)
    v = jnp.var(x, axis=axis, keepdims=True)
    return (x - m) / jnp.sqrt(v + eps)

def _scatter_add(tgt, idx, src, axis=0):
    return tgt.at[idx].add(src)

def _segment_sum(src, seg, n):
    return jax.ops.segment_sum(src, seg, n)
kernel_name = 'mk_decoder_postln_d2_seqx_r8_d5aba8'

def setup_inputs(seed: int=0):
    np.random.seed(seed)
    _w = jnp.asarray

    def _rec_inputs():
        import jax
        import jax.numpy as jnp
        _rk = jax.random.key(seed)
        x = 7.22e-05 + 1 * jax.random.normal(jax.random.fold_in(_rk, 1), (4, 256, 256), jnp.float32)
        _lenS = 256 - jax.random.randint(jax.random.fold_in(_rk, 7), (4,), 0, max(1, 256 // 4) + 1, jnp.int32)
        _lenS2 = 256 - jax.random.randint(jax.random.fold_in(_rk, 8), (4,), 0, max(1, 256 // 4) + 1, jnp.int32)
        _ctx_512P = jax.random.normal(jax.random.fold_in(_rk, 11), (4, 16, 64), jnp.float32)
        _ctx_512c = jax.random.dirichlet(jax.random.fold_in(_rk, 511), 0.3 * jnp.ones((16,), jnp.float32), (4, 256))
        _ctx_512t = jnp.einsum('bsk,bkd->bsd', _ctx_512c, _ctx_512P)
        _ctx_512t = _ctx_512t * jax.lax.rsqrt(jnp.mean(jnp.square(_ctx_512t)) + 1e-12) * 0.953939
        ctx_512 = -0.000514642 + 1.00011 * (_ctx_512t + 0.3 * jax.random.normal(jax.random.fold_in(_rk, 611), (4, 256, 64), jnp.float32))
        return (x, ctx_512)
    x, ctx_512 = _rec_inputs()

    def _L0_attn_setup():
        import jax, jax.numpy as jnp
        import numpy as np
        H, HKV, HD = (16, 4, 128)

        def _rope(x, cos, sin):
            xr = x.reshape(*x.shape[:-1], HD // 2, 2)
            a, b = (xr[..., 0], xr[..., 1])
            c = cos[None, :, None, :]
            s = sin[None, :, None, :]
            return jnp.stack([a * c - b * s, a * s + b * c], axis=-1).reshape(x.shape)
        key = jax.random.key(seed)
        ks = jax.random.split(key, 5)
        B, T, C = (2, 256, 256)
        std = 0.02
        return {'x': jax.random.normal(ks[0], (B, T, C), jnp.float32), 'Wq': jax.random.normal(ks[1], (C, H * HD), jnp.float32) * std, 'bq': jnp.zeros((H * HD,), jnp.float32), 'Wk': jax.random.normal(ks[2], (C, HKV * HD), jnp.float32) * std, 'bk': jnp.zeros((HKV * HD,), jnp.float32), 'Wv': jax.random.normal(ks[3], (C, HKV * HD), jnp.float32) * std, 'bv': jnp.zeros((HKV * HD,), jnp.float32), 'Wo': jax.random.normal(ks[4], (H * HD, C), jnp.float32) * std, 'bo': jnp.zeros((C,), jnp.float32)}
    _L0_attn_all = _L0_attn_setup()
    _L0_attn_in = {k: v for k, v in _L0_attn_all.items() if k in ('Wq', 'bq', 'Wk', 'bk', 'Wv', 'bv', 'Wo', 'bo')}
    del _L0_attn_all

    def _L0_xattn_setup():
        import jax, jax.numpy as jnp
        import numpy as np
        import math
        NUM_Q_HEADS = 32
        NUM_KV_HEADS = 8
        key = jax.random.key(seed)
        k1, k2, k3 = jax.random.split(key, 3)
        B, S, E = (2, 256, 256)
        kv_E = NUM_KV_HEADS * (E // NUM_Q_HEADS)
        q = jax.random.normal(k1, (B, S, E), dtype=jnp.float32)
        k = jax.random.normal(k2, (B, S, kv_E), dtype=jnp.float32)
        v = jax.random.normal(k3, (B, S, kv_E), dtype=jnp.float32)
        return {'q': q, 'k': k, 'v': v}
    _L0_xattn_all = _L0_xattn_setup()
    _L0_xattn_in = {k: v for k, v in _L0_xattn_all.items() if k in ()}
    del _L0_xattn_all

    def _L0_ffn_setup():
        import jax, jax.numpy as jnp
        import numpy as np
        HID = 256
        N_EXP = 32
        F_EXP = 96
        TOP_K = 6
        F_SH = 192
        B, S = (1, 128)
        key = jax.random.key(seed)
        ks = jax.random.split(key, 8)
        s = 0.02
        return {'hidden_states': jax.random.normal(ks[0], (B, S, HID), dtype=jnp.float32), 'gate_w': jax.random.normal(ks[1], (HID, N_EXP), dtype=jnp.float32) * s, 'wg': jax.random.normal(ks[2], (N_EXP, HID, F_EXP), dtype=jnp.float32) * s, 'wu': jax.random.normal(ks[3], (N_EXP, HID, F_EXP), dtype=jnp.float32) * s, 'wd': jax.random.normal(ks[4], (N_EXP, F_EXP, HID), dtype=jnp.float32) * s, 'sg': jax.random.normal(ks[5], (HID, F_SH), dtype=jnp.float32) * s, 'su': jax.random.normal(ks[6], (HID, F_SH), dtype=jnp.float32) * s, 'sd': jax.random.normal(ks[7], (F_SH, HID), dtype=jnp.float32) * s}
    _L0_ffn_all = _L0_ffn_setup()
    _L0_ffn_in = {k: v for k, v in _L0_ffn_all.items() if k in ('gate_w', 'wg', 'wu', 'wd', 'sg', 'su', 'sd')}
    del _L0_ffn_all

    def _L1_attn_setup():
        import math
        import jax, jax.numpy as jnp
        import numpy as np
        H, KV, D = (16, 4, 128)
        HID = 256
        ROPE_BASE = 1000000.0
        EPS = 1e-06

        def _layernorm(x, w, b):
            mu = jnp.mean(x, axis=-1, keepdims=True)
            xc = x - mu
            var = jnp.mean(xc * xc, axis=-1, keepdims=True)
            return xc * jax.lax.rsqrt(var + EPS) * w + b

        def _rope(x, cos, sin):
            xr, xi = (x[..., 0::2], x[..., 1::2])
            c, s = (cos[None, None], sin[None, None])
            out = jnp.stack([xr * c - xi * s, xr * s + xi * c], axis=-1)
            return out.reshape(x.shape)
        key = jax.random.key(seed)
        ks = jax.random.split(key, 3)
        B, S = (2, 256)
        s = 0.02
        return {'x': jax.random.normal(ks[0], (B, S, HID), jnp.float32), 'w_qkv': jax.random.normal(ks[1], (2 * H * D + 2 * KV * D, HID), jnp.float32) * s, 'w_o': jax.random.normal(ks[2], (HID, H * D), jnp.float32) * s, 'q_norm_w': jnp.ones((D,), jnp.float32), 'q_norm_b': jnp.zeros((D,), jnp.float32), 'k_norm_w': jnp.ones((D,), jnp.float32), 'k_norm_b': jnp.zeros((D,), jnp.float32)}
    _L1_attn_all = _L1_attn_setup()
    _L1_attn_in = {k: v for k, v in _L1_attn_all.items() if k in ('w_qkv', 'w_o', 'q_norm_w', 'q_norm_b', 'k_norm_w', 'k_norm_b')}
    del _L1_attn_all

    def _L1_xattn_setup():
        import jax, jax.numpy as jnp
        import numpy as np
        B, N, D = (16, 256, 64)
        H = 4
        TOP_K_RATIO = 0.3
        key = jax.random.key(seed)
        k1, k2, k3, k4 = jax.random.split(key, 4)
        h = jax.random.normal(k1, (B, N, D), dtype=jnp.float32)
        adj_raw = jax.random.uniform(k2, (B, N, N), dtype=jnp.float32)
        lim = 1.0 / np.sqrt(D)
        Wq = jax.random.uniform(k3, (D, D), minval=-lim, maxval=lim, dtype=jnp.float32)
        Wk = jax.random.uniform(k4, (D, D), minval=-lim, maxval=lim, dtype=jnp.float32)
        gamma_raw = jnp.float32(-0.85)
        return {'h': h, 'adj_raw': adj_raw, 'Wq': Wq, 'Wk': Wk, 'gamma_raw': gamma_raw}
    _L1_xattn_all = _L1_xattn_setup()
    _L1_xattn_in = {k: v for k, v in _L1_xattn_all.items() if k in ('Wq', 'Wk', 'gamma_raw')}
    del _L1_xattn_all

    def _L1_ffn_setup():
        import jax, jax.numpy as jnp
        import numpy as np
        B, S, D, H = (4, 256, 256, 1024)

        def fwht(x):
            orig_shape = x.shape
            n = orig_shape[-1]
            x = x.reshape(-1, n)
            h = 1
            while h < n:
                xb = x.reshape(-1, n // (2 * h), 2, h)
                a = xb[:, :, 0, :]
                b = xb[:, :, 1, :]
                x = jnp.stack([a + b, a - b], axis=2).reshape(-1, n)
                h *= 2
            scale = jnp.asarray(1.0 / np.sqrt(n), dtype=x.dtype)
            return (x * scale).reshape(orig_shape)
        key = jax.random.key(seed)
        kx, k1, k2, k3 = jax.random.split(key, 4)
        x = jax.random.normal(kx, (B, S, D), dtype=jnp.float32)
        W1 = jax.random.normal(k1, (H, D), dtype=jnp.float32) * (1.0 / np.sqrt(D))
        W2 = jax.random.normal(k2, (D, H), dtype=jnp.float32) * (1.0 / np.sqrt(H))
        W3 = jax.random.normal(k3, (H, D), dtype=jnp.float32) * (1.0 / np.sqrt(D))
        return {'x': x, 'W1': W1, 'W2': W2, 'W3': W3}
    _L1_ffn_all = _L1_ffn_setup()
    _L1_ffn_in = {k: v for k, v in _L1_ffn_all.items() if k in ('W1', 'W2', 'W3')}
    del _L1_ffn_all
    return {'x': x, 'ctx_512': ctx_512, 'L0_attn_Wq': _L0_attn_in['Wq'], 'L0_attn_bq': _L0_attn_in['bq'], 'L0_attn_Wk': _L0_attn_in['Wk'], 'L0_attn_bk': _L0_attn_in['bk'], 'L0_attn_Wv': _L0_attn_in['Wv'], 'L0_attn_bv': _L0_attn_in['bv'], 'L0_attn_Wo': _L0_attn_in['Wo'], 'L0_attn_bo': _L0_attn_in['bo'], 'L0_ffn_gate_w': _L0_ffn_in['gate_w'], 'L0_ffn_wg': _L0_ffn_in['wg'], 'L0_ffn_wu': _L0_ffn_in['wu'], 'L0_ffn_wd': _L0_ffn_in['wd'], 'L0_ffn_sg': _L0_ffn_in['sg'], 'L0_ffn_su': _L0_ffn_in['su'], 'L0_ffn_sd': _L0_ffn_in['sd'], 'L1_attn_w_qkv': _L1_attn_in['w_qkv'], 'L1_attn_w_o': _L1_attn_in['w_o'], 'L1_attn_q_norm_w': _L1_attn_in['q_norm_w'], 'L1_attn_q_norm_b': _L1_attn_in['q_norm_b'], 'L1_attn_k_norm_w': _L1_attn_in['k_norm_w'], 'L1_attn_k_norm_b': _L1_attn_in['k_norm_b'], 'L1_xattn_Wq': _L1_xattn_in['Wq'], 'L1_xattn_Wk': _L1_xattn_in['Wk'], 'L1_xattn_gamma_raw': _L1_xattn_in['gamma_raw'], 'L1_ffn_W1': _L1_ffn_in['W1'], 'L1_ffn_W2': _L1_ffn_in['W2'], 'L1_ffn_W3': _L1_ffn_in['W3']}

def reference(x, ctx_512, L0_attn_Wq, L0_attn_bq, L0_attn_Wk, L0_attn_bk, L0_attn_Wv, L0_attn_bv, L0_attn_Wo, L0_attn_bo, L0_ffn_gate_w, L0_ffn_wg, L0_ffn_wu, L0_ffn_wd, L0_ffn_sg, L0_ffn_su, L0_ffn_sd, L1_attn_w_qkv, L1_attn_w_o, L1_attn_q_norm_w, L1_attn_q_norm_b, L1_attn_k_norm_w, L1_attn_k_norm_b, L1_xattn_Wq, L1_xattn_Wk, L1_xattn_gamma_raw, L1_ffn_W1, L1_ffn_W2, L1_ffn_W3):
    import jax
    import jax.numpy as jnp

    def _L0_attn_ref(x, Wq, bq, Wk, bk, Wv, bv, Wo, bo):
        import jax, jax.numpy as jnp
        import numpy as np
        H, HKV, HD = (16, 4, 128)

        def _rope(x, cos, sin):
            xr = x.reshape(*x.shape[:-1], HD // 2, 2)
            a, b = (xr[..., 0], xr[..., 1])
            c = cos[None, :, None, :]
            s = sin[None, :, None, :]
            return jnp.stack([a * c - b * s, a * s + b * c], axis=-1).reshape(x.shape)
        B, T, C = x.shape
        G = H // HKV
        q = (x @ Wq + bq).reshape(B, T, H, HD)
        k = (x @ Wk + bk).reshape(B, T, HKV, HD)
        v = (x @ Wv + bv).reshape(B, T, HKV, HD)
        theta = 1.0 / 10000.0 ** (jnp.arange(0, HD, 2, dtype=jnp.float32) / HD)
        freqs = jnp.arange(T, dtype=jnp.float32)[:, None] * theta[None, :]
        cos, sin = (jnp.cos(freqs), jnp.sin(freqs))
        q = _rope(q, cos, sin)
        k = _rope(k, cos, sin)
        q = q.transpose(0, 2, 1, 3).reshape(B, G, HKV, T, HD)
        k = k.transpose(0, 2, 1, 3)
        v = v.transpose(0, 2, 1, 3)
        scale = 1.0 / np.sqrt(H).astype(np.float32)
        scores = jnp.einsum('bgjtd,bjsd->bgjts', q, k) * scale
        mask = jnp.tril(jnp.ones((T, T), dtype=bool))
        scores = jnp.where(mask[None, None, None], scores, -jnp.inf)
        wei = jax.nn.softmax(scores, axis=-1)
        out = jnp.einsum('bgjts,bjsd->bgjtd', wei, v)
        out = out.transpose(0, 3, 1, 2, 4).reshape(B, T, H * HD)
        return out @ Wo + bo

    def _L0_xattn_ref(q, k, v):
        import jax, jax.numpy as jnp
        import numpy as np
        import math
        NUM_Q_HEADS = 32
        NUM_KV_HEADS = 8
        B, S, E = q.shape
        H, KV = (NUM_Q_HEADS, NUM_KV_HEADS)
        D = E // H
        G = H // KV
        scale = math.sqrt(D)
        qh = q.reshape(B, S, KV, G, D).transpose(0, 2, 3, 1, 4)
        kh = k.reshape(B, S, KV, D).transpose(0, 2, 1, 3)
        vh = v.reshape(B, S, KV, D).transpose(0, 2, 1, 3)
        scores = jnp.einsum('bkgsd,bktd->bkgst', qh, kh) / scale
        weights = jax.nn.softmax(scores, axis=-1)
        out = jnp.einsum('bkgst,bktd->bkgsd', weights, vh)
        return out.transpose(0, 3, 1, 2, 4).reshape(B, S, E)

    def _L0_ffn_ref(hidden_states, gate_w, wg, wu, wd, sg, su, sd):
        import jax, jax.numpy as jnp
        import numpy as np
        HID = 256
        N_EXP = 32
        F_EXP = 96
        TOP_K = 6
        F_SH = 192
        B, S = (1, 128)
        orig_shape = hidden_states.shape
        x = hidden_states.reshape(-1, HID)
        scores = jax.nn.sigmoid(x @ gate_w)
        topk_w, topk_i = jax.lax.top_k(scores, TOP_K)
        topk_w = topk_w / (jnp.sum(topk_w, axis=-1, keepdims=True) + 1e-20)
        combine = jnp.sum(jax.nn.one_hot(topk_i, N_EXP, dtype=topk_w.dtype) * topk_w[..., None], axis=1)
        g = jnp.einsum('td,edf->tef', x, wg)
        u = jnp.einsum('td,edf->tef', x, wu)
        act = jax.nn.silu(g) * u
        routed = jnp.einsum('tef,efd,te->td', act, wd, combine)
        routed = routed.reshape(orig_shape)
        shared = jax.nn.silu(hidden_states @ sg) * (hidden_states @ su) @ sd
        return routed + shared

    def _L1_attn_ref(x, w_qkv, w_o, q_norm_w, q_norm_b, k_norm_w, k_norm_b):
        import math
        import jax, jax.numpy as jnp
        import numpy as np
        H, KV, D = (16, 4, 128)
        HID = 256
        ROPE_BASE = 1000000.0
        EPS = 1e-06

        def _layernorm(x, w, b):
            mu = jnp.mean(x, axis=-1, keepdims=True)
            xc = x - mu
            var = jnp.mean(xc * xc, axis=-1, keepdims=True)
            return xc * jax.lax.rsqrt(var + EPS) * w + b

        def _rope(x, cos, sin):
            xr, xi = (x[..., 0::2], x[..., 1::2])
            c, s = (cos[None, None], sin[None, None])
            out = jnp.stack([xr * c - xi * s, xr * s + xi * c], axis=-1)
            return out.reshape(x.shape)
        B, S, _ = x.shape
        qkv = x @ w_qkv.T
        qg, k, v = jnp.split(qkv, [2 * H * D, 2 * H * D + KV * D], axis=-1)
        q, gate = jnp.split(qg, 2, axis=-1)
        q = q.reshape(B, S, H, D).transpose(0, 2, 1, 3)
        k = k.reshape(B, S, KV, D).transpose(0, 2, 1, 3)
        v = v.reshape(B, S, KV, D).transpose(0, 2, 1, 3)
        q = _layernorm(q, q_norm_w, q_norm_b)
        k = _layernorm(k, k_norm_w, k_norm_b)
        inv = 1.0 / ROPE_BASE ** (jnp.arange(0, D, 2, dtype=jnp.float32) / D)
        freqs = jnp.outer(jnp.arange(S, dtype=jnp.float32), inv)
        cos, sin = (jnp.cos(freqs), jnp.sin(freqs))
        q = _rope(q, cos, sin)
        k = _rope(k, cos, sin)
        rep = H // KV
        k = jnp.repeat(k, rep, axis=1)
        v = jnp.repeat(v, rep, axis=1)
        scores = jnp.einsum('bhqd,bhkd->bhqk', q, k) / math.sqrt(D)
        causal = jnp.tril(jnp.ones((S, S), bool))
        scores = jnp.where(causal[None, None], scores, -jnp.inf)
        attn = jax.nn.softmax(scores, axis=-1)
        out = jnp.einsum('bhqk,bhkd->bhqd', attn, v)
        out = out.transpose(0, 2, 1, 3).reshape(B, S, H * D)
        out = out * jax.nn.sigmoid(gate)
        return out @ w_o.T

    def _L1_xattn_ref(h, adj_raw, Wq, Wk, gamma_raw):
        import jax, jax.numpy as jnp
        import numpy as np
        B, N, D = (16, 256, 64)
        H = 4
        TOP_K_RATIO = 0.3
        b, n, dm = h.shape
        d = dm // H
        Q = (h @ Wq.T).reshape(b, n, H, d).transpose(0, 2, 1, 3)
        K = (h @ Wk.T).reshape(b, n, H, d).transpose(0, 2, 1, 3)
        sim = jnp.einsum('bhnd,bhmd->bnm', Q, K) / (jnp.sqrt(jnp.float32(d)) * H)
        k = max(1, int(n * TOP_K_RATIO))
        topk_vals = jax.lax.top_k(sim, k)[0]
        threshold = topk_vals[:, :, -1:]
        sparse_mask = (sim >= threshold).astype(sim.dtype)
        A_learned = jax.nn.sigmoid(sim) * sparse_mask
        A_learned = (A_learned + jnp.swapaxes(A_learned, -1, -2)) * 0.5
        gamma = jax.nn.sigmoid(gamma_raw)
        return (1.0 - gamma) * adj_raw + gamma * A_learned

    def _L1_ffn_ref(x, W1, W2, W3):
        import jax, jax.numpy as jnp
        import numpy as np
        B, S, D, H = (4, 256, 256, 1024)

        def fwht(x):
            orig_shape = x.shape
            n = orig_shape[-1]
            x = x.reshape(-1, n)
            h = 1
            while h < n:
                xb = x.reshape(-1, n // (2 * h), 2, h)
                a = xb[:, :, 0, :]
                b = xb[:, :, 1, :]
                x = jnp.stack([a + b, a - b], axis=2).reshape(-1, n)
                h *= 2
            scale = jnp.asarray(1.0 / np.sqrt(n), dtype=x.dtype)
            return (x * scale).reshape(orig_shape)
        up_gate = jnp.einsum('bsd,hd->bsh', x, W1)
        up_lin = jnp.einsum('bsd,hd->bsh', x, W3)
        hidden = jax.nn.silu(up_gate) * up_lin
        hidden = fwht(hidden)
        out = jnp.einsum('bsh,dh->bsd', hidden, W2)
        return out
    x = _layernorm(x + _L0_attn_ref(x, L0_attn_Wq, L0_attn_bq, L0_attn_Wk, L0_attn_bk, L0_attn_Wv, L0_attn_bv, L0_attn_Wo, L0_attn_bo), axis=-1)
    x = _layernorm(x + _L0_xattn_ref(x, ctx_512, ctx_512), axis=-1)
    x = _layernorm(x + _L0_ffn_ref(x, L0_ffn_gate_w, L0_ffn_wg, L0_ffn_wu, L0_ffn_wd, L0_ffn_sg, L0_ffn_su, L0_ffn_sd), axis=-1)
    x = _layernorm(x + _L1_attn_ref(x, L1_attn_w_qkv, L1_attn_w_o, L1_attn_q_norm_w, L1_attn_q_norm_b, L1_attn_k_norm_w, L1_attn_k_norm_b), axis=-1)
    x = _layernorm(x + _L1_xattn_ref(ctx_512, x, L1_xattn_Wq, L1_xattn_Wk, L1_xattn_gamma_raw), axis=-1)
    x = _layernorm(x + _L1_ffn_ref(x, L1_ffn_W1, L1_ffn_W2, L1_ffn_W3), axis=-1)
    return x

_drawn_inputs = setup_inputs


def setup_inputs(seed=0):
    import zlib

    import numpy as np

    out = dict(_drawn_inputs(seed))
    spreads = {'L0_attn_bq': (0.0, 0.8),
     'L0_attn_bk': (0.0, 0.8),
     'L0_attn_bv': (0.0, 0.1),
     'L0_attn_bo': (0.0, 0.1),
     'L1_attn_q_norm_w': (1.0, 0.6),
     'L1_attn_q_norm_b': (0.0, 0.8),
     'L1_attn_k_norm_w': (1.0, 0.6),
     'L1_attn_k_norm_b': (0.0, 0.8)}
    factors = {'L0_attn_Wq': 4.536,
     'L0_attn_Wk': 4.379,
     'L0_ffn_gate_w': 8.0,
     'L0_ffn_wg': 8.0,
     'L0_ffn_wu': 8.0,
     'L0_ffn_wd': 8.0,
     'L0_ffn_sg': 3.507,
     'L0_ffn_su': 3.451,
     'L0_ffn_sd': 3.454}
    for name, (base, spread) in spreads.items():
        noise = np.random.default_rng([zlib.crc32(name.encode()), seed]).standard_normal(out[name].shape)
        drawn = base * np.exp(spread * noise) if base else spread * noise
        out[name] = jnp.asarray(drawn.astype(out[name].dtype))
    for name, factor in factors.items():
        out[name] = (out[name] * factor).astype(out[name].dtype)
    return out
```

```python
from contextlib import ExitStack

import numpy as np

import concourse.bass as bass
from concourse import mybir

F32 = mybir.dt.float32
F32R = mybir.dt.float32r
BF16 = mybir.dt.bfloat16
ALU = mybir.AluOpType
ACT = mybir.ActivationFunctionType
AX = mybir.AxisListType.X

P = 128
B, T, C = 4, 256, 256
NT = B * T // P
TPB = T // P
KC = C // P
HQ, HKV, HD = 16, 4, 128
LN_EPS = 1e-5
MASKED = -1e30


class Count:

    def __init__(self, sem):
        self.sem, self.n = sem, 0

    def up(self, ins):
        ins.then_inc(self.sem, 1)
        self.n += 1
        return self.n


def bcast(ap, n, axis=1):
    shape = list(ap.shape)
    return ap.unsqueeze(axis).broadcast_to(shape[:axis] + [n] + shape[axis:])


class Common:
    pass


def attention_stage(nc, layer, cm, w, inputs):
    gated = layer == 1
    X, bank = cm.X, cm.bank
    NH = B * HQ
    ident, identb, maskb = cm.ident, cm.identb, cm.maskb
    scale = 0.25 if layer == 0 else HD ** -0.5
    kv_of = (lambda h: h // (HQ // HKV)) if gated else (lambda h: h % HKV)
    QW = HQ * HD
    KG, VG = HQ * HD // 512, HQ * HD // 512 + 1
    col0 = {g: 512 * g for g in range(KG)}
    if gated:
        col0[KG], col0[VG] = 2 * QW, 2 * QW + HKV * HD
    else:
        col0[KG], col0[VG] = QW, QW + HKV * HD
    turned = [(g, i) for g in (KG, 0, 1, 2, 3) for i in range(TPB)]
    NQ = len(turned)
    units = [("turned", g, i) for g, i in turned] + [("value", VG, i) for i in range(TPB)]
    NU = len(units)
    QLAG = 2
    NSTEP = NU + QLAG

    def steps_at(n):
        b, r = n // HQ + 1, n % HQ
        if b >= B or n >= NH:
            return []
        return [(b, k) for k in range(NSTEP) if k * (HQ - 1) // NSTEP == r]

    uses = [("project", 0, k) for k in range(NU)]
    for n in range(NH):
        if gated and n % 2 == 0:
            uses.append(("gate", n // 2))
        uses += [("project", b, k) for b, k in steps_at(n) if k < NU]
    use = {item: k for k, item in enumerate(uses)}

    with ExitStack() as ctx:
        def sb(name, shape, dt=F32):
            return ctx.enter_context(nc.sbuf_tensor(f"L{layer}_{name}", shape, dt))

        def sem(name):
            s = nc.alloc_semaphore(f"L{layer}_{name}")
            cm.stage_sems.append(s)
            return s

        xT = sb("xT", [P, 2, KC, T])
        QT = sb("QT", [P, 2, HQ, T])
        KT = sb("KT", [P, 2, HKV, T])
        V = sb("V", [P, 2, TPB, HKV * HD])
        t_cos = sb("t_cos", [P, 2, 512])
        t_sin = sb("t_sin", [P, 2, 512])
        t_sum = sb("t_sum", [P, 2, 512])
        q_rot = sb("q_rot", [P, 3, 512])
        prob = sb("prob", [P, 3, 384])
        probT = sb("probT", [P, 2, 384])
        outT = sb("outT", [P, 2, T])
        mx = sb("mx", [P, 4, 2])
        nmx = sb("nmx", [P, 4, 2])
        rsum = sb("rsum", [P, 4, 2])
        rinv = sb("rinv", [P, 4, 2])
        ln = LayerNorm(sb, sem)
        if gated:
            gateT = sb("gateT", [P, 4, 2, T])
            ln_graph = LayerNorm(lambda n, s, dt=F32: sb("g" + n, s, dt), lambda n: sem("g" + n))
            r_scaled = Count(sem("r_scaled"))
            g_exp = sb("g_exp", [P, 2, 512])
            sq = sb("sq", [P, 512])
            ssum = sb("ssum", [P, 2, 4])
            lnv = sb("lnv", [P, 2, 4])
            rstd = sb("rstd", [P, 2, 4])
        cosw, sinw, rotb = w.cosw, w.sinw, w.rotb

        x_turned = sem("x_turned")
        xT_ready = sem("xT_ready")
        projected = sem("projected")
        proj_read = sem("proj_read")
        rope_ready = sem("rope_ready")
        rope_summed = sem("rope_summed")
        q_ready = sem("q_ready")
        q_turned = sem("q_turned")
        qT_ready = sem("qT_ready")
        v_ready = sem("v_ready")
        scored = sem("scored")
        max_ready = sem("max_ready")
        exp_done = sem("exp_done")
        prob_ready = sem("prob_ready")
        prob_turned = sem("prob_turned")
        probT_ready = sem("probT_ready")
        out_done = sem("out_done")
        outT_ready = sem("outT_ready")
        y_done = sem("y_done")
        y_read = sem("y_read")
        sq_ready = sem("sq_ready")
        ssum_ready = sem("ssum_ready")
        rstd_ready = sem("rstd_ready")
        gate_exp = sem("gate_exp")
        gate_read = sem("gate_read")
        vown = Count(sem("vector_own"))
        pown = Count(sem("pool_own"))
        aown = Count(sem("scalar_own"))

        b_score = [bank[0], bank[1]]
        b_pT = [bank[2], bank[3]]
        b_out, b_proj, b_turn, b_y = bank[4], bank[5], bank[6], bank[7]

        with nc.Block(f"attention{layer}") as block:

            @block.sync
            def _(sp):
                w.prefetch(sp)

            @block.tensor
            def _(pe):
                def project(b, k):
                    if k == 0:
                        if b >= 1:
                            pe.wait_ge(qT_ready, NQ * b)
                        for kc in range(KC):
                            for i in range(TPB):
                                m = pe.transpose(b_turn[:, kc * T + i * P:kc * T + (i + 1) * P],
                                                 X[:, TPB * b + i, kc * P:(kc + 1) * P], ident[:, :])
                        m.then_inc(x_turned, 1)
                        pe.wait_ge(xT_ready, b + 1)
                    if k < NU:
                        kind, g, i = units[k]
                        u = use["project", b, k]
                        if u >= 1:
                            pe.wait_ge(proj_read, u)
                        for kc in range(KC):
                            m = pe.matmul(b_proj[:, :], xT[:, b % 2, kc, i * P:(i + 1) * P],
                                          w.wqkv[:, kc, col0[g]:col0[g] + 512], start=(kc == 0), stop=(kc == KC - 1))
                        m.then_inc(projected, 1)
                    if QLAG <= k < NQ + QLAG:
                        a = NQ * b + k - QLAG
                        pe.wait_ge(q_ready, a + 1)
                        pe.wait_ge(xT_ready, b + 1)
                        if a >= 1:
                            pe.wait_ge(qT_ready, a)
                        for s in range(4):
                            m = pe.transpose(b_turn[:, s * P:(s + 1) * P], q_rot[:, a % 3, s * P:(s + 1) * P],
                                             ident[:, :])
                        m.then_inc(q_turned, 1)

                def gates(m):
                    pe.wait_ge(proj_read, use["gate", m])
                    for s in range(2):
                        for kc in range(KC):
                            c0 = QW + (2 * m % HQ + s) * HD
                            ins = pe.matmul(b_proj[:, s * T:(s + 1) * T], w.wqkv[:, kc, c0:c0 + HD],
                                            xT[:, 2 * m // HQ % 2, kc, :], start=(kc == 0 and s == 0),
                                            stop=(kc == KC - 1), skip_group_check=True)
                    ins.then_inc(projected, 1)

                def scores(n):
                    b, h = n // HQ, n % HQ
                    j, par, ps = kv_of(h), b % 2, b_score[n % 2]
                    pe.wait_ge(qT_ready, NQ * b + TPB * (h // 4 + 2))
                    if n >= 2:
                        pe.wait_ge(exp_done, n - 1)
                    pe.matmul(ps[:, 0:P], identb[:, :], maskb[:, :], start=True, stop=False, skip_group_check=True)
                    pe.matmul(ps[:, 0:P], QT[:, par, h, 0:P], KT[:, par, j, 0:P], start=False, stop=True,
                              skip_group_check=True)
                    pe.matmul(ps[:, P:3 * P], QT[:, par, h, P:T], KT[:, par, j, :], start=False, stop=False,
                              skip_group_check=True)
                    pe.matmul(ps[:, 2 * P:3 * P], identb[:, :], maskb[:, :], start=False, stop=True,
                              skip_group_check=True).then_inc(scored, 1)

                def turn_prob(n):
                    pe.wait_ge(prob_ready, n + 1)
                    if n >= 2:
                        pe.wait_ge(probT_ready, n - 1)
                    for s in range(3):
                        m = pe.transpose(b_pT[n % 2][:, s * P:(s + 1) * P], prob[:, n % 3, s * P:(s + 1) * P],
                                         ident[:, :])
                    m.then_inc(prob_turned, 1)

                def values(n):
                    b, j = n // HQ, kv_of(n % HQ)
                    pe.wait_ge(probT_ready, n + 1)
                    pe.wait_ge(v_ready, TPB * (b + 1))
                    if n >= 1:
                        pe.wait_ge(outT_ready, n)
                    pe.matmul(b_out[:, 0:T], V[:, b % 2, 0, j * HD:(j + 1) * HD], probT[:, n % 2, 0:T],
                              start=True, stop=False, skip_group_check=True)
                    pe.matmul(b_out[:, P:T], V[:, b % 2, 1, j * HD:(j + 1) * HD], probT[:, n % 2, T:T + P],
                              start=False, stop=True, skip_group_check=True).then_inc(out_done, 1)

                def output(n):
                    b, h = n // HQ, n % HQ
                    pe.wait_ge(outT_ready, n + 1)
                    if h == 0 and b >= 1:
                        pe.wait_ge(y_read, b)
                    for i in range(TPB):
                        m = pe.matmul(b_y[:, i * C:(i + 1) * C], outT[:, n % 2, i * P:(i + 1) * P], w.wo[:, h, :],
                                      start=(h == 0 and i == 0), stop=(h == HQ - 1), skip_group_check=True)
                    m.then_inc(y_done, 1)

                w.wait_tensor(pe)
                for k in range(NSTEP):
                    project(0, k)
                for n in range(NH + 5):
                    if n < NH:
                        scores(n)
                        if gated and n % 2 == 0:
                            gates(n // 2)
                    for b, k in steps_at(n):
                        project(b, k)
                    if 2 <= n < NH + 2:
                        turn_prob(n - 2)
                    if 3 <= n < NH + 3:
                        values(n - 3)
                    if 4 <= n < NH + 4:
                        output(n - 4)

            @block.scalar
            def _(act):
                def project(b, k):
                    if k == 0:
                        act.wait_ge(x_turned, b + 1)
                        act.activation(xT[:, b % 2].rearrange("p k t -> p (k t)"), b_turn[:, :], ACT.Copy)\
                           .then_inc(xT_ready, 1)
                    if gated and k < NU:
                        kind, g, i = units[k]
                        if kind == "turned":
                            u = use["project", b, k]
                            a = NQ * b + k
                            act.wait_ge(projected, u + 1)
                            if a >= 1:
                                act.wait_ge(ssum_ready, a)
                            act.activation(sq[:, :], b_proj[:, :], ACT.Square).then_inc(sq_ready, 1)
                            act.wait_ge(ssum_ready, a + 1)
                            if a >= 2:
                                act.wait_ge(q_ready, a - 1)
                            v = aown.up(act.activation(lnv[:, a % 2, :], ssum[:, a % 2, :], ACT.Ln))
                            act.wait_ge(aown.sem, v)
                            act.activation(rstd[:, a % 2, :], lnv[:, a % 2, :], ACT.Exp, scale=-0.5)\
                               .then_inc(rstd_ready, 1)
                    if QLAG <= k < NQ + QLAG:
                        a = NQ * b + k - QLAG
                        g, i = turned[k - QLAG]
                        act.wait_ge(q_turned, a + 1)
                        if b >= 2:
                            act.wait_ge(scored, HQ * (b - 1))
                        dst = KT if g == KG else QT
                        h0 = 0 if g == KG else 4 * g
                        act.activation(dst[:, b % 2, h0:h0 + 4, i * P:(i + 1) * P],
                                       b_turn[:, :].rearrange("p (s t) -> p s t", s=4), ACT.Copy).then_inc(qT_ready, 1)

                def gates(m):
                    act.wait_ge(projected, use["gate", m] + 1)
                    if m >= 2:
                        act.wait_ge(gate_read, m - 1)
                    act.activation(g_exp[:, m % 2, :], b_proj[:, :], ACT.Exp, scale=-1.0).then_inc(gate_exp, 1)
                    act.wait_ge(gate_exp, m + 1)
                    act.sem_inc(proj_read, 1)

                def exps(n):
                    act.wait_ge(max_ready, n + 1)
                    if n >= 3:
                        act.wait_ge(prob_turned, n - 2)
                    for i, (c0, c1) in enumerate(((0, P), (P, 3 * P))):
                        m = act.activation(prob[:, n % 3, c0:c1], b_score[n % 2][:, c0:c1], ACT.Exp,
                                           bias=nmx[:, n % 4, i:i + 1], scale=scale,
                                           accum_out=rsum[:, n % 4, i:i + 1])
                    m.then_inc(exp_done, 1)

                for k in range(NSTEP):
                    project(0, k)
                for n in range(NH + 8):
                    if gated and n % 2 == 0 and n < NH:
                        gates(n // 2)
                    for b, k in steps_at(n):
                        project(b, k)
                    if 2 <= n < NH + 2:
                        act.wait_ge(prob_turned, n - 1)
                        if n >= 4:
                            act.wait_ge(out_done, n - 3)
                        act.activation(probT[:, n % 2, :], b_pT[n % 2][:, 0:384], ACT.Copy).then_inc(probT_ready, 1)
                    if not gated and 3 <= n < NH + 3:
                        act.wait_ge(out_done, n - 2)
                        if n >= 5:
                            act.wait_ge(y_done, n - 4)
                        act.activation(outT[:, (n - 3) % 2, :], b_out[:, 0:T], ACT.Copy).then_inc(outT_ready, 1)
                    if n < NH:
                        exps(n)
                    if n >= HQ + 4 and (n - HQ - 4) % HQ == 0:
                        ln.rstd(act, (n - HQ - 4) // HQ)
                    if gated and n >= HQ + 6 and (n - HQ - 6) % HQ == 0:
                        ln_graph.rstd(act, (n - HQ - 6) // HQ)

            @block.vector
            def _(dve):
                def project(b, k):
                    if k >= NU:
                        return
                    kind, g, i = units[k]
                    u = use["project", b, k]
                    ps4 = b_proj[:, :].rearrange("p (s d) -> p s d", s=4)
                    pairs = b_proj[:, :].rearrange("p (s e two) -> p s e two", s=4, two=2)
                    if kind == "turned":
                        a = NQ * b + k
                        qk = 1 if g == KG else 0
                        dve.wait_ge(projected, u + 1)
                        if gated:
                            dve.wait_ge(sq_ready, a + 1)
                        if a >= 2:
                            dve.wait_ge(rope_summed, a - 1)
                        dve.tensor_tensor(t_cos[:, a % 2, :].rearrange("p (s d) -> p s d", s=4), ps4,
                                          bcast(cosw(qk, i), 4), ALU.mult)
                        v = vown.up(dve.tensor_tensor(
                            t_sin[:, a % 2, :].rearrange("p (s e two) -> p s e two", s=4, two=2),
                            pairs[:, :, :, ::-1],
                            bcast(sinw(qk, i).rearrange("p (e two) -> p e two", two=2), 4), ALU.mult))
                        dve.wait_ge(vown.sem, v)
                        dve.sem_inc(rope_ready, 1)
                        dve.sem_inc(proj_read, 1)
                        if gated:
                            v = vown.up(dve.tensor_reduce(ssum[:, a % 2, :], sq[:, :].rearrange(
                                "p (s d) -> p s d", s=4), AX, ALU.add))
                            dve.wait_ge(vown.sem, v)
                            dve.tensor_scalar(ssum[:, a % 2, :], ssum[:, a % 2, :], 1.0 / HD, 1e-6, ALU.mult, ALU.add)\
                               .then_inc(ssum_ready, 1)
                    elif kind == "value":
                        dve.wait_ge(projected, u + 1)
                        if b >= 2:
                            dve.wait_ge(out_done, HQ * (b - 1))
                        if gated:
                            v = vown.up(dve.tensor_copy(V[:, b % 2, i, :], b_proj[:, :]))
                        else:
                            v = vown.up(dve.tensor_tensor(V[:, b % 2, i, :], b_proj[:, :], w.bv[:, :], ALU.add))
                        dve.wait_ge(vown.sem, v)
                        dve.sem_inc(proj_read, 1)
                        dve.sem_inc(v_ready, 1)

                def gates(m):
                    dve.wait_ge(gate_exp, m + 1)
                    v = vown.up(dve.tensor_scalar(g_exp[:, m % 2, :], g_exp[:, m % 2, :], 1.0, None, ALU.add))
                    dve.wait_ge(vown.sem, v)
                    if m >= 4:
                        dve.wait_ge(outT_ready, 2 * (m - 3))
                    dve.reciprocal(gateT[:, m % 4, :, :].rearrange("p s t -> p (s t)"), g_exp[:, m % 2, :])\
                        .then_inc(gate_read, 1)

                def maxima(n):
                    ps = b_score[n % 2]
                    dve.wait_ge(scored, n + 1)
                    if n >= 4:
                        dve.wait_ge(exp_done, n - 3)
                    dve.tensor_reduce(mx[:, n % 4, 0:1], ps[:, 0:P], AX, ALU.max)
                    v = vown.up(dve.tensor_reduce(mx[:, n % 4, 1:2], ps[:, P:3 * P], AX, ALU.max))
                    dve.wait_ge(vown.sem, v)
                    dve.tensor_scalar(nmx[:, n % 4, :], mx[:, n % 4, :], -scale, None, ALU.mult).then_inc(max_ready, 1)

                def normalise(n):
                    dve.wait_ge(exp_done, n + 1)
                    v = vown.up(dve.reciprocal(rinv[:, n % 4, :], rsum[:, n % 4, :]))
                    dve.wait_ge(vown.sem, v)
                    for i, (c0, c1) in enumerate(((0, P), (P, 3 * P))):
                        m = dve.tensor_scalar(prob[:, n % 3, c0:c1], prob[:, n % 3, c0:c1], rinv[:, n % 4, i:i + 1],
                                              None, ALU.mult)
                    m.then_inc(prob_ready, 1)

                for k in range(NSTEP):
                    project(0, k)
                for n in range(NH + 8):
                    if n >= HQ + 4 and (n - HQ - 4) % HQ == 0:
                        b = (n - HQ - 4) // HQ
                        dve.wait_ge(y_done, HQ * (b + 1))
                        ln.sums(dve, b, b_y[:, :].rearrange("p (i c) -> p i c", i=TPB), X, vown, y_read,
                                None if gated else w.bo)
                    if n >= HQ + 5 and (n - HQ - 5) % HQ == 0:
                        ln.scale(dve, (n - HQ - 5) // HQ, X)
                    if gated and n >= HQ + 6 and (n - HQ - 6) % HQ == 0:
                        b = (n - HQ - 6) // HQ
                        Xb = X[:, TPB * b:TPB * (b + 1), :]
                        dve.wait_ge(ln.x_new, b + 1)
                        v = r_scaled.up(dve.tensor_scalar(Xb, Xb, w.two_minus_gamma, None, ALU.mult))
                        dve.wait_ge(r_scaled.sem, v)
                        ln_graph.sums(dve, b, w.graph[:, TPB * b:TPB * (b + 1), :], X, vown, None, None)
                    if gated and n >= HQ + 7 and (n - HQ - 7) % HQ == 0:
                        ln_graph.scale(dve, (n - HQ - 7) // HQ, X)
                    if n < NH:
                        maxima(n)
                        if gated and n % 2 == 0:
                            gates(n // 2)
                    if gated and 3 <= n < NH + 3:
                        a = n - 3
                        dve.wait_ge(out_done, a + 1)
                        if a >= 2:
                            dve.wait_ge(y_done, a - 1)
                        dve.wait_ge(gate_read, a // 2 + 1)
                        dve.tensor_tensor(outT[:, a % 2, :], b_out[:, 0:T], gateT[:, a // 2 % 4, a % 2, :],
                                          ALU.mult).then_inc(outT_ready, 1)
                    for b, k in steps_at(n):
                        project(b, k)
                    if 1 <= n < NH + 1:
                        normalise(n - 1)

            @block.gpsimd
            def _(pool):
                for b in range(B):
                    for k in range(NQ):
                        g, i = turned[k]
                        a = NQ * b + k
                        qk = 1 if g == KG else 0
                        pool.wait_ge(rope_ready, a + 1)
                        v = pown.up(pool.tensor_tensor(t_sum[:, a % 2, :], t_cos[:, a % 2, :], t_sin[:, a % 2, :],
                                                       ALU.add))
                        pool.wait_ge(pown.sem, v)
                        pool.sem_inc(rope_summed, 1)
                        s4 = t_sum[:, a % 2, :].rearrange("p (s d) -> p s d", s=4)
                        if gated:
                            pool.wait_ge(rstd_ready, a + 1)
                            v = pown.up(pool.tensor_tensor(
                                s4, s4, rstd[:, a % 2, :].unsqueeze(2).broadcast_to([P, 4, HD]), ALU.mult))
                            pool.wait_ge(pown.sem, v)
                        if a >= 3:
                            pool.wait_ge(q_turned, a - 2)
                        pool.tensor_tensor(q_rot[:, a % 3, :].rearrange("p (s d) -> p s d", s=4), s4,
                                           rotb(qk, g, i), ALU.add).then_inc(q_ready, 1)


def cross_attention_stage(nc, cm, kstack, vstack, prefetch):
    X, bank, ident = cm.X, cm.bank, cm.ident
    G, D, J, SW = 4, 8, 4, 32
    scale = D ** -0.5
    NUNIT = 2 * B

    order = []
    for u in range(NUNIT + 2):
        if 1 <= u <= NUNIT:
            order.append(("queries_shifted", u - 1, 0))
        if u < NUNIT:
            order += [("keys", u, 0), ("queries", u, 0)]
        if u >= 2:
            order += [("values", u - 2, 1), ("outputs", u - 2, 0)]
        for k in range(2 * J):
            if 1 <= u <= NUNIT:
                order.append(("scores", u - 1, k))
            if u < NUNIT:
                order.append(("maxima", u, k))
            if k == 2 * J - 2 and 1 <= u <= NUNIT:
                order.append(("values", u - 1, 0))
            if k == 2 and u >= 2 and u % 2:
                order.append(("normalise", u // 2 - 1, 0))
    RING = ("queries_shifted", "keys", "queries", "scores", "maxima", "outputs")
    turn, k = {}, 0
    for item in order:
        if item[0] in RING:
            turn[item] = (k % 3, k // 3)
            k += 1

    with ExitStack() as ctx:
        def sb(name, shape, dt=F32):
            return ctx.enter_context(nc.sbuf_tensor(f"X0_{name}", shape, dt))

        def sem(name):
            return ctx.enter_context(nc.semaphore(f"X0_{name}"))

        x_hi = sb("x_hi", [P, TPB, C], F32R)
        qstack = sb("qstack", [P, 2, TPB, G, 2 * J, SW])
        qT = sb("qT", [P, 2, G * T], F32R)
        qTs = sb("qTs", [P, 2, G * T], F32R)
        kT = sb("kT", [P, 2, J, T], F32R)
        probT = sb("probT", [P, 2 * J, G * T])
        outT = sb("outT", [P, 2, G * T])
        mx = sb("mx", [P, 2, TPB, G, J])
        rden = sb("rden", [P, 2, G, J])
        att = sb("att", [P, 2, TPB, C])
        ln = LayerNorm(sb, sem)

        filled = [sem(f"pair_filled{s}") for s in range(3)]
        read = [sem(f"pair_read{s}") for s in range(3)]
        stack_zero = sem("stack_zero")
        stack_ready = sem("stack_ready")
        keys_ready = sem("keys_ready")
        queries_ready = sem("queries_ready")
        maxima_in = sem("maxima_in")
        shifted_ready = sem("shifted_ready")
        exp_done = sem("exp_done")
        summed = sem("summed")
        outT_ready = sem("outT_ready")
        outT_read = sem("outT_read")
        vown = Count(sem("vector_own"))

        pair = [(bank[2 * s], bank[2 * s + 1]) for s in range(3)]
        acc = (bank[6], bank[7])
        tile_of = lambda k: (k // G, k % G)
        chunk_of = lambda k: (k // J, k % J)

        with nc.Block("cross_attention") as block:

            @block.sync
            def _(sp):
                prefetch(sp)

            @block.tensor
            def _(pe):
                for kind, u, k in order:
                    b, half = u // 2, u % 2
                    if kind in RING:
                        s, r = turn[kind, u, k]
                        if r:
                            pe.wait_ge(read[s], r)
                    if kind == "keys":
                        for i in range(TPB):
                            m = pe.transpose(pair[s][0][:, i * P:(i + 1) * P],
                                             kstack[:, TPB * b + i, half * P:(half + 1) * P], ident[:, :])
                    elif kind in ("queries", "queries_shifted"):
                        if kind == "queries":
                            pe.wait_ge(stack_ready, b + 1)
                        else:
                            pe.wait_ge(maxima_in, u + 1)
                        for g in range(G):
                            for i in range(TPB):
                                c = (g % 2) * T + i * P
                                m = pe.transpose(pair[s][g // 2][:, c:c + P],
                                                 qstack[:, b % 2, i, g, J * half:J * (half + 1), :]
                                                 .rearrange("p j w -> p (j w)"), ident[:, :])
                    elif kind == "maxima":
                        i, g = tile_of(k)
                        pe.wait_ge(keys_ready, u + 1)
                        pe.wait_ge(queries_ready, u + 1)
                        for h in range(2):
                            m = pe.matmul(pair[s][h][:, :], qT[:, u % 2, g * T + i * P:g * T + (i + 1) * P],
                                          kT[:, u % 2, 2 * h:2 * h + 2, :].rearrange("p j t -> p (j t)"),
                                          start=True, stop=True)
                    elif kind == "scores":
                        c, j = chunk_of(k)
                        pe.wait_ge(shifted_ready, u + 1)
                        for h in range(2):
                            m = pe.matmul(pair[s][h][:, :], kT[:, u % 2, j, c * P:(c + 1) * P],
                                          qTs[:, u % 2, h * 512:(h + 1) * 512], start=True, stop=True)
                    elif kind == "values":
                        pe.wait_ge(exp_done, 2 * J * u + J * (k + 1))
                        if k == 0 and u >= 1:
                            pe.wait_ge(outT_ready, u)
                        for h in range(2):
                            for j in range(J):
                                m = pe.matmul(acc[h][SW * j:SW * (j + 1), :], vstack[:, TPB * b + k, J * half + j, :],
                                              probT[:, J * k + j, h * 512:(h + 1) * 512],
                                              start=(k == 0), stop=(k == 1))
                        m.then_inc(summed, 1)
                    elif kind == "outputs":
                        pe.wait_ge(outT_ready, u + 1)
                        for i in range(TPB):
                            for g in range(G):
                                m = pe.transpose(pair[s][i][:, g * P:(g + 1) * P],
                                                 outT[:, u % 2, g * T + i * P:g * T + (i + 1) * P], ident[:, :])
                    if kind in RING:
                        m.then_inc(filled[s], 1)

            @block.scalar
            def _(act):
                for kind, u, k in order:
                    if kind in RING:
                        s, r = turn[kind, u, k]
                    if kind in ("queries", "queries_shifted"):
                        act.wait_ge(filled[s], r + 1)
                        dst = qT if kind == "queries" else qTs
                        for h in range(2):
                            m = act.activation(dst[:, u % 2, h * 512:(h + 1) * 512], pair[s][h][:, :], ACT.Copy)
                        m.then_inc(queries_ready if kind == "queries" else shifted_ready, 1)
                        act.wait_ge(queries_ready if kind == "queries" else shifted_ready, u + 1)
                        act.sem_inc(read[s], 1)
                    elif kind == "keys":
                        act.wait_ge(filled[s], r + 1)
                        for j in range(J):
                            m = act.activation(kT[:, u % 2, j, :], pair[s][0][:, 0:T], ACT.Copy,
                                               scale=cm.headmask[:, j:j + 1])
                        m.then_inc(keys_ready, 1)
                        act.wait_ge(keys_ready, u + 1)
                        act.sem_inc(read[s], 1)
                    elif kind == "scores":
                        c, j = chunk_of(k)
                        act.wait_ge(filled[s], r + 1)
                        if u >= 1:
                            act.wait_ge(summed, 2 * (u - 1) + c + 1)
                        for h in range(2):
                            m = act.activation(probT[:, k, h * 512:(h + 1) * 512], pair[s][h][:, :], ACT.Exp,
                                               scale=scale)
                        m.then_inc(exp_done, 1)
                        act.wait_ge(exp_done, 2 * J * u + k + 1)
                        act.sem_inc(read[s], 1)
                    elif kind == "normalise":
                        ln.rstd(act, u)

            @block.vector
            def _(dve):
                def stacks(b):
                    Xb = X[:, TPB * b:TPB * (b + 1), :]
                    v = vown.up(dve.tensor_copy(x_hi[:, :, :], Xb))
                    dve.wait_ge(vown.sem, v)
                    if b == 0:
                        dve.wait_ge(stack_zero, 1)
                    if b >= 2:
                        dve.wait_ge(shifted_ready, 2 * (b - 1))
                    for i in range(TPB):
                        hi = x_hi[:, i, :].bitcast(F32).rearrange("p (j g d) -> p g j d", g=G, d=D)
                        xx = X[:, TPB * b + i, :].rearrange("p (j g d) -> p g j d", g=G, d=D)
                        to = qstack[:, b % 2, i]
                        dve.tensor_copy(to[:, :, :, 0:D], hi)
                        dve.tensor_copy(to[:, :, :, D:2 * D], hi)
                        m = dve.tensor_tensor(to[:, :, :, 2 * D:3 * D], xx, hi, ALU.subtract)
                    m.then_inc(stack_ready, 1)

                stacks(0)
                for kind, u, k in order:
                    b, half = u // 2, u % 2
                    if kind in RING:
                        s, r = turn[kind, u, k]
                    if kind == "maxima":
                        i, g = tile_of(k)
                        dve.wait_ge(filled[s], r + 1)
                        for h in range(2):
                            m = dve.tensor_reduce(mx[:, u % 2, i, g, 2 * h:2 * h + 2],
                                                  pair[s][h][:, :].rearrange("p (j t) -> p j t", j=2), AX, ALU.max)
                        v = vown.up(m)
                        dve.wait_ge(vown.sem, v)
                        dve.sem_inc(read[s], 1)
                        if k == 2 * J - 1:
                            dve.tensor_scalar(
                                qstack[:, b % 2, :, :, J * half:J * (half + 1), 3 * D].rearrange("p i g j -> p (i g) j"),
                                mx[:, u % 2].rearrange("p i g j -> p (i g) j"), -1.0, None, ALU.mult)\
                               .then_inc(maxima_in, 1)
                            if half == 0 and b + 1 < B:
                                stacks(b + 1)
                    elif kind == "values" and k == 1:
                        dve.wait_ge(summed, 2 * u + 2)
                        for h in range(2):
                            m = dve.tensor_copy(outT[:, u % 2, h * 512:(h + 1) * 512], acc[h][:, :])
                        m.then_inc(outT_ready, 1)
                    elif kind == "outputs":
                        dve.wait_ge(filled[s], r + 1)
                        for i in range(TPB):
                            o = pair[s][i][:, :].rearrange("p (g j w) -> p g j w", g=G, j=J)
                            v = vown.up(dve.reciprocal(rden[:, i], o[:, :, :, D]))
                        dve.wait_ge(vown.sem, v)
                        for i in range(TPB):
                            o = pair[s][i][:, :].rearrange("p (g j w) -> p g j w", g=G, j=J)
                            to = att[:, b % 2, i, half * P:(half + 1) * P].rearrange("p (j g d) -> p g j d", g=G, d=D)
                            m = dve.tensor_tensor(to, o[:, :, :, 0:D],
                                                  rden[:, i].unsqueeze(3).broadcast_to([P, G, J, D]), ALU.mult)
                        v = vown.up(m)
                        dve.wait_ge(vown.sem, v)
                        dve.sem_inc(read[s], 1)
                        if half == 1:
                            ln.sums(dve, b, att[:, b % 2], X, vown, None, None)
                    elif kind == "normalise":
                        ln.scale(dve, u, X)

            @block.gpsimd
            def _(pool):
                pool.memset(qstack[:, :, :, :, :, :], 0.0).then_inc(stack_zero, 1)


HT = 512


class GatedUnits:

    DLAG = 2

    def __init__(self, sb, sem, n_chunks, n_weighted, bank, xh, xl, w_up, w_down, own):
        self.bank, self.xh, self.xl, self.w_up, self.w_down, self.own = bank, xh, xl, w_up, w_down, own
        self.n_chunks, self.NU = n_chunks, 2 * n_chunks
        self.turn, k = {}, 0
        for n in range(self.NU):
            for kind in ("g", "u", "w")[:3 if n < n_weighted else 2]:
                self.turn[kind, n] = (k % 4, k // 4)
                k += 1
        self.silu = sb("silu", [P, 2, HT])
        self.act_f = sb("act_f", [P, 2, HT])
        self.act_c = sb("act_c", [P, 3, HT])
        self.act_h = sb("act_h", [P, 3, HT], F32R)
        self.act_l = sb("act_l", [P, 3, HT], F32R)
        self.yT = sb("yT", [P, KC, NT * P])
        self.filled = [sem(f"filled{s}") for s in range(4)]
        self.read = [sem(f"read{s}") for s in range(4)]
        self.silu_ready = sem("silu_ready")
        self.act_ready = sem("act_ready")
        self.act_hi_ready = sem("act_hi_ready")
        self.act_lo_ready = sem("act_lo_ready")
        self.down_done = sem("down_done")
        self.yT_ready = sem("yT_ready")
        self.y_turned = sem("y_turned")

    def hidden(self, pe, n, weights):
        c, ht = n // 2, n % 2
        tok = slice(HT * ht, HT * (ht + 1))
        for kind in "gu":
            s, rd = self.turn[kind, n]
            if rd:
                pe.wait_ge(self.read[s], rd)
            for kc in range(KC):
                H, L = self.w_up(kind, c, kc)
                for z, (a, x) in enumerate(((H, self.xh), (H, self.xl), (L, self.xh))):
                    m = pe.matmul(self.bank[s][:, :], a, x[:, kc, tok], start=(kc == 0 and z == 0),
                                  stop=(kc == KC - 1 and z == 2))
            m.then_inc(self.filled[s], 1)
        if ("w", n) in self.turn:
            s, rd = self.turn["w", n]
            if rd:
                pe.wait_ge(self.read[s], rd)
            weights(pe, n, self.bank[s], tok).then_inc(self.filled[s], 1)

    def down(self, pe, n):
        c, ht = n // 2, n % 2
        pe.wait_ge(self.act_lo_ready, n + 1)
        for dc in range(KC):
            H, L = self.w_down(c, dc)
            for z, (w, a) in enumerate(((H, self.act_h), (L, self.act_h), (H, self.act_l))):
                m = pe.matmul(self.bank[4 + 2 * ht + dc][:, :], w, a[:, n % 3, :], start=(c == 0 and z == 0),
                              stop=(c == self.n_chunks - 1 and z == 2))
        m.then_inc(self.down_done, 1)

    def turn_back(self, pe, b, ident):
        pe.wait_ge(self.yT_ready, b // 2 + 1)
        for i in range(TPB):
            for dc in range(KC):
                t = TPB * b + i
                m = pe.transpose(self.bank[b][:, i * C + dc * P:i * C + (dc + 1) * P],
                                 self.yT[:, dc, t * P:(t + 1) * P], ident[:, :])
        m.then_inc(self.y_turned, 1)

    def gate(self, act, n):
        s, rd = self.turn["g", n]
        act.wait_ge(self.filled[s], rd + 1)
        if n >= 2:
            act.wait_ge(self.act_ready, n - 1)
        act.activation(self.silu[:, n % 2, :], self.bank[s][:, :], ACT.Silu).then_inc(self.silu_ready, 1)
        act.wait_ge(self.silu_ready, n + 1)
        act.sem_inc(self.read[s], 1)

    def high(self, act, n):
        act.wait_ge(self.act_ready, n + 1)
        if n >= 3:
            act.wait_ge(self.down_done, n - 2)
        act.activation(self.act_h[:, n % 3, :], self.act_c[:, n % 3, :], ACT.Copy).then_inc(self.act_hi_ready, 1)

    def keep(self, act):
        act.wait_ge(self.down_done, self.NU)
        for ht in range(2):
            for dc in range(KC):
                m = act.activation(self.yT[:, dc, HT * ht:HT * (ht + 1)], self.bank[4 + 2 * ht + dc][:, :], ACT.Copy)
            m.then_inc(self.yT_ready, 1)

    def product(self, dve, n):
        s, rd = self.turn["u", n]
        dve.wait_ge(self.silu_ready, n + 1)
        dve.wait_ge(self.filled[s], rd + 1)
        if n >= 3:
            dve.wait_ge(self.act_lo_ready, n - 2)
        if ("w", n) in self.turn:
            v = self.own.up(dve.tensor_tensor(self.act_f[:, n % 2, :], self.bank[s][:, :], self.silu[:, n % 2, :],
                                              ALU.mult))
            dve.wait_ge(self.own.sem, v)
            dve.sem_inc(self.read[s], 1)
            s, rd = self.turn["w", n]
            dve.wait_ge(self.filled[s], rd + 1)
            dve.tensor_tensor(self.act_c[:, n % 3, :], self.bank[s][:, :], self.act_f[:, n % 2, :], ALU.mult)\
                .then_inc(self.act_ready, 1)
        else:
            dve.tensor_tensor(self.act_c[:, n % 3, :], self.bank[s][:, :], self.silu[:, n % 2, :], ALU.mult)\
                .then_inc(self.act_ready, 1)
        dve.wait_ge(self.act_ready, n + 1)
        dve.sem_inc(self.read[s], 1)

    def low(self, dve, n):
        dve.wait_ge(self.act_hi_ready, n + 1)
        dve.tensor_tensor(self.act_l[:, n % 3, :], self.act_c[:, n % 3, :], self.act_h[:, n % 3, :].bitcast(F32),
                          ALU.subtract).then_inc(self.act_lo_ready, 1)


def norm_all(dve, ln, units, bank, X, own):
    for b in range(B):
        dve.wait_ge(units.y_turned, b + 1)
        ln.sums(dve, b, bank[b][:, :].rearrange("p (i c) -> p i c", i=TPB), X, own, None, None)
        if b >= 1:
            ln.scale(dve, b - 1, X)
    ln.scale(dve, B - 1, X)


def turn_x(pe, X, bank, ident, x_turned):
    for ht in range(2):
        for kc in range(KC):
            for i in range(4):
                m = pe.transpose(bank[2 * ht + kc][:, i * P:(i + 1) * P],
                                 X[:, 4 * ht + i, kc * P:(kc + 1) * P], ident[:, :])
            m.then_inc(x_turned, 1)


def high_x(act, bank, xh, x_turned, xh_ready):
    for j in range(4):
        ht, kc = j // 2, j % 2
        act.wait_ge(x_turned, j + 1)
        act.activation(xh[:, kc, HT * ht:HT * (ht + 1)], bank[j][:, :], ACT.Copy).then_inc(xh_ready, 1)


def low_x(dve, bank, xh, xl, xh_ready, xl_ready):
    for j in range(4):
        ht, kc = j // 2, j % 2
        dve.wait_ge(xh_ready, j + 1)
        dve.tensor_tensor(xl[:, kc, HT * ht:HT * (ht + 1)], bank[j][:, :],
                          xh[:, kc, HT * ht:HT * (ht + 1)].bitcast(F32), ALU.subtract).then_inc(xl_ready, 1)


NE, FE, TOPK, FS = 32, 96, 6, 192
NCH = NE * FE // P
NSH = -(-FS // P)
GCH = 3
NGRP = NCH // GCH + 1
GW = GCH * P
RAW, SPLIT = 3, 2


def moe_loads(A, q):
    e0 = 4 * q
    for kc in range(KC):
        for name, n in (("g", "L0_ffn_wg"), ("u", "L0_ffn_wu")):
            yield (name, kc), A[n][e0:e0 + 4, kc * P:(kc + 1) * P, :].rearrange("e p f -> p e f")
    yield ("d", 0), A["L0_ffn_wd"].rearrange("e f d -> (e f) d")[GW * q:GW * (q + 1), :]\
        .rearrange("(c p) d -> p c d", p=P)


def moe_load(sp, A, q, raw, loaded):
    s = q % RAW
    if q < NGRP - 1:
        for (name, kc), src in moe_loads(A, q):
            if name == "d":
                dst = raw[s]["d"][:, :, :]
            else:
                dst = raw[s][name][:, kc, :].rearrange("p (e f) -> p e f", f=FE)
            sp.dma_start(dst, src).then_inc(loaded[s], 16)
        return
    for name, n in (("g", "L0_ffn_sg"), ("u", "L0_ffn_su")):
        sp.dma_start(raw[s][name][:, :, 0:FS], A[n].rearrange("(k p) f -> p k f", p=P)).then_inc(loaded[s], 16)
    sp.dma_start(raw[s]["d"][:, 0, :], A["L0_ffn_sd"][0:P, :]).then_inc(loaded[s], 16)
    sp.dma_start(raw[s]["d"][0:FS - P, 1, :], A["L0_ffn_sd"][P:FS, :]).then_inc(loaded[s], 16)


def moe_stage(nc, cm, A, raw, loaded, sim, kth, unranked, prefetch):
    X, bank, ident, identb = cm.X, cm.bank, cm.ident, cm.identb
    last_unit = lambda q: 2 * min(GCH * (q + 1), NCH + NSH) - 1
    with ExitStack() as ctx:
        def sb(name, shape, dt=F32):
            return ctx.enter_context(nc.sbuf_tensor(f"M_{name}", shape, dt))

        def sem(name):
            return ctx.enter_context(nc.semaphore(f"M_{name}"))

        xh = sb("xh", [P, KC, NT * P], F32R)
        xl = sb("xl", [P, KC, NT * P], F32R)
        hi = [{n: sb(f"hi_{n}{s}", [P, GCH if n == "d" else KC, C if n == "d" else GW], F32R) for n in "gud"}
              for s in range(SPLIT)]
        lo = [{n: sb(f"lo_{n}{s}", [P, GCH if n == "d" else KC, C if n == "d" else GW], F32R) for n in "gud"}
              for s in range(SPLIT)]
        gate_w = sb("gate_w", [P, KC, NE])
        gate_h = sb("gate_h", [P, KC, NE], F32R)
        gate_l = sb("gate_l", [P, KC, NE], F32R)
        sel = sb("sel", [3 * NE, NCH * P], BF16)
        score = sb("score", [P, NT, NE + 8])
        e_neg = sb("e_neg", [P, NT, NE])
        top = sb("top", [P, NT, 8])
        rest = sb("rest", [P, NT, NE + 8])
        den = sb("den", [P, NT])
        comb = sb("comb", [P, NT, NE])
        parts = sb("parts", [P, NT, 3, NE], BF16)
        combT = sb("combT", [3 * NE, NT * P], BF16)
        ln = LayerNorm(sb, sem)

        small_loaded = sem("small_loaded")
        x_turned = sem("x_turned")
        xh_ready = sem("xh_ready")
        xl_ready = sem("xl_ready")
        logits_done = sem("logits_done")
        exp_ready = sem("exp_ready")
        parts_ready = sem("parts_ready")
        parts_turned = sem("parts_turned")
        combT_ready = sem("combT_ready")
        gate_ready = sem("gate_ready")
        hi_ready = sem("hi_ready")
        lo_ready = sem("lo_ready")
        padded = sem("padded")
        vown = Count(sem("vector_own"))

        def w_up(kind, c, kc):
            q, r = c // GCH, c % GCH
            return (hi[q % SPLIT][kind][:, kc, r * P:(r + 1) * P], lo[q % SPLIT][kind][:, kc, r * P:(r + 1) * P])

        def w_down(c, dc):
            q, r = c // GCH, c % GCH
            return (hi[q % SPLIT]["d"][:, r, dc * P:(dc + 1) * P], lo[q % SPLIT]["d"][:, r, dc * P:(dc + 1) * P])

        un = GatedUnits(sb, sem, NCH + NSH, 2 * NCH, bank, xh, xl, w_up, w_down, vown)
        NU = un.NU

        NLOAD = [5] * (NGRP - 1) + [4]

        def group_loaded(q):
            return 16 * sum(NLOAD[p] for p in range(q % RAW, q + 1, RAW))

        with nc.Block("experts") as block:

            @block.sync
            def _(sp):
                sp.dma_start(gate_w[:, :, :], A["L0_ffn_gate_w"].rearrange("(k p) e -> p k e", p=P))\
                    .then_inc(small_loaded, 16)
                sp.dma_start(sel[:, :], A["c_sel"]).then_inc(small_loaded, 16)
                prefetch(sp)
                for q in range(RAW, NGRP):
                    sp.wait_ge(lo_ready, q - RAW + 1)
                    sp.wait_ge(hi_ready, q - RAW + 1)
                    if q == NGRP - 1:
                        sp.wait_ge(padded, 1)
                    moe_load(sp, A, q, raw, loaded)

            @block.tensor
            def _(pe):
                turn_x(pe, X, bank, ident, x_turned)
                pe.wait_ge(gate_ready, 2)
                pe.wait_ge(xl_ready, 4)
                for t in range(NT):
                    for kc in range(KC):
                        for n, (a, g) in enumerate(((xh, gate_h), (xh, gate_l), (xl, gate_h))):
                            m = pe.matmul(bank[4][:, NE * t:NE * (t + 1)], a[:, kc, t * P:(t + 1) * P], g[:, kc, :],
                                          start=(t == 0 and kc == 0 and n == 0), stop=(kc == KC - 1 and n == 2),
                                          skip_group_check=True)
                m.then_inc(logits_done, 1)

                def weights(pe, n, to, tok):
                    if n == 0:
                        pe.wait_ge(parts_ready, 1)
                        for t in range(NT):
                            m = pe.transpose(bank[5][0:3 * NE, :].bitcast(BF16)[:, t * P:(t + 1) * P],
                                             parts[:, t].rearrange("p z e -> p (z e)"), identb[:, :])
                        m.then_inc(parts_turned, 1)
                        pe.wait_ge(combT_ready, 1)
                    c = n // 2
                    return pe.matmul(to[:, :], sel[:, c * P:(c + 1) * P], combT[:, tok], start=True, stop=True)

                for n in range(NU + un.DLAG):
                    if n < NU:
                        if n % (2 * GCH) == 0:
                            pe.wait_ge(hi_ready, n // (2 * GCH) + 1)
                            pe.wait_ge(lo_ready, n // (2 * GCH) + 1)
                        un.hidden(pe, n, weights)
                    if n == 0:
                        pe.wait_ge(exp_ready, 1)
                    if n >= un.DLAG:
                        un.down(pe, n - un.DLAG)
                for b in range(B):
                    un.turn_back(pe, b, ident)

            @block.scalar
            def _(act):
                high_x(act, bank, xh, x_turned, xh_ready)
                act.wait_ge(logits_done, 1)
                act.activation(e_neg[:, :, :].rearrange("p t e -> p (t e)"), bank[4][:, 0:NT * NE], ACT.Exp,
                               scale=-1.0).then_inc(exp_ready, 1)
                for n in range(NU + 1):
                    if n < NU:
                        un.gate(act, n)
                    if n >= 1:
                        un.high(act, n - 1)
                un.keep(act)
                for b in range(B):
                    ln.rstd(act, b)

            @block.vector
            def _(dve):
                def split_hi(q):
                    dve.wait_ge(loaded[q % RAW], group_loaded(q))
                    if q >= SPLIT:
                        dve.wait_ge(un.down_done, last_unit(q - SPLIT) + 1)
                    for name in "gud":
                        m = dve.tensor_copy(hi[q % SPLIT][name][:, :, :], raw[q % RAW][name][:, :, :])
                    m.then_inc(hi_ready, 1)

                dve.wait_ge(small_loaded, 32)
                dve.tensor_copy(gate_h[:, :, :], gate_w[:, :, :]).then_inc(gate_ready, 1)
                dve.wait_ge(gate_ready, 1)
                dve.tensor_tensor(gate_l[:, :, :], gate_w[:, :, :], gate_h[:, :, :].bitcast(F32), ALU.subtract)\
                    .then_inc(gate_ready, 1)
                low_x(dve, bank, xh, xl, xh_ready, xl_ready)
                split_hi(0)
                v = vown.up(dve.memset(score[:, :, :], -1.0))
                dve.wait_ge(exp_ready, 1)
                dve.wait_ge(vown.sem, v)
                v = vown.up(dve.tensor_scalar(e_neg[:, :, :], e_neg[:, :, :], 1.0, None, ALU.add))
                dve.wait_ge(vown.sem, v)
                v = vown.up(dve.reciprocal(score[:, :, 0:NE], e_neg[:, :, :]))
                dve.wait_ge(vown.sem, v)
                for t in range(NT):
                    v = vown.up(dve.max(top[:, t, :], score[:, t, :]))
                dve.wait_ge(vown.sem, v)
                v = vown.up(dve.memset(top[:, :, TOPK:8], -1.0))
                dve.wait_ge(vown.sem, v)
                for t in range(NT):
                    v = vown.up(dve.match_replace(rest[:, t, :], top[:, t, :], score[:, t, :], 0.0))
                dve.wait_ge(vown.sem, v)
                v = vown.up(dve.tensor_tensor(comb[:, :, :], score[:, :, 0:NE], rest[:, :, 0:NE], ALU.subtract))
                dve.wait_ge(vown.sem, v)
                v = vown.up(dve.tensor_reduce(den[:, :], comb[:, :, :], AX, ALU.add))
                dve.wait_ge(vown.sem, v)
                v = vown.up(dve.tensor_scalar(den[:, :], den[:, :], 1e-20, None, ALU.add))
                dve.wait_ge(vown.sem, v)
                v = vown.up(dve.reciprocal(den[:, :], den[:, :]))
                dve.wait_ge(vown.sem, v)
                v = vown.up(dve.tensor_tensor(comb[:, :, :], comb[:, :, :],
                                              den[:, :].unsqueeze(2).broadcast_to([P, NT, NE]), ALU.mult))
                for z in range(3):
                    dve.wait_ge(vown.sem, v)
                    v = vown.up(dve.tensor_copy(parts[:, :, z, :], comb[:, :, :]))
                    dve.wait_ge(vown.sem, v)
                    if z < 2:
                        v = vown.up(dve.tensor_tensor(comb[:, :, :], comb[:, :, :], parts[:, :, z, :], ALU.subtract))
                dve.sem_inc(parts_ready, 1)
                dve.wait_ge(parts_turned, 1)
                dve.tensor_copy(combT[:, :], bank[5][0:3 * NE, :].bitcast(BF16)).then_inc(combT_ready, 1)
                KTH = int(T * 0.3)
                rounds = -(-KTH // 8)
                assert KTH - 8 * (rounds - 1) == 4
                ranked = {}

                def rank(r, t, replace):
                    src = sim if r == 0 else unranked
                    if replace:
                        dve.wait_ge(vown.sem, ranked[t])
                        ranked[t] = vown.up(dve.match_replace(unranked[:, t, :], kth[:, t, :], src[:, t, :], -3e38))
                    else:
                        if r:
                            dve.wait_ge(vown.sem, ranked[t])
                        ranked[t] = vown.up(dve.max(kth[:, t, :], src[:, t, :]))

                ranking = [(r, t, replace) for r in range(rounds) for replace in (False, True)[:2 if r < rounds - 1 else 1]
                           for t in range(NT)]
                per_unit = -(-len(ranking) // NU)
                for n in range(NU + 1):
                    for item in ranking[per_unit * n:per_unit * (n + 1)]:
                        rank(*item)
                    if n < NU:
                        q = n // 2 // GCH + 1
                        if n % (2 * GCH) == 2 * GCH - 4 and q < NGRP:
                            split_hi(q)
                        un.product(dve, n)
                    if n >= 1:
                        un.low(dve, n - 1)
                norm_all(dve, ln, un, bank, X, vown)

            @block.gpsimd
            def _(pool):
                for q in range(NGRP):
                    pool.wait_ge(hi_ready, q + 1)
                    for name in "gud":
                        m = pool.tensor_tensor(lo[q % SPLIT][name][:, :, :], raw[q % RAW][name][:, :, :],
                                               hi[q % SPLIT][name][:, :, :].bitcast(F32), ALU.subtract)
                    m.then_inc(lo_ready, 1)
                    if q == NGRP - 1 - RAW:
                        s = (NGRP - 1) % RAW
                        pool.wait_ge(lo_ready, q + 1)
                        for name in "gu":
                            pool.memset(raw[s][name][:, :, FS:GW], 0.0)
                        pool.memset(raw[s]["d"][:, 1:GCH, :], 0.0).then_inc(padded, 1)


def prepare_layer1(nc, cm, A, wA, sim, kth, w1_loaded):
    bank, ident = cm.bank, cm.ident
    NR = (2 * HQ + 2 * HKV)
    centered = lambda r: r < HQ or 2 * HQ <= r < 2 * HQ + HKV
    keep = ExitStack()

    def sb(name, shape, dt=F32):
        return keep.enter_context(nc.sbuf_tensor(f"P1_{name}", shape, dt))

    def sem(name):
        return keep.enter_context(nc.semaphore(f"P1_{name}"))

    w = Weights()
    wT = sb("wT", [P, KC, NR * P])
    tab = sb("tab", [P, 3, 2, TPB, HD])
    gam = sb("gam", [P, 4])
    raw = wA[:, :].rearrange("p (r c) -> p r c", c=C)
    wo = wA[:, 0:HQ * C].rearrange("p (h n) -> p h n", h=HQ)
    with ExitStack() as ctx:
        def tmp(name, shape, dt=F32):
            return ctx.enter_context(nc.sbuf_tensor(f"P1_{name}", shape, dt))

        center = tmp("center", [P, P])
        wo_raw = tmp("wo_raw", [P, KC, HQ * HD])
        rope = tmp("rope", [P, 2, TPB, HD])
        norm = tmp("norm", [P, 4, HD])
        swapped = tmp("swapped", [P, 4, HD])
        sig = tmp("sig", [P, NT, T])
        loaded, filled, wo_loaded = sem("loaded"), sem("filled"), sem("wo_loaded")
        copied = [sem(f"copied{s}") for s in range(4)]
        sig_exp, a_ready, a_turned, gam_exp = sem("sig_exp"), sem("a_ready"), sem("a_turned"), sem("gam_exp")
        own = Count(sem("vector_own"))
        NG = NR // 4
        NF = KC * NG + HQ // 2

        with nc.Block("prepare1") as block:

            @block.sync
            def _(sp):
                sp.dma_start(center[:, :], A["c_center"]).then_inc(loaded, 16)
                sp.dma_start(rope[:, :, :, :], A["c_rope1"].rearrange("s (i p) d -> p s i d", p=P)).then_inc(loaded, 16)
                for z, name in enumerate(("q_norm_w", "k_norm_w", "q_norm_b", "k_norm_b")):
                    sp.dma_start(norm[:, z, :], A["L1_attn_" + name].partition_broadcast(P)).then_inc(loaded, 16)
                sp.dma_start(gam[:, 0:1], A["L1_xattn_gamma_raw"].partition_broadcast(P)).then_inc(loaded, 16)
                sp.dma_start(wo_raw[:, :, :], A["L1_attn_w_o"].rearrange("(k p) n -> p k n", p=P))\
                    .then_inc(wo_loaded, 16)

            @block.tensor
            def _(pe):
                pe.wait_ge(loaded, 7 * 16)
                pe.wait_ge(w1_loaded, 4 * 16)
                for z in range(NF):
                    to = bank[z % 4]
                    if z >= 4:
                        pe.wait_ge(copied[z % 4], z // 4)
                    if z < KC * NG:
                        kc = z % KC
                        for s in range(4):
                            r = 4 * (z // KC) + s
                            src, dst = raw[:, r, kc * P:(kc + 1) * P], to[:, s * P:(s + 1) * P]
                            if centered(r):
                                m = pe.matmul(dst, src, center[:, :], start=True, stop=True, skip_group_check=True)
                            else:
                                m = pe.transpose(dst, src, ident[:, :])
                    else:
                        if z == KC * NG:
                            pe.wait_ge(wo_loaded, 16)
                        h0 = 2 * (z - KC * NG)
                        for s in range(4):
                            h, nch = h0 + s // 2, s % 2
                            m = pe.transpose(to[:, s * P:(s + 1) * P], wo_raw[:, nch, h * HD:(h + 1) * HD], ident[:, :])
                    m.then_inc(filled, 1)
                pe.wait_ge(a_ready, 1)
                for b in range(B):
                    for i in range(TPB):
                        for j in range(TPB):
                            m = pe.transpose(bank[4 + b][:, i * T + j * P:i * T + (j + 1) * P],
                                             sig[:, TPB * b + j, i * P:(i + 1) * P], ident[:, :])
                    m.then_inc(a_turned, 1)

            def copy_out(eng, copy, z):
                eng.wait_ge(filled, z + 1)
                if z < KC * NG:
                    dst = wT[:, z % KC, 512 * (z // KC):512 * (z // KC + 1)]
                else:
                    h0 = 2 * (z - KC * NG)
                    dst = wo[:, h0:h0 + 2, :].rearrange("p h n -> p (h n)")
                copy(dst, bank[z % 4][:, :]).then_inc(copied[z % 4], 1)

            @block.scalar
            def _(act):
                act.preload_act_table_set("natural_log_exp_and_others")
                act.wait_ge(loaded, 7 * 16)
                act.activation(gam[:, 1:2], gam[:, 0:1], ACT.Exp, scale=-1.0).then_inc(gam_exp, 1)
                act.activation(sig[:, :, :], sim[:, :, :], ACT.Exp, scale=-1.0).then_inc(sig_exp, 1)
                for z in range(0, NF, 2):
                    copy_out(act, lambda o, i: act.activation(o, i, ACT.Copy), z)

            @block.vector
            def _(dve):
                dve.wait_ge(gam_exp, 1)
                v = own.up(dve.tensor_scalar(gam[:, 1:2], gam[:, 1:2], 1.0, None, ALU.add))
                dve.wait_ge(own.sem, v)
                v = own.up(dve.reciprocal(gam[:, 1:2], gam[:, 1:2]))
                dve.wait_ge(own.sem, v)
                v = own.up(dve.tensor_scalar(gam[:, 2:3], gam[:, 1:2], -1.0, 2.0, ALU.mult, ALU.add))
                v = own.up(dve.tensor_scalar(gam[:, 3:4], gam[:, 1:2], 0.5, None, ALU.mult))
                dve.wait_ge(sig_exp, 1)
                v = own.up(dve.tensor_scalar(sig[:, :, :], sig[:, :, :], 1.0, None, ALU.add))
                dve.wait_ge(own.sem, v)
                v = own.up(dve.reciprocal(sig[:, :, :], sig[:, :, :]))
                dve.wait_ge(own.sem, v)
                for t in range(NT):
                    v = own.up(dve.scalar_tensor_tensor(sig[:, t, :], sim[:, t, :], kth[:, t, 3:4], sig[:, t, :],
                                                        ALU.is_ge, ALU.mult))
                dve.wait_ge(own.sem, v)
                dve.sem_inc(a_ready, 1)
                for z in range(1, NF, 2):
                    copy_out(dve, lambda o, i: dve.tensor_copy(o, i), z)
                v = own.up(dve.tensor_copy(swapped[:, :, :].rearrange("p z (e two) -> p (z e) two", two=2),
                                           norm[:, :, :].rearrange("p z (e two) -> p (z e) two", two=2)[:, :, ::-1]))
                dve.wait_ge(own.sem, v)
                with nc.sbuf_tensor("P1_b_sin", [P, TPB, HD], F32) as b_sin:
                    for qk in range(2):
                        if qk:
                            dve.wait_ge(own.sem, v)
                        own.up(dve.tensor_tensor(tab[:, 0, qk], bcast(norm[:, qk, :], TPB), rope[:, 0], ALU.mult))
                        own.up(dve.tensor_tensor(tab[:, 1, qk], bcast(swapped[:, qk, :], TPB), rope[:, 1], ALU.mult))
                        own.up(dve.tensor_tensor(tab[:, 2, qk], bcast(norm[:, 2 + qk, :], TPB), rope[:, 0], ALU.mult))
                        v = own.up(dve.tensor_tensor(b_sin[:, :, :], bcast(swapped[:, 2 + qk, :], TPB), rope[:, 1],
                                                     ALU.mult))
                        dve.wait_ge(own.sem, v)
                        v = own.up(dve.tensor_tensor(tab[:, 2, qk], tab[:, 2, qk], b_sin[:, :, :], ALU.add))
                for b in range(B):
                    s = sim[:, TPB * b:TPB * (b + 1), :]
                    dve.wait_ge(a_turned, b + 1)
                    v = own.up(dve.tensor_tensor(s, bank[4 + b][:, :].rearrange("p (i m) -> p i m", i=TPB),
                                                 sig[:, TPB * b:TPB * (b + 1), :], ALU.add))
                    dve.wait_ge(own.sem, v)
                    v = own.up(dve.tensor_scalar(s, s, gam[:, 3:4], None, ALU.mult))

    w.wqkv, w.wo, w.bo = wT, wo, None
    w.cosw = lambda qk, i: tab[:, 0, qk, i, :]
    w.sinw = lambda qk, i: tab[:, 1, qk, i, :]
    w.rotb = lambda qk, g, i: bcast(tab[:, 2, qk, i, :], 4)
    w.wait_tensor = lambda pe: None
    w.graph, w.two_minus_gamma = sim, gam[:, 2:3]
    w.ffn_loaded = nc.alloc_semaphore("ffn_loaded")

    def prefetch(sp):
        for z, name in enumerate(("L1_ffn_W1", "L1_ffn_W3")):
            sp.dma_start(wA[:, 4096 + 2048 * z:6144 + 2048 * z].rearrange("p (r c) -> p r c", c=C),
                         A[name].rearrange("(r p) c -> p r c", p=P)).then_inc(w.ffn_loaded, 16)
        sp.dma_start(wA[:, 8192:10240].rearrange("p (k h) -> p k h", k=KC),
                     A["L1_ffn_W2"].rearrange("(k p) h -> p k h", p=P)).then_inc(w.ffn_loaded, 16)

    w.prefetch = prefetch
    return w, keep


def dense_stage(nc, cm, A, wA, ffn_loaded):
    X, bank, ident = cm.X, cm.bank, cm.ident
    HID = 1024
    NC_ = HID // P
    raw_up = {"g": wA[:, 4096:6144].rearrange("p (r c) -> p r c", c=C),
              "u": wA[:, 6144:8192].rearrange("p (r c) -> p r c", c=C)}
    raw_down = wA[:, 8192:10240].rearrange("p (k h) -> p k h", k=KC)
    with ExitStack() as ctx:
        def sb(name, shape, dt=F32):
            return ctx.enter_context(nc.sbuf_tensor(f"D_{name}", shape, dt))

        def sem(name):
            return ctx.enter_context(nc.semaphore(f"D_{name}"))

        xh = sb("xh", [P, KC, NT * P], F32R)
        xl = sb("xl", [P, KC, NT * P], F32R)
        up_h = {n: sb(f"up_h_{n}", [P, KC, HID], F32R) for n in "gu"}
        up_l = {n: sb(f"up_l_{n}", [P, KC, HID], F32R) for n in "gu"}
        mid = sb("mid", [P, 2, NC_, C])
        mid_h = sb("mid_h", [P, NC_, C], F32R)
        mid_l = sb("mid_l", [P, NC_, C], F32R)
        down_h = sb("down_h", [P, NC_, C], F32R)
        down_l = sb("down_l", [P, NC_, C], F32R)
        had = sb("had", [P, P])
        had_r = sb("had_r", [P, P], F32R)
        ln = LayerNorm(sb, sem)

        had_loaded = sem("had_loaded")
        filled = sem("prep_filled")
        hi_ready = sem("prep_hi_ready")
        lo_ready = sem("prep_lo_ready")
        mid_ready = sem("mid_ready")
        x_turned = sem("x_turned")
        xh_ready = sem("xh_ready")
        xl_ready = sem("xl_ready")
        had_ready = sem("had_ready")
        vown = Count(sem("vector_own"))
        fills = [("turn", z) for z in range(4)] + [("up", n, kc, r) for n in "gu" for kc in range(KC) for r in range(2)]             + [("had", z) for z in range(4)]

        def w_up(kind, c, kc):
            return up_h[kind][:, kc, c * P:(c + 1) * P], up_l[kind][:, kc, c * P:(c + 1) * P]

        def w_down(c, dc):
            return down_h[:, c, dc * P:(dc + 1) * P], down_l[:, c, dc * P:(dc + 1) * P]

        un = GatedUnits(sb, sem, NC_, 0, bank, xh, xl, w_up, w_down, vown)
        NU = un.NU

        def parts_of(f):
            if f[0] == "up":
                _, n, kc, r = f
                return up_h[n][:, kc, 512 * r:512 * (r + 1)], up_l[n][:, kc, 512 * r:512 * (r + 1)]
            z = f[1]
            return (down_h[:, 2 * z:2 * z + 2, :].rearrange("p k d -> p (k d)"),
                    down_l[:, 2 * z:2 * z + 2, :].rearrange("p k d -> p (k d)"))

        with nc.Block("dense") as block:

            @block.sync
            def _(sp):
                sp.dma_start(had[:, :], A["c_hadamard"]).then_inc(had_loaded, 16)

            @block.tensor
            def _(pe):
                turn_x(pe, X, bank, ident, x_turned)
                pe.wait_ge(ffn_loaded, 3 * 16)
                for n, f in enumerate(fills):
                    to = bank[4 + n % 4]
                    if n >= 4:
                        pe.wait_ge(lo_ready, n - 3)
                    if f[0] == "turn":
                        for s in range(4):
                            c, dc = 2 * f[1] + s // 2, s % 2
                            m = pe.transpose(to[:, s * P:(s + 1) * P], raw_down[:, dc, c * P:(c + 1) * P], ident[:, :])
                    elif f[0] == "up":
                        _, name, kc, r = f
                        for s in range(4):
                            m = pe.transpose(to[:, s * P:(s + 1) * P], raw_up[name][:, 4 * r + s, kc * P:(kc + 1) * P],
                                             ident[:, :])
                    else:
                        z = f[1]
                        pe.wait_ge(mid_ready, 2)
                        for p, src in enumerate((mid_h, mid_l)):
                            m = pe.matmul(to[:, :], had_r[:, :], src[:, 2 * z:2 * z + 2, :].rearrange("p k d -> p (k d)"),
                                          start=(p == 0), stop=(p == 1))
                    m.then_inc(filled, 1)
                pe.wait_ge(xl_ready, 4)
                pe.wait_ge(lo_ready, len(fills))
                for n in range(NU + un.DLAG):
                    if n < NU:
                        un.hidden(pe, n, None)
                    if n >= un.DLAG:
                        un.down(pe, n - un.DLAG)
                for b in range(B):
                    un.turn_back(pe, b, ident)

            @block.scalar
            def _(act):
                high_x(act, bank, xh, x_turned, xh_ready)
                for n, f in enumerate(fills):
                    if f[0] == "turn":
                        continue
                    act.wait_ge(filled, n + 1)
                    act.activation(parts_of(f)[0], bank[4 + n % 4][:, :], ACT.Copy).then_inc(hi_ready, 1)
                for n in range(NU + 1):
                    if n < NU:
                        un.gate(act, n)
                    if n >= 1:
                        un.high(act, n - 1)
                un.keep(act)
                for b in range(B):
                    ln.rstd(act, b)

            @block.vector
            def _(dve):
                dve.wait_ge(had_loaded, 16)
                dve.tensor_copy(had_r[:, :], had[:, :]).then_inc(had_ready, 1)
                low_x(dve, bank, xh, xl, xh_ready, xl_ready)
                for n, f in enumerate(fills):
                    dve.wait_ge(filled, n + 1)
                    if f[0] == "turn":
                        z = f[1]
                        dve.tensor_scalar(mid[:, 0, 2 * z:2 * z + 2, :].rearrange("p k d -> p (k d)"),
                                          bank[4 + n % 4][:, :], HID ** -0.5, None, ALU.mult).then_inc(lo_ready, 1)
                        continue
                    hi, lo = parts_of(f)
                    dve.wait_ge(hi_ready, n - 3)
                    dve.tensor_tensor(lo, bank[4 + n % 4][:, :], hi.bitcast(F32), ALU.subtract).then_inc(lo_ready, 1)
                for n in range(NU + 1):
                    if n < NU:
                        un.product(dve, n)
                    if n >= 1:
                        un.low(dve, n - 1)
                norm_all(dve, ln, un, bank, X, vown)

            @block.gpsimd
            def _(pool):
                own = Count(sem("pool_own"))
                pool.wait_ge(lo_ready, 4)
                for z in range(3):
                    a = mid[:, z % 2].rearrange("p (k two s) d -> p k two (s d)", two=2, s=1 << z)
                    o = mid[:, (z + 1) % 2].rearrange("p (k two s) d -> p k two (s d)", two=2, s=1 << z)
                    own.up(pool.tensor_tensor(o[:, :, 0], a[:, :, 0], a[:, :, 1], ALU.add))
                    v = own.up(pool.tensor_tensor(o[:, :, 1], a[:, :, 0], a[:, :, 1], ALU.subtract))
                    pool.wait_ge(own.sem, v)
                v = own.up(pool.tensor_copy(mid_h[:, :, :], mid[:, 1]))
                pool.wait_ge(own.sem, v)
                pool.sem_inc(mid_ready, 1)
                pool.tensor_tensor(mid_l[:, :, :], mid[:, 1], mid_h[:, :, :].bitcast(F32), ALU.subtract)\
                    .then_inc(mid_ready, 1)


class LayerNorm:

    def __init__(self, sb, sem):
        self.r = sb("ln_r", [P, 2, TPB, C])
        self.stats = sb("ln_stats", [P, 2, TPB, 6])
        self.mv = sb("ln_mv", [P, 2, TPB, 2])
        self.ve = sb("ln_ve", [P, 2, TPB])
        self.lv = sb("ln_lv", [P, 2, TPB])
        self.rs = sb("ln_rs", [P, 2, TPB])
        self.var_ready = sem("ln_var_ready")
        self.log_ready = sem("ln_log_ready")
        self.rstd_ready = sem("ln_rstd_ready")
        self.x_new = sem("x_new")

    def sums(self, dve, n, y, X, own, y_read, bias):
        r = self.r[:, n % 2]
        Xb = X[:, TPB * n:TPB * (n + 1), :]
        if n >= 2:
            dve.wait_ge(self.x_new, n - 1)
        v = own.up(dve.tensor_tensor(r, y, Xb, ALU.add))
        dve.wait_ge(own.sem, v)
        if y_read is not None:
            dve.sem_inc(y_read, 1)
        if bias is not None:
            v = own.up(dve.tensor_tensor(r, r, bcast(bias[:, :], TPB), ALU.add))
            dve.wait_ge(own.sem, v)
        for i in range(TPB):
            v = own.up(dve.bn_stats(self.stats[:, n % 2, i, :], r[:, i, :]))
        dve.wait_ge(own.sem, v)
        for i in range(TPB):
            v = own.up(dve.bn_aggr(self.mv[:, n % 2, i, :], self.stats[:, n % 2, i, :]))
        dve.wait_ge(own.sem, v)
        dve.tensor_scalar(self.ve[:, n % 2, :], self.mv[:, n % 2, :, 1], LN_EPS, None, ALU.add)\
            .then_inc(self.var_ready, 1)

    def rstd(self, act, n):
        act.wait_ge(self.var_ready, n + 1)
        act.activation(self.lv[:, n % 2, :], self.ve[:, n % 2, :], ACT.Ln).then_inc(self.log_ready, 1)
        act.wait_ge(self.log_ready, n + 1)
        act.activation(self.rs[:, n % 2, :], self.lv[:, n % 2, :], ACT.Exp, scale=-0.5).then_inc(self.rstd_ready, 1)

    def scale(self, dve, n, X):
        dve.wait_ge(self.rstd_ready, n + 1)
        for i in range(TPB):
            m = dve.tensor_scalar(X[:, TPB * n + i, :], self.r[:, n % 2, i, :], self.mv[:, n % 2, i, 0:1],
                                  self.rs[:, n % 2, i:i + 1], ALU.subtract, ALU.mult)
        m.then_inc(self.x_new, 1)


N_CONST = 12


class Weights:
    pass


def release_semaphores(nc, cm):
    nc.clear_and_free_semaphores(cm.stage_sems)
    nc.all_engine_barrier()
    cm.stage_sems = []


def decoder(nc, A, out, stages=6):
    with ExitStack() as ctx:
        def sb(name, shape, dt=F32):
            return ctx.enter_context(nc.sbuf_tensor(name, shape, dt))

        def sem(name):
            return ctx.enter_context(nc.semaphore(name))

        cm = Common()
        cm.stage_sems = []
        cm.X = X = sb("X", [P, NT, C])
        cm.ident = sb("ident", [P, P])
        cm.identb = sb("identb", [P, P], BF16)
        cm.maskb = sb("maskb", [P, P], BF16)
        cm.headmask = sb("headmask", [P, 4])
        rope = sb("rope", [P, 2, TPB, HD])
        cm.bank = [ctx.enter_context(nc.psum_tensor(f"bank{i}", [P, 512], F32)) for i in range(8)]
        x_loaded = sem("x_loaded")
        const_loaded = sem("const_loaded")
        w0_loaded = sem("w0_loaded")
        stored = sem("stored")
        wA = sb("wA", [P, 10240])

        w0 = Weights()
        wqkv0 = wA[:, 0:6144].rearrange("p (k n) -> p k n", k=KC)
        wo0 = wA[:, 6144:10240].rearrange("p (h n) -> p h n", h=HQ)

        sim = sb("sim", [P, NT, T])
        kth = sb("kth", [P, NT, 8])
        l0x = ExitStack()
        moe = ExitStack()
        kstack = l0x.enter_context(nc.sbuf_tensor("kstack", [P, NT, 256], F32))
        vstack = l0x.enter_context(nc.sbuf_tensor("vstack", [P, NT, 8, 32], F32))
        with ExitStack() as l0:
            brow = l0.enter_context(nc.sbuf_tensor("brow", [P, 3072], F32))
            bo = l0.enter_context(nc.sbuf_tensor("bo", [P, C], F32))
            rb = l0.enter_context(nc.sbuf_tensor("rb", [P, TPB, 2560], F32))
            ctxs = l0.enter_context(nc.sbuf_tensor("ctxs", [P, NT, 64], F32))
            c_hi = l0.enter_context(nc.sbuf_tensor("c_hi", [P, NT, 64], F32R))
            gw = l0.enter_context(nc.sbuf_tensor("gw", [64, 2, 64], F32))
            gwT = l0.enter_context(nc.sbuf_tensor("gwT", [64, 2, 64], F32))
            stack_clear = sem("stack_clear")
            ctx_turned, w_turned, gw_ready, ctxT_ready = map(sem, ("ctx_turned", "w_turned", "gw_ready", "ctxT_ready"))
            gq_done, gq_ready, similar = map(sem, ("gq_done", "gq_ready", "similar"))
            bank = cm.bank
            tmp0 = ExitStack()
            ctxT = tmp0.enter_context(nc.sbuf_tensor("ctxT", [64, NT * P], F32))
            gqT = tmp0.enter_context(nc.sbuf_tensor("gqT", [64, 2, NT * P], F32))
            with nc.Block("prepare0") as block:

                @block.sync
                def _(sp):
                    sp.dma_start(X[:, :, :], A["x"].rearrange("b (i p) c -> p (b i) c", p=P)).then_inc(x_loaded, 16)
                    for dst, name in ((cm.ident, "c_ident"), (cm.identb, "c_identb"), (cm.maskb, "c_maskb"),
                                      (cm.headmask, "c_headmask")):
                        sp.dma_start(dst[:, :], A[name]).then_inc(const_loaded, 16)
                    sp.dma_start(rope[:, :, :, :], A["c_rope0"].rearrange("s (i p) d -> p s i d", p=P))\
                        .then_inc(const_loaded, 16)
                    off = 0
                    for name, n in (("L0_attn_bq", 2048), ("L0_attn_bk", 512), ("L0_attn_bv", 512)):
                        sp.dma_start(brow[:, off:off + n], A[name].partition_broadcast(P)).then_inc(const_loaded, 16)
                        off += n
                    sp.dma_start(bo[:, :], A["L0_attn_bo"].partition_broadcast(P)).then_inc(const_loaded, 16)
                    sp.dma_start(ctxs[:, :, :], A["ctx_512"].rearrange("b (i p) c -> p (b i) c", p=P))\
                        .then_inc(const_loaded, 16)
                    for z, name in enumerate(("L1_xattn_Wq", "L1_xattn_Wk")):
                        sp.dma_start(gw[:, z, :], A[name]).then_inc(const_loaded, 16)
                    for kc in range(KC):
                        off = 0
                        for name, n in (("L0_attn_Wq", 2048), ("L0_attn_Wk", 512), ("L0_attn_Wv", 512)):
                            sp.dma_start(wqkv0[:, kc, off:off + n], A[name][kc * P:(kc + 1) * P, :])\
                                .then_inc(w0_loaded, 16)
                            off += n
                    sp.dma_start(wo0, A["L0_attn_Wo"].rearrange("(h d) n -> d h n", d=HD)).then_inc(w0_loaded, 16)

                @block.scalar
                def _(act):
                    act.preload_act_table_set("natural_log_exp_and_others")
                    for ht in range(2):
                        act.wait_ge(ctx_turned, ht + 1)
                        act.activation(ctxT[:, ht * 512:(ht + 1) * 512], bank[4 + ht][0:64, :], ACT.Copy)\
                           .then_inc(ctxT_ready, 1)
                    for z in range(2):
                        for ht in range(2):
                            act.wait_ge(gq_done, 2 * z + ht + 1)
                            act.activation(gqT[:, z, ht * 512:(ht + 1) * 512], bank[4 + ht if z == 0 else 6 + ht][0:64, :],
                                           ACT.Copy).then_inc(gq_ready, 1)

                @block.gpsimd
                def _(pool):
                    pool.memset(kstack[:, :, :], 0.0).then_inc(stack_clear, 1)
                    pool.memset(vstack[:, :, :, :], 0.0).then_inc(stack_clear, 1)

                @block.vector
                def _(dve):
                    own = Count(sem("prep_vector_own"))
                    dve.wait_ge(const_loaded, N_CONST * 16)
                    v = own.up(dve.tensor_copy(c_hi[:, :, :], ctxs[:, :, :]))
                    dve.wait_ge(own.sem, v)
                    dve.wait_ge(stack_clear, 2)
                    ks = kstack[:, :, :].rearrange("p t (h w) -> p (t h) w", w=32)
                    vs = vstack[:, :, :, :].rearrange("p t h w -> p (t h) w")
                    hi = c_hi[:, :, :].bitcast(F32).rearrange("p t (h d) -> p (t h) d", d=8)
                    cs = ctxs[:, :, :].rearrange("p t (h d) -> p (t h) d", d=8)
                    dve.tensor_copy(ks[:, :, 0:8], hi)
                    dve.tensor_tensor(ks[:, :, 8:16], cs, hi, ALU.subtract)
                    dve.tensor_copy(ks[:, :, 16:24], hi)
                    dve.memset(ks[:, :, 24:25], 1.0)
                    dve.tensor_copy(vs[:, :, 0:8], cs)
                    dve.memset(vs[:, :, 8:9], 1.0)
                    dve.wait_ge(w_turned, 1)
                    dve.tensor_copy(gwT[:, :, :], bank[6][0:64, 0:128].rearrange("p (k n) -> p k n", k=2))\
                        .then_inc(gw_ready, 1)
                    for b in range(B):
                        dve.wait_ge(similar, b + 1)
                        m = dve.tensor_scalar(sim[:, TPB * b:TPB * (b + 1), :].rearrange("p i m -> p (i m)"),
                                              bank[b][:, :], 1.0 / 16, None, ALU.mult)
                    with nc.sbuf_tensor("rb_t", [P, 2560], F32) as tmp:
                        for i in range(TPB):
                            nh = 2560 // HD
                            src = brow[:, 0:2560].rearrange("p (s d) -> p s d", s=nh)
                            src2 = brow[:, 0:2560].rearrange("p (s two) -> p s two", two=2)
                            dst = rb[:, i, :].rearrange("p (s d) -> p s d", s=nh)
                            if i:
                                dve.wait_ge(own.sem, own.n)
                            v = own.up(dve.tensor_tensor(dst, src, bcast(rope[:, 0, i, :], nh), ALU.mult))
                            v = own.up(dve.tensor_copy(tmp[:, :].rearrange("p (s two) -> p s two", two=2),
                                                       src2[:, :, ::-1]))
                            dve.wait_ge(own.sem, v)
                            t3 = tmp[:, :].rearrange("p (s d) -> p s d", s=nh)
                            v = own.up(dve.tensor_tensor(t3, t3, bcast(rope[:, 1, i, :], nh), ALU.mult))
                            dve.wait_ge(own.sem, v)
                            v = own.up(dve.tensor_tensor(dst, dst, t3, ALU.add))

                @block.tensor
                def _(pe):
                    pe.wait_ge(const_loaded, N_CONST * 16)
                    for t in range(NT):
                        m = pe.transpose(bank[4 + t // 4][0:64, (t % 4) * P:(t % 4 + 1) * P], ctxs[:, t, :],
                                         cm.ident[:, :])
                        if t % 4 == 3:
                            m.then_inc(ctx_turned, 1)
                    for z in range(2):
                        m = pe.transpose(bank[6][0:64, z * 64:(z + 1) * 64], gw[:, z, :], cm.ident[0:64, 0:64])
                    m.then_inc(w_turned, 1)
                    pe.wait_ge(gw_ready, 1)
                    pe.wait_ge(ctxT_ready, 2)
                    for z in range(2):
                        for ht in range(2):
                            m = pe.matmul(bank[4 + ht if z == 0 else 6 + ht][0:64, :], gwT[:, z, :],
                                          ctxT[:, ht * 512:(ht + 1) * 512], start=True, stop=True)
                            m.then_inc(gq_done, 1)
                    pe.wait_ge(gq_ready, 4)
                    for b in range(B):
                        for i in range(TPB):
                            m = pe.matmul(bank[b][:, i * T:(i + 1) * T], gqT[:, 0, b * T + i * P:b * T + (i + 1) * P],
                                          gqT[:, 1, b * T:(b + 1) * T], start=True, stop=True, skip_group_check=True)
                        m.then_inc(similar, 1)

            tmp0.close()
            w0.wqkv, w0.wo, w0.bo = wqkv0, wo0, bo
            w0.bv = brow[:, 2560:3072]
            w0.cosw = lambda qk, i: rope[:, 0, i, :]
            w0.sinw = lambda qk, i: rope[:, 1, i, :]
            w0.rotb = lambda qk, g, i: rb[:, i, (2048 if qk else 512 * g):(2048 if qk else 512 * g) + 512]\
                .rearrange("p (s d) -> p s d", s=4)
            w0.prefetch = lambda sp: None
            w0.wait_tensor = lambda pe: (pe.wait_ge(w0_loaded, 7 * 16), pe.wait_ge(const_loaded, N_CONST * 16),
                                         pe.wait_ge(x_loaded, 16))
            attention_stage(nc, 0, cm, w0, A)
        release_semaphores(nc, cm)
        if stages >= 2:
            raw = [{n: moe.enter_context(nc.sbuf_tensor(f"raw_{n}{s}", [P, GCH if n == "d" else KC,
                                                                        C if n == "d" else GW], F32)) for n in "gud"}
                   for s in range(RAW)]
            raw_loaded = [sem(f"raw_loaded{s}") for s in range(RAW)]
            cross_attention_stage(nc, cm, kstack, vstack,
                                  lambda sp: [moe_load(sp, A, q, raw, raw_loaded) for q in range(RAW)])
        w1_loaded = sem("w1_loaded")
        if stages >= 3:
            def prefetch1(sp):
                for r in range(4):
                    sp.dma_start(wA[:, 2560 * r:2560 * (r + 1)].rearrange("p (r c) -> p r c", c=C),
                                 A["L1_attn_w_qkv"][1280 * r:1280 * (r + 1), :].rearrange("(r p) c -> p r c", p=P))\
                        .then_inc(w1_loaded, 16)

            moe_stage(nc, cm, A, raw, raw_loaded, sim, kth, kstack, prefetch1)
        moe.close()
        l0x.close()
        if stages >= 4:
            w1, keep1 = prepare_layer1(nc, cm, A, wA, sim, kth, w1_loaded)
            attention_stage(nc, 1, cm, w1, A)
            keep1.close()
            release_semaphores(nc, cm)
        if stages >= 6:
            dense_stage(nc, cm, A, wA, w1.ffn_loaded)

        with nc.Block("store") as block:
            @block.sync
            def _(sp):
                sp.dma_start(out.rearrange("b (i p) c -> p (b i) c", p=P), X[:, :, :]).then_inc(stored, 16)
                sp.wait_ge(stored, 16)


def constants():
    bf = np.dtype("bfloat16")
    k = {"c_ident": np.eye(P, dtype=np.float32), "c_identb": np.eye(P, dtype=np.float32).astype(bf),
         "c_maskb": np.triu(np.full((P, P), MASKED, np.float32), 1).astype(bf)}
    k["c_center"] = (np.eye(P) - 1.0 / P).astype(np.float32)
    had = np.ones((1, 1), np.float32)
    while len(had) < P:
        had = np.block([[had, had], [had, -had]])
    k["c_hadamard"] = had.astype(np.float32)
    sel = np.zeros((3 * NE, NCH * P), np.float32)
    for z in range(3):
        sel[z * NE + np.arange(NCH * P) // FE, np.arange(NCH * P)] = 1
    k["c_sel"] = sel.astype(bf)
    k["c_headmask"] = np.repeat(np.eye(4, dtype=np.float32), 32, axis=0)
    for layer, base in ((0, 10000.0), (1, 1000000.0)):
        inv = (1.0 / np.float32(base) ** (np.arange(0, HD, 2, dtype=np.float32) / np.float32(HD))).astype(np.float32)
        f = (np.arange(T, dtype=np.float32)[:, None] * inv[None, :]).astype(np.float32)
        c, s = np.cos(f), np.sin(f)
        cc = np.repeat(c, 2, axis=1)
        ss = np.stack([-s, s], axis=-1).reshape(T, HD)
        k[f"c_rope{layer}"] = np.stack([cc, ss]).astype(np.float32)
    return k


_INS = ['x', 'ctx_512', 'L0_attn_Wq', 'L0_attn_bq', 'L0_attn_Wk', 'L0_attn_bk', 'L0_attn_Wv', 'L0_attn_bv',
        'L0_attn_Wo', 'L0_attn_bo', 'L0_ffn_gate_w', 'L0_ffn_wg', 'L0_ffn_wu', 'L0_ffn_wd', 'L0_ffn_sg',
        'L0_ffn_su', 'L0_ffn_sd', 'L1_attn_w_qkv', 'L1_attn_w_o', 'L1_attn_q_norm_w', 'L1_attn_q_norm_b',
        'L1_attn_k_norm_w', 'L1_attn_k_norm_b', 'L1_xattn_Wq', 'L1_xattn_Wk', 'L1_xattn_gamma_raw', 'L1_ffn_W1',
        'L1_ffn_W2', 'L1_ffn_W3']


def kernel(**inputs):
    import numpy as _np
    import concourse.bacc as _bacc
    from concourse import mybir as _mybir
    from concourse.bass_utils import run_bass_kernel_spmd as _run

    nc = _bacc.Bacc("TRN2", target_bir_lowering=False, num_devices=1)
    arrays, A = {}, {}
    for name in _INS:
        a = _np.ascontiguousarray(inputs[name])
        if name == "L1_xattn_gamma_raw":
            a = a.reshape(1)
        arrays[f"in_{name}"] = a
    for name, a in constants().items():
        arrays[f"in_{name}"] = a
    for name, a in arrays.items():
        A[name[3:]] = nc.dram_tensor(name, a.shape, _mybir.dt.from_np(a.dtype), kind="ExternalInput").ap()
    out = nc.dram_tensor("out", (B, T, C), F32, kind="ExternalOutput").ap()
    decoder(nc, A, out)
    r = _run(nc, [arrays], core_ids=[0])
    return r.results[0]["out"]
```

```python
from contextlib import ExitStack

import numpy as np

import concourse.bass as bass
from concourse import mybir

F32 = mybir.dt.float32
F32R = mybir.dt.float32r
BF16 = mybir.dt.bfloat16
ALU = mybir.AluOpType
ACT = mybir.ActivationFunctionType
AX = mybir.AxisListType.X

P = 128
B, T, C = 4, 256, 256
NT = B * T // P
TPB = T // P
KC = C // P
HQ, HKV, HD = 16, 4, 128
LN_EPS = 1e-5
QK_EPS = 1e-6
MASKED = -1e30


class Count:

    def __init__(self, sem):
        self.sem, self.n = sem, 0

    def up(self, ins):
        ins.then_inc(self.sem, 1)
        self.n += 1
        return self.n


def bcast(ap, n, axis=1):
    shape = list(ap.shape)
    return ap.unsqueeze(axis).broadcast_to(shape[:axis] + [n] + shape[axis:])


class Common:
    pass


def attention_stage(nc, layer, cm, w, inputs):
    gated = layer == 1
    X, bank = cm.X, cm.bank
    NH = B * HQ
    ident, identb, maskb = cm.ident, cm.identb, cm.maskb
    scale = 0.25 if layer == 0 else HD ** -0.5
    kv_of = (lambda h: h // (HQ // HKV)) if gated else (lambda h: h % HKV)
    QW = HQ * HD
    KG, VG = HQ * HD // 512, HQ * HD // 512 + 1
    col0 = {g: 512 * g for g in range(KG)}
    if gated:
        col0[KG], col0[VG] = 2 * QW, 2 * QW + HKV * HD
    else:
        col0[KG], col0[VG] = QW, QW + HKV * HD
    turned = [(g, i) for g in (KG, 0, 1, 2, 3) for i in range(TPB)]
    NQ = len(turned)
    units = [("turned", g, i) for g, i in turned] + [("value", VG, i) for i in range(TPB)]
    NU = len(units)
    QLAG = 3 if gated else 2
    NSTEP = NU + QLAG
    PROJ_HEADS = 10 if gated else HQ - 1
    GATE_PAIRS = 10

    def steps_at(n):
        b, r = n // HQ + 1, n % HQ
        if b >= B or n >= NH:
            return []
        return [(b, k) for k in range(NSTEP) if k * PROJ_HEADS // NSTEP == r]

    def gates_at(n):
        b, r = n // HQ + 1, n % HQ - PROJ_HEADS
        if not gated or b >= B or n >= NH or r < 0:
            return []
        return [b * HQ // 2 + m for m in range(HQ // 2) if m * (HQ - PROJ_HEADS) // (HQ // 2) == r]

    uses = [("project", 0, k) for k in range(NU)]
    if gated:
        uses += [("gate", m) for m in range(HQ // 2)]
    for n in range(NH):
        uses += [("project", b, k) for b, k in steps_at(n) if k < NU]
        uses += [("gate", m) for m in gates_at(n)]
    use = {item: k for k, item in enumerate(uses)}

    with ExitStack() as ctx:
        def sb(name, shape, dt=F32):
            return ctx.enter_context(nc.sbuf_tensor(f"L{layer}_{name}", shape, dt))

        def sem(name):
            s = nc.alloc_semaphore(f"L{layer}_{name}")
            cm.stage_sems.append(s)
            return s

        xT = sb("xT", [P, 2, KC, T])
        QT = sb("QT", [P, 2, HQ, T])
        KT = sb("KT", [P, 2, HKV, T])
        V = sb("V", [P, 2, TPB, HKV * HD])
        NSIN = 1 if gated else 2
        t_cos = sb("t_cos", [P, 2, 512])
        t_sin = sb("t_sin", [P, NSIN, 512])
        q_rot = sb("q_rot", [P, 3, 512])
        prob = sb("prob", [P, 3, 384])
        probT = sb("probT", [P, 2, 384])
        outT = sb("outT", [P, 2, T])
        mx = sb("mx", [P, 4, 2])
        nmx = sb("nmx", [P, 4, 2])
        rsum = sb("rsum", [P, 4, 2])
        rinv = sb("rinv", [P, 4, 2])
        ln = LayerNorm(sb, sem)
        if gated:
            gateT = sb("gateT", [P, GATE_PAIRS, 2, T])
            ln_graph = LayerNorm(lambda n, s, dt=F32: sb("g" + n, s, dt), lambda n: sem("g" + n), ln.r, 1)
            r_scaled = Count(sem("r_scaled"))
            sq = sb("sq", [P, 512])
            ssum = sb("ssum", [P, 2, 4])
            eps = sb("eps", [P, 1])
            lnv = sb("lnv", [P, 2, 4])
            rstd = sb("rstd", [P, 2, 4])
        cosw, sinw = w.cosw, w.sinw
        if gated:
            rotb = w.rotb
        qb = sb("qb", [P, 2, 512])

        x_turned = sem("x_turned")
        xT_ready = sem("xT_ready")
        projected = sem("projected")
        proj_read = [sem("proj_read0"), sem("proj_read1")]
        rope_ready = sem("rope_ready")
        rope_read = sem("rope_read")
        q_ready = sem("q_ready")
        q_turned = sem("q_turned")
        qT_ready = sem("qT_ready")
        v_ready = sem("v_ready")
        scored = sem("scored")
        max_ready = sem("max_ready")
        exp_done = sem("exp_done")
        prob_ready = sem("prob_ready")
        prob_turned = sem("prob_turned")
        probT_ready = sem("probT_ready")
        out_done = sem("out_done")
        outT_ready = sem("outT_ready")
        y_done = sem("y_done")
        y_read = sem("y_read")
        copied = sem("copied")
        squared = sem("squared")
        log_done = sem("log_done")
        eps_ready = sem("eps_ready")
        rstd_ready = sem("rstd_ready")
        gate_ready = sem("gate_ready")
        vown = Count(sem("vector_own"))
        pown = Count(sem("pool_own"))
        aown = Count(sem("scalar_own"))

        b_score = [bank[0], bank[1]]
        b_proj = [bank[2], bank[3]]
        b_pT, b_out, b_turn, b_y = bank[4], bank[5], bank[6], bank[7]

        with nc.Block(f"attention{layer}") as block:

            @block.sync
            def _(sp):
                w.prefetch(sp)

            @block.tensor
            def _(pe):
                def project(b, k):
                    if k == 0:
                        if b >= 1:
                            pe.wait_ge(qT_ready, NQ * b)
                        for kc in range(KC):
                            for i in range(TPB):
                                m = pe.transpose(b_turn[:, kc * T + i * P:kc * T + (i + 1) * P],
                                                 X[:, TPB * b + i, kc * P:(kc + 1) * P], ident[:, :])
                        m.then_inc(x_turned, 1)
                        pe.wait_ge(xT_ready, b + 1)
                        if b == 0:
                            w.wait_qk(pe)
                    if k < NU:
                        kind, g, i = units[k]
                        if (b, k) == (0, NQ):
                            w.wait_v(pe)
                        u = use["project", b, k]
                        if u >= 2:
                            pe.wait_ge(proj_read[u % 2], u // 2)
                        for kc in range(KC):
                            m = pe.matmul(b_proj[u % 2][:, :], xT[:, b % 2, kc, i * P:(i + 1) * P],
                                          w.wqkv[:, kc, col0[g]:col0[g] + 512], start=(kc == 0), stop=(kc == KC - 1))
                        m.then_inc(projected, 1)
                    if QLAG <= k < NQ + QLAG:
                        a = NQ * b + k - QLAG
                        pe.wait_ge(q_ready, a + 1)
                        pe.wait_ge(xT_ready, b + 1)
                        if a >= 1:
                            pe.wait_ge(qT_ready, a)
                        for s in range(4):
                            m = pe.transpose(b_turn[:, s * P:(s + 1) * P], q_rot[:, a % 3, s * P:(s + 1) * P],
                                             ident[:, :])
                        m.then_inc(q_turned, 1)

                def gates(m):
                    u = use["gate", m]
                    pe.wait_ge(proj_read[u % 2], u // 2)
                    for s in range(2):
                        for kc in range(KC):
                            c0 = QW + (2 * m % HQ + s) * HD
                            ins = pe.matmul(b_proj[u % 2][:, s * T:(s + 1) * T], w.wqkv[:, kc, c0:c0 + HD],
                                            xT[:, 2 * m // HQ % 2, kc, :], start=(kc == 0 and s == 0),
                                            stop=(kc == KC - 1), skip_group_check=True)
                    ins.then_inc(projected, 1)

                def scores(n):
                    b, h = n // HQ, n % HQ
                    j, par, ps = kv_of(h), b % 2, b_score[n % 2]
                    pe.wait_ge(qT_ready, NQ * b + TPB * (h // 4 + 2))
                    if n >= 2:
                        pe.wait_ge(exp_done, n - 1)
                    pe.matmul(ps[:, 0:P], identb[:, :], maskb[:, :], start=True, stop=False, skip_group_check=True)
                    pe.matmul(ps[:, 0:P], QT[:, par, h, 0:P], KT[:, par, j, 0:P], start=False, stop=True,
                              skip_group_check=True)
                    pe.matmul(ps[:, P:3 * P], QT[:, par, h, P:T], KT[:, par, j, :], start=False, stop=False,
                              skip_group_check=True)
                    pe.matmul(ps[:, 2 * P:3 * P], identb[:, :], maskb[:, :], start=False, stop=True,
                              skip_group_check=True).then_inc(scored, 1)

                def turn_prob(n):
                    pe.wait_ge(prob_ready, n + 1)
                    if n >= 1:
                        pe.wait_ge(probT_ready, n)
                    for s in range(3):
                        m = pe.transpose(b_pT[:, s * P:(s + 1) * P], prob[:, n % 3, s * P:(s + 1) * P],
                                         ident[:, :])
                    m.then_inc(prob_turned, 1)

                def values(n):
                    b, j = n // HQ, kv_of(n % HQ)
                    pe.wait_ge(probT_ready, n + 1)
                    pe.wait_ge(v_ready, TPB * (b + 1))
                    if n >= 1:
                        pe.wait_ge(outT_ready, n)
                    pe.matmul(b_out[:, 0:T], V[:, b % 2, 0, j * HD:(j + 1) * HD], probT[:, n % 2, 0:T],
                              start=True, stop=False, skip_group_check=True)
                    pe.matmul(b_out[:, P:T], V[:, b % 2, 1, j * HD:(j + 1) * HD], probT[:, n % 2, T:T + P],
                              start=False, stop=True, skip_group_check=True).then_inc(out_done, 1)

                def output(n):
                    b, h = n // HQ, n % HQ
                    pe.wait_ge(outT_ready, n + 1)
                    if n == 0:
                        w.wait_o(pe)
                    if h == 0 and b >= 1:
                        pe.wait_ge(y_read, b)
                    for i in range(TPB):
                        m = pe.matmul(b_y[:, i * C:(i + 1) * C], outT[:, n % 2, i * P:(i + 1) * P], w.wo[:, h, :],
                                      start=(h == 0 and i == 0), stop=(h == HQ - 1), skip_group_check=True)
                    m.then_inc(y_done, 1)

                w.wait_x(pe)
                for k in range(NSTEP):
                    project(0, k)
                if gated:
                    for m in range(HQ // 2):
                        gates(m)
                for n in range(NH + 5):
                    if n < NH:
                        scores(n)
                    for b, k in steps_at(n)[:1]:
                        project(b, k)
                    for m in gates_at(n)[:1]:
                        gates(m)
                    if 2 <= n < NH + 2:
                        turn_prob(n - 2)
                    if 3 <= n < NH + 3:
                        values(n - 3)
                    for b, k in steps_at(n)[1:]:
                        project(b, k)
                    for m in gates_at(n)[1:]:
                        gates(m)
                    if 4 <= n < NH + 4:
                        output(n - 4)

            @block.scalar
            def _(act):
                def project(b, k):
                    if k == 0:
                        act.wait_ge(x_turned, b + 1)
                        act.activation(xT[:, b % 2].rearrange("p k t -> p (k t)"), b_turn[:, :], ACT.Copy)\
                           .then_inc(xT_ready, 1)
                    if gated and k < NU:
                        kind, g, i = units[k]
                        if kind == "turned":
                            u = use["project", b, k]
                            a = NQ * b + k
                            act.wait_ge(projected, u + 1)
                            if a >= 2:
                                act.wait_ge(rope_ready, a - 1)
                            act.activation(qb[:, a % 2, :], b_proj[u % 2][:, :], ACT.Copy).then_inc(copied, 1)
                            act.wait_ge(copied, a + 1)
                            act.sem_inc(proj_read[u % 2], 1)
                            if a == 0:
                                act.wait_ge(eps_ready, 1)
                            else:
                                act.wait_ge(squared, a)
                            if a >= 2:
                                act.wait_ge(log_done, a - 1)
                            for s in range(4):
                                m = act.activation(sq[:, s * P:(s + 1) * P], qb[:, a % 2, s * P:(s + 1) * P],
                                                   ACT.Square, accum_out=ssum[:, a % 2, s:s + 1])
                            m.then_inc(squared, 1)
                    if gated and 1 <= k <= NQ:
                        a = NQ * b + k - 1
                        act.wait_ge(squared, a + 1)
                        if a >= 2:
                            act.wait_ge(rstd_ready, a - 1)
                        act.activation(lnv[:, a % 2, :], ssum[:, a % 2, :], ACT.Ln, bias=eps[:, 0:1], scale=1.0 / HD)\
                           .then_inc(log_done, 1)
                        act.wait_ge(log_done, a + 1)
                        if a >= 2:
                            act.wait_ge(q_ready, a - 1)
                        act.activation(rstd[:, a % 2, :], lnv[:, a % 2, :], ACT.Exp, scale=-0.5)\
                           .then_inc(rstd_ready, 1)
                    if QLAG <= k < NQ + QLAG:
                        a = NQ * b + k - QLAG
                        g, i = turned[k - QLAG]
                        act.wait_ge(q_turned, a + 1)
                        if b >= 2:
                            act.wait_ge(scored, HQ * (b - 1))
                        dst = KT if g == KG else QT
                        h0 = 0 if g == KG else 4 * g
                        act.activation(dst[:, b % 2, h0:h0 + 4, i * P:(i + 1) * P],
                                       b_turn[:, :].rearrange("p (s t) -> p s t", s=4), ACT.Copy).then_inc(qT_ready, 1)

                def gates(m):
                    u = use["gate", m]
                    act.wait_ge(projected, u + 1)
                    if m >= GATE_PAIRS:
                        act.wait_ge(outT_ready, 2 * (m - GATE_PAIRS) + 2)
                    act.activation(gateT[:, m % GATE_PAIRS, :, :].rearrange("p s t -> p (s t)"), b_proj[u % 2][:, :],
                                   ACT.Tanh, scale=0.5).then_inc(gate_ready, 1)
                    act.wait_ge(gate_ready, m + 1)
                    act.sem_inc(proj_read[u % 2], 1)

                def exps(n):
                    act.wait_ge(max_ready, n + 1)
                    if n >= 3:
                        act.wait_ge(prob_turned, n - 2)
                    for i, (c0, c1) in enumerate(((0, P), (P, 3 * P))):
                        m = act.activation(prob[:, n % 3, c0:c1], b_score[n % 2][:, c0:c1], ACT.Exp,
                                           bias=nmx[:, n % 4, i:i + 1], scale=scale,
                                           accum_out=rsum[:, n % 4, i:i + 1])
                    m.then_inc(exp_done, 1)

                for k in range(NSTEP):
                    project(0, k)
                if gated:
                    act.preload_act_table_set("exp_and_others")
                    for m in range(HQ // 2):
                        gates(m)
                    act.preload_act_table_set("natural_log_exp_and_others")
                for n in range(NH + 8):
                    for b, k in steps_at(n)[:1]:
                        project(b, k)
                    if gates_at(n) and n % HQ == PROJ_HEADS:
                        act.preload_act_table_set("exp_and_others")
                    for m in gates_at(n)[:1]:
                        gates(m)
                    if 2 <= n < NH + 2:
                        act.wait_ge(prob_turned, n - 1)
                        if n >= 4:
                            act.wait_ge(out_done, n - 3)
                        act.activation(probT[:, n % 2, :], b_pT[:, 0:384], ACT.Copy).then_inc(probT_ready, 1)
                    if not gated and 3 <= n < NH + 3:
                        act.wait_ge(out_done, n - 2)
                        if n >= 5:
                            act.wait_ge(y_done, n - 4)
                        act.activation(outT[:, (n - 3) % 2, :], b_out[:, 0:T], ACT.Copy).then_inc(outT_ready, 1)
                    if n < NH:
                        exps(n)
                    for b, k in steps_at(n)[1:]:
                        project(b, k)
                    for m in gates_at(n)[1:]:
                        gates(m)
                    if gates_at(n) and n % HQ == HQ - 1:
                        act.preload_act_table_set("natural_log_exp_and_others")
                    if n >= HQ + 4 and (n - HQ - 4) % HQ == 0:
                        ln.rstd(act, (n - HQ - 4) // HQ)
                    if gated and n >= HQ + 6 and (n - HQ - 6) % HQ == 0:
                        ln_graph.rstd(act, (n - HQ - 6) // HQ)

            @block.vector
            def _(dve):
                def project(b, k):
                    if k >= NU:
                        return
                    kind, g, i = units[k]
                    u = use["project", b, k]
                    if kind == "turned":
                        a = NQ * b + k
                        qk = 1 if g == KG else 0
                        if gated:
                            dve.wait_ge(copied, a + 1)
                        else:
                            dve.wait_ge(projected, u + 1)
                            c0 = col0[g]
                            v = vown.up(dve.tensor_tensor(qb[:, a % 2, :], b_proj[u % 2][:, :],
                                                          w.bias[:, c0:c0 + 512], ALU.add))
                            dve.wait_ge(vown.sem, v)
                            dve.sem_inc(proj_read[u % 2], 1)
                        x = qb[:, a % 2, :]
                        ps4 = x.rearrange("p (s d) -> p s d", s=4)
                        pairs = x.rearrange("p (s e two) -> p s e two", s=4, two=2)
                        if a >= 2:
                            dve.wait_ge(rope_read if gated else q_ready, a - 1)
                        dve.tensor_tensor(t_cos[:, a % 2, :].rearrange("p (s d) -> p s d", s=4), ps4,
                                          bcast(cosw(qk, i), 4), ALU.mult)
                        v = vown.up(dve.tensor_tensor(
                            t_sin[:, a % NSIN, :].rearrange("p (s e two) -> p s e two", s=4, two=2),
                            pairs[:, :, :, ::-1],
                            bcast(sinw(qk, i).rearrange("p (e two) -> p e two", two=2), 4), ALU.mult))
                        dve.wait_ge(vown.sem, v)
                        if gated:
                            v = vown.up(dve.tensor_tensor(t_cos[:, a % 2, :], t_cos[:, a % 2, :], t_sin[:, a % NSIN, :],
                                                          ALU.add))
                            dve.wait_ge(vown.sem, v)
                        dve.sem_inc(rope_ready, 1)
                    elif kind == "value":
                        dve.wait_ge(projected, u + 1)
                        if b >= 2:
                            dve.wait_ge(out_done, HQ * (b - 1))
                        if gated:
                            v = vown.up(dve.tensor_copy(V[:, b % 2, i, :], b_proj[u % 2][:, :]))
                        else:
                            v = vown.up(dve.tensor_tensor(V[:, b % 2, i, :], b_proj[u % 2][:, :],
                                                          w.bias[:, col0[VG]:col0[VG] + 512], ALU.add))
                        dve.wait_ge(vown.sem, v)
                        dve.sem_inc(proj_read[u % 2], 1)
                        dve.sem_inc(v_ready, 1)

                def maxima(n):
                    ps = b_score[n % 2]
                    dve.wait_ge(scored, n + 1)
                    if n >= 4:
                        dve.wait_ge(exp_done, n - 3)
                    dve.tensor_reduce(mx[:, n % 4, 0:1], ps[:, 0:P], AX, ALU.max)
                    v = vown.up(dve.tensor_reduce(mx[:, n % 4, 1:2], ps[:, P:3 * P], AX, ALU.max))
                    dve.wait_ge(vown.sem, v)
                    dve.tensor_scalar(nmx[:, n % 4, :], mx[:, n % 4, :], -scale, None, ALU.mult).then_inc(max_ready, 1)

                def normalise(n):
                    dve.wait_ge(exp_done, n + 1)
                    v = vown.up(dve.reciprocal(rinv[:, n % 4, :], rsum[:, n % 4, :]))
                    dve.wait_ge(vown.sem, v)
                    for i, (c0, c1) in enumerate(((0, P), (P, 3 * P))):
                        m = dve.tensor_scalar(prob[:, n % 3, c0:c1], prob[:, n % 3, c0:c1], rinv[:, n % 4, i:i + 1],
                                              None, ALU.mult)
                    m.then_inc(prob_ready, 1)

                for k in range(NSTEP):
                    project(0, k)
                for n in range(NH + 8):
                    if n >= HQ + 4 and (n - HQ - 4) % HQ == 0:
                        b = (n - HQ - 4) // HQ
                        dve.wait_ge(y_done, HQ * (b + 1))
                        if gated and b:
                            dve.wait_ge(ln_graph.x_new, b)
                        ln.sums(dve, b, b_y[:, :].rearrange("p (i c) -> p i c", i=TPB), X, vown, y_read,
                                None if gated else w.bo)
                    if n >= HQ + 5 and (n - HQ - 5) % HQ == 0:
                        ln.scale(dve, (n - HQ - 5) // HQ, X)
                    if gated and n >= HQ + 6 and (n - HQ - 6) % HQ == 0:
                        b = (n - HQ - 6) // HQ
                        Xb = X[:, TPB * b:TPB * (b + 1), :]
                        dve.wait_ge(ln.x_new, b + 1)
                        v = r_scaled.up(dve.tensor_scalar(Xb, Xb, w.two_minus_gamma, None, ALU.mult))
                        dve.wait_ge(r_scaled.sem, v)
                        ln_graph.sums(dve, b, w.graph[:, TPB * b:TPB * (b + 1), :], X, vown, None, None)
                    if gated and n >= HQ + 7 and (n - HQ - 7) % HQ == 0:
                        ln_graph.scale(dve, (n - HQ - 7) // HQ, X)
                    if n < NH:
                        maxima(n)
                    if gated and 3 <= n < NH + 3:
                        a = n - 3
                        dve.wait_ge(out_done, a + 1)
                        if a >= 2:
                            dve.wait_ge(y_done, a - 1)
                        dve.wait_ge(gate_ready, a // 2 + 1)
                        dve.scalar_tensor_tensor(outT[:, a % 2, :], gateT[:, a // 2 % GATE_PAIRS, a % 2, :], 1.0,
                                                 b_out[:, 0:T], ALU.add, ALU.mult).then_inc(outT_ready, 1)
                    if 1 <= n < NH + 1:
                        normalise(n - 1)
                    for b, k in steps_at(n)[:1]:
                        project(b, k)
                    for b, k in steps_at(n)[1:]:
                        project(b, k)

            @block.gpsimd
            def _(pool):
                if gated:
                    pool.memset(eps[:, :], QK_EPS).then_inc(eps_ready, 1)
                for b in range(B):
                    for k in range(NQ):
                        g, i = turned[k]
                        a = NQ * b + k
                        qk = 1 if g == KG else 0
                        pool.wait_ge(rope_ready, a + 1)
                        if a >= 3:
                            pool.wait_ge(q_turned, a - 2)
                        q = q_rot[:, a % 3, :]
                        if gated:
                            q4 = q.rearrange("p (s d) -> p s d", s=4)
                            pool.wait_ge(rstd_ready, a + 1)
                            v = pown.up(pool.tensor_tensor(
                                q4, t_cos[:, a % 2, :].rearrange("p (s d) -> p s d", s=4),
                                rstd[:, a % 2, :].unsqueeze(2).broadcast_to([P, 4, HD]), ALU.mult))
                            pool.wait_ge(pown.sem, v)
                            pool.sem_inc(rope_read, 1)
                            pool.tensor_tensor(q4, q4, rotb(qk, i), ALU.add).then_inc(q_ready, 1)
                        else:
                            pool.tensor_tensor(q, t_cos[:, a % 2, :], t_sin[:, a % NSIN, :], ALU.add)\
                                .then_inc(q_ready, 1)


def cross_attention_stage(nc, cm, kstack, vstack, prefetch):
    X, bank, ident = cm.X, cm.bank, cm.ident
    G, D, J, SW = 4, 8, 4, 32
    scale = D ** -0.5
    NUNIT = 2 * B

    order = [("keys", 0, 0), ("queries", 0, 0)]
    for u in range(NUNIT + 3):
        for k in range(2 * J):
            if u < NUNIT:
                order.append(("maxima", u, k))
            if k < 2 and 2 <= u < NUNIT + 2:
                order.append(("scores", u - 2, 2 * J - 2 + k))
            if k >= 2 and 1 <= u < NUNIT + 1:
                order.append(("scores", u - 1, k - 2))
            if k == 1 and 1 <= u < NUNIT + 1:
                order.append(("queries_shifted", u - 1, 0))
            if k == 4 and u + 1 < NUNIT:
                order += [("keys", u + 1, 0), ("queries", u + 1, 0)]
            if k == 2 and u >= 4 and u % 2 == 0:
                order.append(("normalise", u // 2 - 2, 0))
            if k == 3 and 2 <= u < NUNIT + 2:
                order.append(("values", u - 2, 1))
            if k == 6 and 2 <= u < NUNIT + 2:
                order.append(("outputs", u - 2, 0))
            if k == 7 and 1 <= u < NUNIT + 1:
                order.append(("values", u - 1, 0))
    RING, FILLS = 6, {"queries_shifted": 2, "keys": 1, "queries": 2, "scores": 2, "maxima": 2, "outputs": 2}
    turn, n_fill = {}, 0
    for item in order:
        for h in range(FILLS.get(item[0], 0)):
            turn[item + (h,)] = (n_fill % RING, n_fill // RING)
            n_fill += 1

    with ExitStack() as ctx:
        def sb(name, shape, dt=F32):
            return ctx.enter_context(nc.sbuf_tensor(f"X0_{name}", shape, dt))

        def sem(name):
            return ctx.enter_context(nc.semaphore(f"X0_{name}"))

        x_hi = sb("x_hi", [P, TPB, C], F32R)
        qstack = sb("qstack", [P, 2, TPB, G, 2 * J, SW])
        qT = sb("qT", [P, 2, G * T], F32R)
        qTs = sb("qTs", [P, 2, G * T], F32R)
        kT = sb("kT", [P, 3, J, T], F32R)
        probT = sb("probT", [P, 2 * J, G * T])
        outT = sb("outT", [P, 2, G * T])
        mx = sb("mx", [P, 2, TPB, G, J])
        rden = sb("rden", [P, 2, G, J])
        att = sb("att", [P, 2, TPB, C])
        ln = LayerNorm(sb, sem)

        filled = [sem(f"bank_filled{s}") for s in range(RING)]
        read = [sem(f"bank_read{s}") for s in range(RING)]
        stack_zero = sem("stack_zero")
        hi_ready = sem("hi_ready")
        stack_ready = sem("stack_ready")
        maxima_in = sem("maxima_in")
        summed = sem("summed")
        outT_ready = sem("outT_ready")
        vown = Count(sem("vector_own"))

        acc = (bank[6], bank[7])
        tile_of = lambda k: (k // G, k % G)
        chunk_of = lambda k: (k // J, k % J)

        def wait_filled(eng, *fill):
            s, r = turn[fill]
            eng.wait_ge(filled[s], r + 1)
            return bank[s]

        def wait_free(eng, *fill):
            s, r = turn[fill]
            if r:
                eng.wait_ge(read[s], r)
            return bank[s]

        def wait_read(eng, kind, u, ks):
            last = {}
            for k in ks:
                for h in range(FILLS[kind]):
                    s, r = turn[kind, u, k, h]
                    last[s] = r + 1
            for s, r in last.items():
                eng.wait_ge(read[s], r)

        with nc.Block("cross_attention") as block:

            @block.sync
            def _(sp):
                prefetch(sp)

            @block.tensor
            def _(pe):
                for kind, u, k in order:
                    b, half = u // 2, u % 2
                    if kind == "keys":
                        to = wait_free(pe, kind, u, k, 0)
                        for i in range(TPB):
                            m = pe.transpose(to[:, i * P:(i + 1) * P],
                                             kstack[:, TPB * b + i, half * P:(half + 1) * P], ident[:, :])
                        m.then_inc(filled[turn[kind, u, k, 0][0]], 1)
                    elif kind in ("queries", "queries_shifted"):
                        if kind == "queries":
                            pe.wait_ge(stack_ready, b + 1)
                        else:
                            pe.wait_ge(maxima_in, u + 1)
                        for h in range(2):
                            to = wait_free(pe, kind, u, k, h)
                            for g in (2 * h, 2 * h + 1):
                                for i in range(TPB):
                                    c = (g % 2) * T + i * P
                                    m = pe.transpose(to[:, c:c + P],
                                                     qstack[:, b % 2, i, g, J * half:J * (half + 1), :]
                                                     .rearrange("p j w -> p (j w)"), ident[:, :])
                            m.then_inc(filled[turn[kind, u, k, h][0]], 1)
                    elif kind == "maxima":
                        i, g = tile_of(k)
                        if k == 0:
                            wait_read(pe, "keys", u, [0])
                            wait_read(pe, "queries", u, [0])
                        for h in range(2):
                            to = wait_free(pe, kind, u, k, h)
                            pe.matmul(to[:, :], qT[:, u % 2, g * T + i * P:g * T + (i + 1) * P],
                                      kT[:, u % 3, 2 * h:2 * h + 2, :].rearrange("p j t -> p (j t)"),
                                      start=True, stop=True).then_inc(filled[turn[kind, u, k, h][0]], 1)
                    elif kind == "scores":
                        c, j = chunk_of(k)
                        if k == 0:
                            wait_read(pe, "queries_shifted", u, [0])
                        for h in range(2):
                            to = wait_free(pe, kind, u, k, h)
                            pe.matmul(to[:, :], kT[:, u % 3, j, c * P:(c + 1) * P],
                                      qTs[:, u % 2, h * 512:(h + 1) * 512], start=True, stop=True)                              .then_inc(filled[turn[kind, u, k, h][0]], 1)
                    elif kind == "values":
                        wait_read(pe, "scores", u, range(J * k, J * (k + 1)))
                        if k == 0 and u >= 1:
                            pe.wait_ge(outT_ready, u)
                        for h in range(2):
                            for j in range(J):
                                m = pe.matmul(acc[h][SW * j:SW * (j + 1), :], vstack[:, TPB * b + k, J * half + j, :],
                                              probT[:, J * k + j, h * 512:(h + 1) * 512],
                                              start=(k == 0), stop=(k == 1))
                        m.then_inc(summed, 1)
                    elif kind == "outputs":
                        pe.wait_ge(outT_ready, u + 1)
                        for i in range(TPB):
                            to = wait_free(pe, kind, u, k, i)
                            for g in range(G):
                                m = pe.transpose(to[:, g * P:(g + 1) * P],
                                                 outT[:, u % 2, g * T + i * P:g * T + (i + 1) * P], ident[:, :])
                            m.then_inc(filled[turn[kind, u, k, i][0]], 1)

            @block.scalar
            def _(act):
                for kind, u, k in order:
                    if kind in ("queries", "queries_shifted"):
                        dst = qT if kind == "queries" else qTs
                        for h in range(2):
                            src = wait_filled(act, kind, u, k, h)
                            act.activation(dst[:, u % 2, h * 512:(h + 1) * 512], src[:, :], ACT.Copy)                               .then_inc(read[turn[kind, u, k, h][0]], 1)
                    elif kind == "keys":
                        src = wait_filled(act, kind, u, k, 0)
                        for j in range(J):
                            m = act.activation(kT[:, u % 3, j, :], src[:, 0:T], ACT.Copy,
                                               scale=cm.headmask[:, j:j + 1])
                        m.then_inc(read[turn[kind, u, k, 0][0]], 1)
                    elif kind == "scores":
                        c, j = chunk_of(k)
                        if u >= 1:
                            act.wait_ge(summed, 2 * (u - 1) + c + 1)
                        for h in range(2):
                            src = wait_filled(act, kind, u, k, h)
                            act.activation(probT[:, k, h * 512:(h + 1) * 512], src[:, :], ACT.Exp, scale=scale)                               .then_inc(read[turn[kind, u, k, h][0]], 1)
                    elif kind == "normalise":
                        ln.rstd(act, u)

            @block.vector
            def _(dve):
                def high(b):
                    if b >= 1:
                        dve.wait_ge(stack_ready, b)
                    dve.tensor_copy(x_hi[:, :, :], X[:, TPB * b:TPB * (b + 1), :]).then_inc(hi_ready, 1)

                high(0)
                for kind, u, k in order:
                    b, half = u // 2, u % 2
                    if kind == "maxima":
                        i, g = tile_of(k)
                        for h in range(2):
                            src = wait_filled(dve, kind, u, k, h)
                            dve.tensor_reduce(mx[:, u % 2, i, g, 2 * h:2 * h + 2],
                                              src[:, :].rearrange("p (j t) -> p j t", j=2), AX, ALU.max)                               .then_inc(read[turn[kind, u, k, h][0]], 1)
                        if k == 2 * J - 1:
                            wait_read(dve, kind, u, range(2 * J))
                            dve.tensor_scalar(
                                qstack[:, b % 2, :, :, J * half:J * (half + 1), 3 * D].rearrange("p i g j -> p (i g) j"),
                                mx[:, u % 2].rearrange("p i g j -> p (i g) j"), -1.0, None, ALU.mult)                               .then_inc(maxima_in, 1)
                            if half == 0 and b + 1 < B:
                                high(b + 1)
                    elif kind == "values" and k == 1:
                        dve.wait_ge(summed, 2 * u + 2)
                        for h in range(2):
                            m = dve.tensor_copy(outT[:, u % 2, h * 512:(h + 1) * 512], acc[h][:, :])
                        m.then_inc(outT_ready, 1)
                    elif kind == "outputs":
                        for i in range(TPB):
                            o = wait_filled(dve, kind, u, k, i)[:, :].rearrange("p (g j w) -> p g j w", g=G, j=J)
                            v = vown.up(dve.reciprocal(rden[:, i], o[:, :, :, D]))
                        dve.wait_ge(vown.sem, v)
                        for i in range(TPB):
                            s, r = turn[kind, u, k, i]
                            o = bank[s][:, :].rearrange("p (g j w) -> p g j w", g=G, j=J)
                            to = att[:, b % 2, i, half * P:(half + 1) * P].rearrange("p (j g d) -> p g j d", g=G, d=D)
                            dve.tensor_tensor(to, o[:, :, :, 0:D], rden[:, i].unsqueeze(3).broadcast_to([P, G, J, D]),
                                              ALU.mult).then_inc(read[s], 1)
                        if half == 1:
                            wait_read(dve, kind, u - 1, [0])
                            wait_read(dve, kind, u, [0])
                            ln.sums(dve, b, att[:, b % 2], X, vown, None, None)
                    elif kind == "normalise":
                        ln.scale(dve, u, X)

            @block.gpsimd
            def _(pool):
                for b in range(B):
                    if b < 2:
                        pool.memset(qstack[:, b], 0.0).then_inc(stack_zero, 1)
                        pool.wait_ge(stack_zero, b + 1)
                    pool.wait_ge(hi_ready, b + 1)
                    if b >= 2:
                        wait_read(pool, "queries_shifted", 2 * b - 3, [0])
                    for i in range(TPB):
                        hi = x_hi[:, i, :].bitcast(F32).rearrange("p (j g d) -> p g j d", g=G, d=D)
                        xx = X[:, TPB * b + i, :].rearrange("p (j g d) -> p g j d", g=G, d=D)
                        to = qstack[:, b % 2, i]
                        pool.tensor_copy(to[:, :, :, 0:D], hi)
                        pool.tensor_copy(to[:, :, :, D:2 * D], hi)
                        m = pool.tensor_tensor(to[:, :, :, 2 * D:3 * D], xx, hi, ALU.subtract)
                    m.then_inc(stack_ready, 1)


HT = 512


class GatedUnits:

    DLAG = 2

    def __init__(self, sb, sem, n_chunks, n_weighted, bank, xh, xl, w_up, w_down, own):
        self.bank, self.xh, self.xl, self.w_up, self.w_down, self.own = bank, xh, xl, w_up, w_down, own
        self.n_chunks, self.NU = n_chunks, 2 * n_chunks
        self.turn, k = {}, 0
        for n in range(self.NU):
            for kind in ("g", "u", "w")[:3 if n < n_weighted else 2]:
                self.turn[kind, n] = (k % 4, k // 4)
                k += 1
        self.silu = sb("silu", [P, 2, HT])
        self.act_f = sb("act_f", [P, 2, HT])
        self.act_c = sb("act_c", [P, 3, HT])
        self.act_h = sb("act_h", [P, 3, HT], F32R)
        self.act_l = sb("act_l", [P, 3, HT], F32R)
        self.yT = sb("yT", [P, KC, NT * P])
        self.filled = [sem(f"filled{s}") for s in range(4)]
        self.read = [sem(f"read{s}") for s in range(4)]
        self.silu_ready = sem("silu_ready")
        self.act_ready = sem("act_ready")
        self.act_hi_ready = sem("act_hi_ready")
        self.act_lo_ready = sem("act_lo_ready")
        self.down_done = sem("down_done")
        self.yT_ready = sem("yT_ready")
        self.y_turned = sem("y_turned")

    def hidden(self, pe, n, weights):
        c, ht = n // 2, n % 2
        tok = slice(HT * ht, HT * (ht + 1))
        for kind in "gu":
            s, rd = self.turn[kind, n]
            if rd:
                pe.wait_ge(self.read[s], rd)
            for kc in range(KC):
                H, L = self.w_up(kind, c, kc)
                for z, (a, x) in enumerate(((H, self.xh), (H, self.xl), (L, self.xh))):
                    m = pe.matmul(self.bank[s][:, :], a, x[:, kc, tok], start=(kc == 0 and z == 0),
                                  stop=(kc == KC - 1 and z == 2))
            m.then_inc(self.filled[s], 1)
        if ("w", n) in self.turn:
            s, rd = self.turn["w", n]
            if rd:
                pe.wait_ge(self.read[s], rd)
            weights(pe, n, self.bank[s], tok).then_inc(self.filled[s], 1)

    def down(self, pe, n):
        c, ht = n // 2, n % 2
        pe.wait_ge(self.act_lo_ready, n + 1)
        for dc in range(KC):
            H, L = self.w_down(c, dc)
            for z, (w, a) in enumerate(((H, self.act_h), (L, self.act_h), (H, self.act_l))):
                m = pe.matmul(self.bank[4 + 2 * ht + dc][:, :], w, a[:, n % 3, :], start=(c == 0 and z == 0),
                              stop=(c == self.n_chunks - 1 and z == 2))
        m.then_inc(self.down_done, 1)

    def turn_back(self, pe, b, ident):
        pe.wait_ge(self.yT_ready, b // 2 + 1)
        for i in range(TPB):
            for dc in range(KC):
                t = TPB * b + i
                m = pe.transpose(self.bank[b][:, i * C + dc * P:i * C + (dc + 1) * P],
                                 self.yT[:, dc, t * P:(t + 1) * P], ident[:, :])
        m.then_inc(self.y_turned, 1)

    def gate(self, act, n):
        s, rd = self.turn["g", n]
        act.wait_ge(self.filled[s], rd + 1)
        if n >= 2:
            act.wait_ge(self.act_ready, n - 1)
        act.activation(self.silu[:, n % 2, :], self.bank[s][:, :], ACT.Silu).then_inc(self.silu_ready, 1)
        act.wait_ge(self.silu_ready, n + 1)
        act.sem_inc(self.read[s], 1)

    def high(self, act, n):
        act.wait_ge(self.act_ready, n + 1)
        if n >= 3:
            act.wait_ge(self.down_done, n - 2)
        act.activation(self.act_h[:, n % 3, :], self.act_c[:, n % 3, :], ACT.Copy).then_inc(self.act_hi_ready, 1)

    def keep(self, act):
        act.wait_ge(self.down_done, self.NU)
        for ht in range(2):
            for dc in range(KC):
                m = act.activation(self.yT[:, dc, HT * ht:HT * (ht + 1)], self.bank[4 + 2 * ht + dc][:, :], ACT.Copy)
            m.then_inc(self.yT_ready, 1)

    def product(self, dve, n):
        s, rd = self.turn["u", n]
        dve.wait_ge(self.silu_ready, n + 1)
        dve.wait_ge(self.filled[s], rd + 1)
        if n >= 3:
            dve.wait_ge(self.act_lo_ready, n - 2)
        if ("w", n) in self.turn:
            v = self.own.up(dve.tensor_tensor(self.act_f[:, n % 2, :], self.bank[s][:, :], self.silu[:, n % 2, :],
                                              ALU.mult))
            dve.wait_ge(self.own.sem, v)
            dve.sem_inc(self.read[s], 1)
            s, rd = self.turn["w", n]
            dve.wait_ge(self.filled[s], rd + 1)
            dve.tensor_tensor(self.act_c[:, n % 3, :], self.bank[s][:, :], self.act_f[:, n % 2, :], ALU.mult)\
                .then_inc(self.act_ready, 1)
        else:
            dve.tensor_tensor(self.act_c[:, n % 3, :], self.bank[s][:, :], self.silu[:, n % 2, :], ALU.mult)\
                .then_inc(self.act_ready, 1)
        dve.wait_ge(self.act_ready, n + 1)
        dve.sem_inc(self.read[s], 1)

    def low(self, dve, n):
        dve.wait_ge(self.act_hi_ready, n + 1)
        dve.tensor_tensor(self.act_l[:, n % 3, :], self.act_c[:, n % 3, :], self.act_h[:, n % 3, :].bitcast(F32),
                          ALU.subtract).then_inc(self.act_lo_ready, 1)


def norm_all(dve, ln, units, bank, X, own):
    for b in range(B):
        dve.wait_ge(units.y_turned, b + 1)
        ln.sums(dve, b, bank[b][:, :].rearrange("p (i c) -> p i c", i=TPB), X, own, None, None)
        if b >= 1:
            ln.scale(dve, b - 1, X)
    ln.scale(dve, B - 1, X)


def turn_x(pe, X, bank, ident, x_turned):
    for ht in range(2):
        for kc in range(KC):
            for i in range(4):
                m = pe.transpose(bank[2 * ht + kc][:, i * P:(i + 1) * P],
                                 X[:, 4 * ht + i, kc * P:(kc + 1) * P], ident[:, :])
            m.then_inc(x_turned, 1)


def high_x(act, bank, xh, x_turned, xh_ready):
    for j in range(4):
        ht, kc = j // 2, j % 2
        act.wait_ge(x_turned, j + 1)
        act.activation(xh[:, kc, HT * ht:HT * (ht + 1)], bank[j][:, :], ACT.Copy).then_inc(xh_ready, 1)


def low_x(dve, bank, xh, xl, xh_ready, xl_ready):
    for j in range(4):
        ht, kc = j // 2, j % 2
        dve.wait_ge(xh_ready, j + 1)
        dve.tensor_tensor(xl[:, kc, HT * ht:HT * (ht + 1)], bank[j][:, :],
                          xh[:, kc, HT * ht:HT * (ht + 1)].bitcast(F32), ALU.subtract).then_inc(xl_ready, 1)


NE, FE, TOPK, FS = 32, 96, 6, 192
NCH = NE * FE // P
NSH = -(-FS // P)
GCH = 3
NGRP = NCH // GCH + 1
GW = GCH * P
RAW, SPLIT = 3, 2


def moe_loads(A, q):
    e0 = 4 * q
    for kc in range(KC):
        for name, n in (("g", "L0_ffn_wg"), ("u", "L0_ffn_wu")):
            yield (name, kc), A[n][e0:e0 + 4, kc * P:(kc + 1) * P, :].rearrange("e p f -> p e f")
    yield ("d", 0), A["L0_ffn_wd"].rearrange("e f d -> (e f) d")[GW * q:GW * (q + 1), :]\
        .rearrange("(c p) d -> p c d", p=P)


def moe_load(sp, A, q, raw, loaded):
    s = q % RAW
    if q < NGRP - 1:
        for (name, kc), src in moe_loads(A, q):
            if name == "d":
                dst = raw[s]["d"][:, :, :]
            else:
                dst = raw[s][name][:, kc, :].rearrange("p (e f) -> p e f", f=FE)
            sp.dma_start(dst, src).then_inc(loaded[s], 16)
        return
    for name, n in (("g", "L0_ffn_sg"), ("u", "L0_ffn_su")):
        sp.dma_start(raw[s][name][:, :, 0:FS], A[n].rearrange("(k p) f -> p k f", p=P)).then_inc(loaded[s], 16)
    sp.dma_start(raw[s]["d"][:, 0, :], A["L0_ffn_sd"][0:P, :]).then_inc(loaded[s], 16)
    sp.dma_start(raw[s]["d"][0:FS - P, 1, :], A["L0_ffn_sd"][P:FS, :]).then_inc(loaded[s], 16)


def moe_stage(nc, cm, A, raw, loaded, sim, kth, unranked, prefetch):
    X, bank, ident, identb = cm.X, cm.bank, cm.ident, cm.identb
    last_unit = lambda q: 2 * min(GCH * (q + 1), NCH + NSH) - 1
    with ExitStack() as ctx:
        def sb(name, shape, dt=F32):
            return ctx.enter_context(nc.sbuf_tensor(f"M_{name}", shape, dt))

        def sem(name):
            return ctx.enter_context(nc.semaphore(f"M_{name}"))

        xh = sb("xh", [P, KC, NT * P], F32R)
        xl = sb("xl", [P, KC, NT * P], F32R)
        hi = [{n: sb(f"hi_{n}{s}", [P, GCH if n == "d" else KC, C if n == "d" else GW], F32R) for n in "gud"}
              for s in range(SPLIT)]
        lo = [{n: sb(f"lo_{n}{s}", [P, GCH if n == "d" else KC, C if n == "d" else GW], F32R) for n in "gud"}
              for s in range(SPLIT)]
        gate_w = sb("gate_w", [P, KC, NE])
        gate_h = sb("gate_h", [P, KC, NE], F32R)
        gate_l = sb("gate_l", [P, KC, NE], F32R)
        sel = sb("sel", [3 * NE, NCH * P], BF16)
        score = sb("score", [P, NT, NE + 8])
        e_neg = sb("e_neg", [P, NT, NE])
        top = sb("top", [P, NT, 8])
        rest = sb("rest", [P, NT, NE + 8])
        den = sb("den", [P, NT])
        comb = sb("comb", [P, NT, NE])
        parts = sb("parts", [P, NT, 3, NE], BF16)
        combT = sb("combT", [3 * NE, NT * P], BF16)
        ln = LayerNorm(sb, sem)

        small_loaded = sem("small_loaded")
        x_turned = sem("x_turned")
        xh_ready = sem("xh_ready")
        xl_ready = sem("xl_ready")
        logits_done = sem("logits_done")
        exp_ready = sem("exp_ready")
        parts_ready = sem("parts_ready")
        parts_turned = sem("parts_turned")
        combT_ready = sem("combT_ready")
        gate_ready = sem("gate_ready")
        hi_ready = sem("hi_ready")
        lo_ready = sem("lo_ready")
        padded = sem("padded")
        vown = Count(sem("vector_own"))

        def w_up(kind, c, kc):
            q, r = c // GCH, c % GCH
            return (hi[q % SPLIT][kind][:, kc, r * P:(r + 1) * P], lo[q % SPLIT][kind][:, kc, r * P:(r + 1) * P])

        def w_down(c, dc):
            q, r = c // GCH, c % GCH
            return (hi[q % SPLIT]["d"][:, r, dc * P:(dc + 1) * P], lo[q % SPLIT]["d"][:, r, dc * P:(dc + 1) * P])

        un = GatedUnits(sb, sem, NCH + NSH, 2 * NCH, bank, xh, xl, w_up, w_down, vown)
        NU = un.NU

        NLOAD = [5] * (NGRP - 1) + [4]

        def group_loaded(q):
            return 16 * sum(NLOAD[p] for p in range(q % RAW, q + 1, RAW))

        with nc.Block("experts") as block:

            @block.sync
            def _(sp):
                sp.dma_start(gate_w[:, :, :], A["L0_ffn_gate_w"].rearrange("(k p) e -> p k e", p=P))\
                    .then_inc(small_loaded, 16)
                sp.dma_start(sel[:, :], A["c_sel"]).then_inc(small_loaded, 16)
                prefetch(sp)
                for q in range(RAW, NGRP):
                    sp.wait_ge(lo_ready, q - RAW + 1)
                    sp.wait_ge(hi_ready, q - RAW + 1)
                    if q == NGRP - 1:
                        sp.wait_ge(padded, 1)
                    moe_load(sp, A, q, raw, loaded)

            @block.tensor
            def _(pe):
                turn_x(pe, X, bank, ident, x_turned)
                pe.wait_ge(gate_ready, 2)
                pe.wait_ge(xl_ready, 4)
                for t in range(NT):
                    for kc in range(KC):
                        for n, (a, g) in enumerate(((xh, gate_h), (xh, gate_l), (xl, gate_h))):
                            m = pe.matmul(bank[4][:, NE * t:NE * (t + 1)], a[:, kc, t * P:(t + 1) * P], g[:, kc, :],
                                          start=(t == 0 and kc == 0 and n == 0), stop=(kc == KC - 1 and n == 2),
                                          skip_group_check=True)
                m.then_inc(logits_done, 1)

                def weights(pe, n, to, tok):
                    if n == 0:
                        pe.wait_ge(parts_ready, 1)
                        for t in range(NT):
                            m = pe.transpose(bank[5][0:3 * NE, :].bitcast(BF16)[:, t * P:(t + 1) * P],
                                             parts[:, t].rearrange("p z e -> p (z e)"), identb[:, :])
                        m.then_inc(parts_turned, 1)
                        pe.wait_ge(combT_ready, 1)
                    c = n // 2
                    return pe.matmul(to[:, :], sel[:, c * P:(c + 1) * P], combT[:, tok], start=True, stop=True)

                for n in range(NU + un.DLAG):
                    if n < NU:
                        if n % (2 * GCH) == 0:
                            pe.wait_ge(hi_ready, n // (2 * GCH) + 1)
                            pe.wait_ge(lo_ready, n // (2 * GCH) + 1)
                        un.hidden(pe, n, weights)
                    if n == 0:
                        pe.wait_ge(exp_ready, 1)
                    if n >= un.DLAG:
                        un.down(pe, n - un.DLAG)
                for b in range(B):
                    un.turn_back(pe, b, ident)

            @block.scalar
            def _(act):
                high_x(act, bank, xh, x_turned, xh_ready)
                act.wait_ge(logits_done, 1)
                act.activation(e_neg[:, :, :].rearrange("p t e -> p (t e)"), bank[4][:, 0:NT * NE], ACT.Exp,
                               scale=-1.0).then_inc(exp_ready, 1)
                for n in range(NU + 1):
                    if n < NU:
                        un.gate(act, n)
                    if n >= 1:
                        un.high(act, n - 1)
                un.keep(act)
                for b in range(B):
                    ln.rstd(act, b)

            @block.vector
            def _(dve):
                def split_hi(q):
                    dve.wait_ge(loaded[q % RAW], group_loaded(q))
                    if q >= SPLIT:
                        dve.wait_ge(un.down_done, last_unit(q - SPLIT) + 1)
                    for name in "gud":
                        m = dve.tensor_copy(hi[q % SPLIT][name][:, :, :], raw[q % RAW][name][:, :, :])
                    m.then_inc(hi_ready, 1)

                dve.wait_ge(small_loaded, 32)
                dve.tensor_copy(gate_h[:, :, :], gate_w[:, :, :]).then_inc(gate_ready, 1)
                dve.wait_ge(gate_ready, 1)
                dve.tensor_tensor(gate_l[:, :, :], gate_w[:, :, :], gate_h[:, :, :].bitcast(F32), ALU.subtract)\
                    .then_inc(gate_ready, 1)
                low_x(dve, bank, xh, xl, xh_ready, xl_ready)
                split_hi(0)
                v = vown.up(dve.memset(score[:, :, :], -1.0))
                dve.wait_ge(exp_ready, 1)
                dve.wait_ge(vown.sem, v)
                v = vown.up(dve.tensor_scalar(e_neg[:, :, :], e_neg[:, :, :], 1.0, None, ALU.add))
                dve.wait_ge(vown.sem, v)
                v = vown.up(dve.reciprocal(score[:, :, 0:NE], e_neg[:, :, :]))
                dve.wait_ge(vown.sem, v)
                for t in range(NT):
                    v = vown.up(dve.max(top[:, t, :], score[:, t, :]))
                dve.wait_ge(vown.sem, v)
                v = vown.up(dve.memset(top[:, :, TOPK:8], -1.0))
                dve.wait_ge(vown.sem, v)
                for t in range(NT):
                    v = vown.up(dve.match_replace(rest[:, t, :], top[:, t, :], score[:, t, :], 0.0))
                dve.wait_ge(vown.sem, v)
                v = vown.up(dve.tensor_tensor(comb[:, :, :], score[:, :, 0:NE], rest[:, :, 0:NE], ALU.subtract))
                dve.wait_ge(vown.sem, v)
                v = vown.up(dve.tensor_reduce(den[:, :], comb[:, :, :], AX, ALU.add))
                dve.wait_ge(vown.sem, v)
                v = vown.up(dve.tensor_scalar(den[:, :], den[:, :], 1e-20, None, ALU.add))
                dve.wait_ge(vown.sem, v)
                v = vown.up(dve.reciprocal(den[:, :], den[:, :]))
                dve.wait_ge(vown.sem, v)
                v = vown.up(dve.tensor_tensor(comb[:, :, :], comb[:, :, :],
                                              den[:, :].unsqueeze(2).broadcast_to([P, NT, NE]), ALU.mult))
                for z in range(3):
                    dve.wait_ge(vown.sem, v)
                    v = vown.up(dve.tensor_copy(parts[:, :, z, :], comb[:, :, :]))
                    dve.wait_ge(vown.sem, v)
                    if z < 2:
                        v = vown.up(dve.tensor_tensor(comb[:, :, :], comb[:, :, :], parts[:, :, z, :], ALU.subtract))
                dve.sem_inc(parts_ready, 1)
                dve.wait_ge(parts_turned, 1)
                dve.tensor_copy(combT[:, :], bank[5][0:3 * NE, :].bitcast(BF16)).then_inc(combT_ready, 1)
                KTH = int(T * 0.3)
                rounds = -(-KTH // 8)
                assert KTH - 8 * (rounds - 1) == 4
                ranked = {}

                def rank(r, t, replace):
                    src = sim if r == 0 else unranked
                    if replace:
                        dve.wait_ge(vown.sem, ranked[t])
                        ranked[t] = vown.up(dve.match_replace(unranked[:, t, :], kth[:, t, :], src[:, t, :], -3e38))
                    else:
                        if r:
                            dve.wait_ge(vown.sem, ranked[t])
                        ranked[t] = vown.up(dve.max(kth[:, t, :], src[:, t, :]))

                ranking = [(r, t, replace) for r in range(rounds) for replace in (False, True)[:2 if r < rounds - 1 else 1]
                           for t in range(NT)]
                per_unit = -(-len(ranking) // NU)
                for n in range(NU + 1):
                    for item in ranking[per_unit * n:per_unit * (n + 1)]:
                        rank(*item)
                    if n < NU:
                        q = n // 2 // GCH + 1
                        if n % (2 * GCH) == 2 * GCH - 4 and q < NGRP:
                            split_hi(q)
                        un.product(dve, n)
                    if n >= 1:
                        un.low(dve, n - 1)
                norm_all(dve, ln, un, bank, X, vown)

            @block.gpsimd
            def _(pool):
                for q in range(NGRP):
                    pool.wait_ge(hi_ready, q + 1)
                    for name in "gud":
                        m = pool.tensor_tensor(lo[q % SPLIT][name][:, :, :], raw[q % RAW][name][:, :, :],
                                               hi[q % SPLIT][name][:, :, :].bitcast(F32), ALU.subtract)
                    m.then_inc(lo_ready, 1)
                    if q == NGRP - 1 - RAW:
                        s = (NGRP - 1) % RAW
                        pool.wait_ge(lo_ready, q + 1)
                        for name in "gu":
                            pool.memset(raw[s][name][:, :, FS:GW], 0.0)
                        pool.memset(raw[s]["d"][:, 1:GCH, :], 0.0).then_inc(padded, 1)


def prepare_layer1(nc, cm, A, wA, sim, kth, w1_loaded):
    bank, ident = cm.bank, cm.ident
    NR = (2 * HQ + 2 * HKV)
    centered = lambda r: r < HQ or 2 * HQ <= r < 2 * HQ + HKV
    keep = ExitStack()

    def sb(name, shape, dt=F32):
        return keep.enter_context(nc.sbuf_tensor(f"P1_{name}", shape, dt))

    def sem(name):
        return keep.enter_context(nc.semaphore(f"P1_{name}"))

    w = Weights()
    wT = sb("wT", [P, KC, NR * P])
    tab = sb("tab", [P, 3, 2, TPB, HD])
    gam = sb("gam", [P, 4])
    raw = wA[:, :].rearrange("p (r c) -> p r c", c=C)
    wo = wA[:, 0:HQ * C].rearrange("p (h n) -> p h n", h=HQ)
    with ExitStack() as ctx:
        def tmp(name, shape, dt=F32):
            return ctx.enter_context(nc.sbuf_tensor(f"P1_{name}", shape, dt))

        center = tmp("center", [P, P])
        wo_raw = tmp("wo_raw", [P, KC, HQ * HD])
        rope = tmp("rope", [P, 2, TPB, HD])
        norm = tmp("norm", [P, 4, HD])
        swapped = tmp("swapped", [P, 4, HD])
        sig = tmp("sig", [P, NT, T])
        loaded, filled, wo_loaded = sem("loaded"), sem("filled"), sem("wo_loaded")
        copied = [sem(f"copied{s}") for s in range(4)]
        sig_exp, a_ready, a_turned, gam_exp = sem("sig_exp"), sem("a_ready"), sem("a_turned"), sem("gam_exp")
        own = Count(sem("vector_own"))
        NG = NR // 4
        NF = KC * NG + HQ // 2

        with nc.Block("prepare1") as block:

            @block.sync
            def _(sp):
                sp.dma_start(center[:, :], A["c_center"]).then_inc(loaded, 16)
                sp.dma_start(rope[:, :, :, :], A["c_rope1"].rearrange("s (i p) d -> p s i d", p=P)).then_inc(loaded, 16)
                for z, name in enumerate(("q_norm_w", "k_norm_w", "q_norm_b", "k_norm_b")):
                    sp.dma_start(norm[:, z, :], A["L1_attn_" + name].partition_broadcast(P)).then_inc(loaded, 16)
                sp.dma_start(gam[:, 0:1], A["L1_xattn_gamma_raw"].partition_broadcast(P)).then_inc(loaded, 16)
                sp.dma_start(wo_raw[:, :, :], A["L1_attn_w_o"].rearrange("(k p) n -> p k n", p=P))\
                    .then_inc(wo_loaded, 16)

            @block.tensor
            def _(pe):
                pe.wait_ge(loaded, 7 * 16)
                pe.wait_ge(w1_loaded, 4 * 16)
                for z in range(NF):
                    to = bank[z % 4]
                    if z >= 4:
                        pe.wait_ge(copied[z % 4], z // 4)
                    if z < KC * NG:
                        kc = z % KC
                        for s in range(4):
                            r = 4 * (z // KC) + s
                            src, dst = raw[:, r, kc * P:(kc + 1) * P], to[:, s * P:(s + 1) * P]
                            if centered(r):
                                m = pe.matmul(dst, src, center[:, :], start=True, stop=True, skip_group_check=True)
                            else:
                                m = pe.transpose(dst, src, ident[:, :])
                    else:
                        if z == KC * NG:
                            pe.wait_ge(wo_loaded, 16)
                        h0 = 2 * (z - KC * NG)
                        for s in range(4):
                            h, nch = h0 + s // 2, s % 2
                            m = pe.transpose(to[:, s * P:(s + 1) * P], wo_raw[:, nch, h * HD:(h + 1) * HD], ident[:, :])
                    m.then_inc(filled, 1)
                pe.wait_ge(a_ready, 1)
                for b in range(B):
                    for i in range(TPB):
                        for j in range(TPB):
                            m = pe.transpose(bank[4 + b][:, i * T + j * P:i * T + (j + 1) * P],
                                             sig[:, TPB * b + j, i * P:(i + 1) * P], ident[:, :])
                    m.then_inc(a_turned, 1)

            def copy_out(eng, copy, halve, z):
                eng.wait_ge(filled, z + 1)
                if z < KC * NG:
                    dst = wT[:, z % KC, 512 * (z // KC):512 * (z // KC + 1)]
                else:
                    copy = halve
                    h0 = 2 * (z - KC * NG)
                    dst = wo[:, h0:h0 + 2, :].rearrange("p h n -> p (h n)")
                copy(dst, bank[z % 4][:, :]).then_inc(copied[z % 4], 1)

            @block.scalar
            def _(act):
                act.preload_act_table_set("natural_log_exp_and_others")
                act.wait_ge(loaded, 7 * 16)
                act.activation(gam[:, 1:2], gam[:, 0:1], ACT.Exp, scale=-1.0).then_inc(gam_exp, 1)
                act.activation(sig[:, :, :], sim[:, :, :], ACT.Exp, scale=-1.0).then_inc(sig_exp, 1)
                for z in range(0, NF, 2):
                    copy_out(act, lambda o, i: act.activation(o, i, ACT.Copy),
                             lambda o, i: act.activation(o, i, ACT.Copy, scale=0.5), z)

            @block.vector
            def _(dve):
                dve.wait_ge(gam_exp, 1)
                v = own.up(dve.tensor_scalar(gam[:, 1:2], gam[:, 1:2], 1.0, None, ALU.add))
                dve.wait_ge(own.sem, v)
                v = own.up(dve.reciprocal(gam[:, 1:2], gam[:, 1:2]))
                dve.wait_ge(own.sem, v)
                v = own.up(dve.tensor_scalar(gam[:, 2:3], gam[:, 1:2], -1.0, 2.0, ALU.mult, ALU.add))
                v = own.up(dve.tensor_scalar(gam[:, 3:4], gam[:, 1:2], 0.5, None, ALU.mult))
                dve.wait_ge(sig_exp, 1)
                v = own.up(dve.tensor_scalar(sig[:, :, :], sig[:, :, :], 1.0, None, ALU.add))
                dve.wait_ge(own.sem, v)
                v = own.up(dve.reciprocal(sig[:, :, :], sig[:, :, :]))
                dve.wait_ge(own.sem, v)
                for t in range(NT):
                    v = own.up(dve.scalar_tensor_tensor(sig[:, t, :], sim[:, t, :], kth[:, t, 3:4], sig[:, t, :],
                                                        ALU.is_ge, ALU.mult))
                dve.wait_ge(own.sem, v)
                dve.sem_inc(a_ready, 1)
                for z in range(1, NF, 2):
                    copy_out(dve, lambda o, i: dve.tensor_copy(o, i),
                             lambda o, i: dve.tensor_scalar(o, i, 0.5, None, ALU.mult), z)
                v = own.up(dve.tensor_copy(swapped[:, :, :].rearrange("p z (e two) -> p (z e) two", two=2),
                                           norm[:, :, :].rearrange("p z (e two) -> p (z e) two", two=2)[:, :, ::-1]))
                dve.wait_ge(own.sem, v)
                with nc.sbuf_tensor("P1_b_sin", [P, TPB, HD], F32) as b_sin:
                    for qk in range(2):
                        if qk:
                            dve.wait_ge(own.sem, v)
                        own.up(dve.tensor_tensor(tab[:, 0, qk], bcast(norm[:, qk, :], TPB), rope[:, 0], ALU.mult))
                        own.up(dve.tensor_tensor(tab[:, 1, qk], bcast(swapped[:, qk, :], TPB), rope[:, 1], ALU.mult))
                        own.up(dve.tensor_tensor(tab[:, 2, qk], bcast(norm[:, 2 + qk, :], TPB), rope[:, 0], ALU.mult))
                        v = own.up(dve.tensor_tensor(b_sin[:, :, :], bcast(swapped[:, 2 + qk, :], TPB), rope[:, 1],
                                                     ALU.mult))
                        dve.wait_ge(own.sem, v)
                        v = own.up(dve.tensor_tensor(tab[:, 2, qk], tab[:, 2, qk], b_sin[:, :, :], ALU.add))
                for b in range(B):
                    s = sim[:, TPB * b:TPB * (b + 1), :]
                    dve.wait_ge(a_turned, b + 1)
                    v = own.up(dve.tensor_tensor(s, bank[4 + b][:, :].rearrange("p (i m) -> p i m", i=TPB),
                                                 sig[:, TPB * b:TPB * (b + 1), :], ALU.add))
                    dve.wait_ge(own.sem, v)
                    v = own.up(dve.tensor_scalar(s, s, gam[:, 3:4], None, ALU.mult))

    w.wqkv, w.wo, w.bo = wT, wo, None
    w.cosw = lambda qk, i: tab[:, 0, qk, i, :]
    w.sinw = lambda qk, i: tab[:, 1, qk, i, :]
    w.rotb = lambda qk, i: bcast(tab[:, 2, qk, i, :], 4)
    w.wait_x = w.wait_qk = w.wait_v = w.wait_o = lambda pe: None
    w.graph, w.two_minus_gamma = sim, gam[:, 2:3]
    w.ffn_loaded = nc.alloc_semaphore("ffn_loaded")

    def prefetch(sp):
        for z, name in enumerate(("L1_ffn_W1", "L1_ffn_W3")):
            sp.dma_start(wA[:, 4096 + 2048 * z:6144 + 2048 * z].rearrange("p (r c) -> p r c", c=C),
                         A[name].rearrange("(r p) c -> p r c", p=P)).then_inc(w.ffn_loaded, 16)
        sp.dma_start(wA[:, 8192:10240].rearrange("p (k h) -> p k h", k=KC),
                     A["L1_ffn_W2"].rearrange("(k p) h -> p k h", p=P)).then_inc(w.ffn_loaded, 16)

    w.prefetch = prefetch
    return w, keep


def dense_stage(nc, cm, A, wA, ffn_loaded):
    X, bank, ident = cm.X, cm.bank, cm.ident
    HID = 1024
    NC_ = HID // P
    raw_up = {"g": wA[:, 4096:6144].rearrange("p (r c) -> p r c", c=C),
              "u": wA[:, 6144:8192].rearrange("p (r c) -> p r c", c=C)}
    raw_down = wA[:, 8192:10240].rearrange("p (k h) -> p k h", k=KC)
    with ExitStack() as ctx:
        def sb(name, shape, dt=F32):
            return ctx.enter_context(nc.sbuf_tensor(f"D_{name}", shape, dt))

        def sem(name):
            return ctx.enter_context(nc.semaphore(f"D_{name}"))

        xh = sb("xh", [P, KC, NT * P], F32R)
        xl = sb("xl", [P, KC, NT * P], F32R)
        up_h = {n: sb(f"up_h_{n}", [P, KC, HID], F32R) for n in "gu"}
        up_l = {n: sb(f"up_l_{n}", [P, KC, HID], F32R) for n in "gu"}
        mid = sb("mid", [P, 2, NC_, C])
        mid_h = sb("mid_h", [P, NC_, C], F32R)
        mid_l = sb("mid_l", [P, NC_, C], F32R)
        down_h = sb("down_h", [P, NC_, C], F32R)
        down_l = sb("down_l", [P, NC_, C], F32R)
        had = sb("had", [P, P])
        had_r = sb("had_r", [P, P], F32R)
        ln = LayerNorm(sb, sem)

        had_loaded = sem("had_loaded")
        filled = sem("prep_filled")
        hi_ready = sem("prep_hi_ready")
        lo_ready = sem("prep_lo_ready")
        mid_ready = sem("mid_ready")
        x_turned = sem("x_turned")
        xh_ready = sem("xh_ready")
        xl_ready = sem("xl_ready")
        had_ready = sem("had_ready")
        vown = Count(sem("vector_own"))
        fills = [("turn", z) for z in range(4)] + [("up", n, kc, r) for n in "gu" for kc in range(KC) for r in range(2)]             + [("had", z) for z in range(4)]

        def w_up(kind, c, kc):
            return up_h[kind][:, kc, c * P:(c + 1) * P], up_l[kind][:, kc, c * P:(c + 1) * P]

        def w_down(c, dc):
            return down_h[:, c, dc * P:(dc + 1) * P], down_l[:, c, dc * P:(dc + 1) * P]

        un = GatedUnits(sb, sem, NC_, 0, bank, xh, xl, w_up, w_down, vown)
        NU = un.NU

        def parts_of(f):
            if f[0] == "up":
                _, n, kc, r = f
                return up_h[n][:, kc, 512 * r:512 * (r + 1)], up_l[n][:, kc, 512 * r:512 * (r + 1)]
            z = f[1]
            return (down_h[:, 2 * z:2 * z + 2, :].rearrange("p k d -> p (k d)"),
                    down_l[:, 2 * z:2 * z + 2, :].rearrange("p k d -> p (k d)"))

        with nc.Block("dense") as block:

            @block.sync
            def _(sp):
                sp.dma_start(had[:, :], A["c_hadamard"]).then_inc(had_loaded, 16)

            @block.tensor
            def _(pe):
                turn_x(pe, X, bank, ident, x_turned)
                pe.wait_ge(ffn_loaded, 3 * 16)
                for n, f in enumerate(fills):
                    to = bank[4 + n % 4]
                    if n >= 4:
                        pe.wait_ge(lo_ready, n - 3)
                    if f[0] == "turn":
                        for s in range(4):
                            c, dc = 2 * f[1] + s // 2, s % 2
                            m = pe.transpose(to[:, s * P:(s + 1) * P], raw_down[:, dc, c * P:(c + 1) * P], ident[:, :])
                    elif f[0] == "up":
                        _, name, kc, r = f
                        for s in range(4):
                            m = pe.transpose(to[:, s * P:(s + 1) * P], raw_up[name][:, 4 * r + s, kc * P:(kc + 1) * P],
                                             ident[:, :])
                    else:
                        z = f[1]
                        pe.wait_ge(mid_ready, 2)
                        for p, src in enumerate((mid_h, mid_l)):
                            m = pe.matmul(to[:, :], had_r[:, :], src[:, 2 * z:2 * z + 2, :].rearrange("p k d -> p (k d)"),
                                          start=(p == 0), stop=(p == 1))
                    m.then_inc(filled, 1)
                pe.wait_ge(xl_ready, 4)
                pe.wait_ge(lo_ready, len(fills))
                for n in range(NU + un.DLAG):
                    if n < NU:
                        un.hidden(pe, n, None)
                    if n >= un.DLAG:
                        un.down(pe, n - un.DLAG)
                for b in range(B):
                    un.turn_back(pe, b, ident)

            @block.scalar
            def _(act):
                high_x(act, bank, xh, x_turned, xh_ready)
                for n, f in enumerate(fills):
                    if f[0] == "turn":
                        continue
                    act.wait_ge(filled, n + 1)
                    act.activation(parts_of(f)[0], bank[4 + n % 4][:, :], ACT.Copy).then_inc(hi_ready, 1)
                for n in range(NU + 1):
                    if n < NU:
                        un.gate(act, n)
                    if n >= 1:
                        un.high(act, n - 1)
                un.keep(act)
                for b in range(B):
                    ln.rstd(act, b)

            @block.vector
            def _(dve):
                dve.wait_ge(had_loaded, 16)
                dve.tensor_copy(had_r[:, :], had[:, :]).then_inc(had_ready, 1)
                low_x(dve, bank, xh, xl, xh_ready, xl_ready)
                for n, f in enumerate(fills):
                    dve.wait_ge(filled, n + 1)
                    if f[0] == "turn":
                        z = f[1]
                        dve.tensor_scalar(mid[:, 0, 2 * z:2 * z + 2, :].rearrange("p k d -> p (k d)"),
                                          bank[4 + n % 4][:, :], HID ** -0.5, None, ALU.mult).then_inc(lo_ready, 1)
                        continue
                    hi, lo = parts_of(f)
                    dve.wait_ge(hi_ready, n - 3)
                    dve.tensor_tensor(lo, bank[4 + n % 4][:, :], hi.bitcast(F32), ALU.subtract).then_inc(lo_ready, 1)
                for n in range(NU + 1):
                    if n < NU:
                        un.product(dve, n)
                    if n >= 1:
                        un.low(dve, n - 1)
                norm_all(dve, ln, un, bank, X, vown)

            @block.gpsimd
            def _(pool):
                own = Count(sem("pool_own"))
                pool.wait_ge(lo_ready, 4)
                for z in range(3):
                    a = mid[:, z % 2].rearrange("p (k two s) d -> p k two (s d)", two=2, s=1 << z)
                    o = mid[:, (z + 1) % 2].rearrange("p (k two s) d -> p k two (s d)", two=2, s=1 << z)
                    own.up(pool.tensor_tensor(o[:, :, 0], a[:, :, 0], a[:, :, 1], ALU.add))
                    v = own.up(pool.tensor_tensor(o[:, :, 1], a[:, :, 0], a[:, :, 1], ALU.subtract))
                    pool.wait_ge(own.sem, v)
                v = own.up(pool.tensor_copy(mid_h[:, :, :], mid[:, 1]))
                pool.wait_ge(own.sem, v)
                pool.sem_inc(mid_ready, 1)
                pool.tensor_tensor(mid_l[:, :, :], mid[:, 1], mid_h[:, :, :].bitcast(F32), ALU.subtract)\
                    .then_inc(mid_ready, 1)


class LayerNorm:

    def __init__(self, sb, sem, r=None, turn=0):
        self.r, self.turn = r if r is not None else sb("ln_r", [P, 2, TPB, C]), turn
        self.stats = sb("ln_stats", [P, 2, TPB, 6])
        self.mv = sb("ln_mv", [P, 2, TPB, 2])
        self.ve = sb("ln_ve", [P, 2, TPB])
        self.lv = sb("ln_lv", [P, 2, TPB])
        self.rs = sb("ln_rs", [P, 2, TPB])
        self.var_ready = sem("ln_var_ready")
        self.log_ready = sem("ln_log_ready")
        self.rstd_ready = sem("ln_rstd_ready")
        self.x_new = sem("x_new")

    def sums(self, dve, n, y, X, own, y_read, bias):
        r = self.r[:, (n + self.turn) % 2]
        Xb = X[:, TPB * n:TPB * (n + 1), :]
        if n >= 2:
            dve.wait_ge(self.x_new, n - 1)
        v = own.up(dve.tensor_tensor(r, y, Xb, ALU.add))
        dve.wait_ge(own.sem, v)
        if y_read is not None:
            dve.sem_inc(y_read, 1)
        if bias is not None:
            v = own.up(dve.tensor_tensor(r, r, bcast(bias[:, :], TPB), ALU.add))
            dve.wait_ge(own.sem, v)
        for i in range(TPB):
            v = own.up(dve.bn_stats(self.stats[:, n % 2, i, :], r[:, i, :]))
        dve.wait_ge(own.sem, v)
        for i in range(TPB):
            v = own.up(dve.bn_aggr(self.mv[:, n % 2, i, :], self.stats[:, n % 2, i, :]))
        dve.wait_ge(own.sem, v)
        dve.tensor_scalar(self.ve[:, n % 2, :], self.mv[:, n % 2, :, 1], LN_EPS, None, ALU.add)\
            .then_inc(self.var_ready, 1)

    def rstd(self, act, n):
        act.wait_ge(self.var_ready, n + 1)
        act.activation(self.lv[:, n % 2, :], self.ve[:, n % 2, :], ACT.Ln).then_inc(self.log_ready, 1)
        act.wait_ge(self.log_ready, n + 1)
        act.activation(self.rs[:, n % 2, :], self.lv[:, n % 2, :], ACT.Exp, scale=-0.5).then_inc(self.rstd_ready, 1)

    def scale(self, dve, n, X):
        dve.wait_ge(self.rstd_ready, n + 1)
        for i in range(TPB):
            m = dve.tensor_scalar(X[:, TPB * n + i, :], self.r[:, (n + self.turn) % 2, i, :], self.mv[:, n % 2, i, 0:1],
                                  self.rs[:, n % 2, i:i + 1], ALU.subtract, ALU.mult)
        m.then_inc(self.x_new, 1)


NBIAS = -(-(3072 + C) // 512)


class Weights:
    pass


def release_semaphores(nc, cm):
    nc.clear_and_free_semaphores(cm.stage_sems)
    nc.all_engine_barrier()
    cm.stage_sems = []


def decoder(nc, A, out, stages=6):
    with ExitStack() as ctx:
        def sb(name, shape, dt=F32):
            return ctx.enter_context(nc.sbuf_tensor(name, shape, dt))

        def sem(name):
            return ctx.enter_context(nc.semaphore(name))

        cm = Common()
        cm.stage_sems = []
        cm.X = X = sb("X", [P, NT, C])
        cm.ident = sb("ident", [P, P])
        cm.identb = sb("identb", [P, P], BF16)
        cm.maskb = sb("maskb", [P, P], BF16)
        cm.headmask = sb("headmask", [P, 4])
        cm.bank = [ctx.enter_context(nc.psum_tensor(f"bank{i}", [P, 512], F32)) for i in range(8)]
        x_loaded = sem("x_loaded")
        ctx_loaded = sem("ctx_loaded")
        bias_loaded = sem("bias_loaded")
        wv0_loaded = sem("wv0_loaded")
        wo0_loaded = sem("wo0_loaded")
        w0_loaded = sem("w0_loaded")
        stored = sem("stored")
        wA = sb("wA", [P, 10240])

        w0 = Weights()
        wqkv0 = wA[:, 0:6144].rearrange("p (k n) -> p k n", k=KC)
        wo0 = wA[:, 6144:10240].rearrange("p (h n) -> p h n", h=HQ)

        sim = sb("sim", [P, NT, T])
        kth = sb("kth", [P, NT, 8])
        l0x = ExitStack()
        moe = ExitStack()
        kstack = l0x.enter_context(nc.sbuf_tensor("kstack", [P, NT, 256], F32))
        vstack = l0x.enter_context(nc.sbuf_tensor("vstack", [P, NT, 8, 32], F32))
        with ExitStack() as l0:
            brow = l0.enter_context(nc.sbuf_tensor("brow", [P, 3072 + C], F32))
            bias1 = l0.enter_context(nc.sbuf_tensor("bias1", [1, 3072 + C], F32))
            rope = l0.enter_context(nc.sbuf_tensor("rope", [P, 2, TPB, HD], F32))
            ones1 = l0.enter_context(nc.sbuf_tensor("ones1", [1, P], F32))
            ctxs = l0.enter_context(nc.sbuf_tensor("ctxs", [P, NT, 64], F32))
            c_hi = l0.enter_context(nc.sbuf_tensor("c_hi", [P, NT, 64], F32R))
            gw = l0.enter_context(nc.sbuf_tensor("gw", [64, 2, 64], F32))
            gwT = l0.enter_context(nc.sbuf_tensor("gwT", [64, 2, 64], F32))
            stack_clear = sem("stack_clear")
            ctx_turned, w_turned, gw_ready, ctxT_ready = map(sem, ("ctx_turned", "w_turned", "gw_ready", "ctxT_ready"))
            bias_spread, bias_read, ones_ready = map(sem, ("bias_spread", "bias_read", "ones_ready"))
            gq_done, gq_ready, similar = map(sem, ("gq_done", "gq_ready", "similar"))
            bank = cm.bank
            tmp0 = ExitStack()
            ctxT = tmp0.enter_context(nc.sbuf_tensor("ctxT", [64, NT * P], F32))
            gqT = tmp0.enter_context(nc.sbuf_tensor("gqT", [64, 2, NT * P], F32))
            with nc.Block("prepare0") as block:

                @block.sync
                def _(sp):
                    sp.dma_start(cm.ident[:, :], A["c_ident"]).then_inc(ctx_loaded, 16)
                    sp.dma_start(ctxs[:, :, :], A["ctx_512"].rearrange("b (i p) c -> p (b i) c", p=P))\
                        .then_inc(ctx_loaded, 16)
                    for z, name in enumerate(("L1_xattn_Wq", "L1_xattn_Wk")):
                        sp.dma_start(gw[:, z, :], A[name]).then_inc(ctx_loaded, 16)
                    off = 0
                    for name, n in (("L0_attn_bq", 2048), ("L0_attn_bk", 512), ("L0_attn_bv", 512), ("L0_attn_bo", C)):
                        sp.dma_start(bias1[:, off:off + n], A[name].unsqueeze(0)).then_inc(bias_loaded, 16)
                        off += n
                    sp.dma_start(X[:, :, :], A["x"].rearrange("b (i p) c -> p (b i) c", p=P)).then_inc(x_loaded, 16)
                    for name, c0, n in (("L0_attn_Wk", 2048, 512), ("L0_attn_Wq", 0, 2048)):
                        sp.dma_start(wqkv0[:, :, c0:c0 + n], A[name].rearrange("(k p) n -> p k n", p=P))\
                          .then_inc(w0_loaded, 16)
                        if c0:
                            sp.dma_start(rope[:, :, :, :], A["c_rope0"].rearrange("s (i p) d -> p s i d", p=P))\
                              .then_inc(w0_loaded, 16)
                            for dst, name in ((cm.identb, "c_identb"), (cm.maskb, "c_maskb"),
                                              (cm.headmask, "c_headmask")):
                                sp.dma_start(dst[:, :], A[name]).then_inc(w0_loaded, 16)
                    sp.dma_start(wqkv0[:, :, 2560:3072], A["L0_attn_Wv"].rearrange("(k p) n -> p k n", p=P))\
                      .then_inc(wv0_loaded, 16)
                    sp.dma_start(wo0, A["L0_attn_Wo"].rearrange("(h d) n -> d h n", d=HD)).then_inc(wo0_loaded, 16)

                @block.scalar
                def _(act):
                    act.preload_act_table_set("natural_log_exp_and_others")
                    for ht in range(2):
                        act.wait_ge(ctx_turned, ht + 1)
                        act.activation(ctxT[:, ht * 512:(ht + 1) * 512], bank[4 + ht][0:64, :], ACT.Copy)\
                           .then_inc(ctxT_ready, 1)
                    for z in range(2):
                        for ht in range(2):
                            act.wait_ge(gq_done, 2 * z + ht + 1)
                            act.activation(gqT[:, z, ht * 512:(ht + 1) * 512], bank[4 + ht if z == 0 else 6 + ht][0:64, :],
                                           ACT.Copy).then_inc(gq_ready, 1)
                    for c in range(NBIAS):
                        act.wait_ge(bias_spread, c + 1)
                        n = min(512, 3072 + C - 512 * c)
                        act.activation(brow[:, 512 * c:512 * c + n], bank[4 + c % 4][:, 0:n], ACT.Copy)\
                           .then_inc(bias_read, 1)

                @block.gpsimd
                def _(pool):
                    pool.memset(ones1[:, :], 1.0).then_inc(ones_ready, 1)
                    pool.memset(kstack[:, :, :], 0.0).then_inc(stack_clear, 1)
                    pool.memset(vstack[:, :, :, :], 0.0).then_inc(stack_clear, 1)

                @block.vector
                def _(dve):
                    own = Count(sem("prep_vector_own"))
                    dve.wait_ge(ctx_loaded, 4 * 16)
                    v = own.up(dve.tensor_copy(c_hi[:, :, :], ctxs[:, :, :]))
                    dve.wait_ge(own.sem, v)
                    dve.wait_ge(stack_clear, 2)
                    ks = kstack[:, :, :].rearrange("p t (h w) -> p (t h) w", w=32)
                    vs = vstack[:, :, :, :].rearrange("p t h w -> p (t h) w")
                    hi = c_hi[:, :, :].bitcast(F32).rearrange("p t (h d) -> p (t h) d", d=8)
                    cs = ctxs[:, :, :].rearrange("p t (h d) -> p (t h) d", d=8)
                    dve.tensor_copy(ks[:, :, 0:8], hi)
                    dve.tensor_tensor(ks[:, :, 8:16], cs, hi, ALU.subtract)
                    dve.tensor_copy(ks[:, :, 16:24], hi)
                    dve.memset(ks[:, :, 24:25], 1.0)
                    dve.tensor_copy(vs[:, :, 0:8], cs)
                    dve.memset(vs[:, :, 8:9], 1.0)
                    dve.wait_ge(w_turned, 1)
                    dve.tensor_copy(gwT[:, :, :], bank[6][0:64, 0:128].rearrange("p (k n) -> p k n", k=2))\
                        .then_inc(gw_ready, 1)
                    for b in range(B):
                        dve.wait_ge(similar, b + 1)
                        m = dve.tensor_scalar(sim[:, TPB * b:TPB * (b + 1), :].rearrange("p i m -> p (i m)"),
                                              bank[b][:, :], 1.0 / 16, None, ALU.mult)

                @block.tensor
                def _(pe):
                    pe.wait_ge(ctx_loaded, 4 * 16)
                    for t in range(NT):
                        m = pe.transpose(bank[4 + t // 4][0:64, (t % 4) * P:(t % 4 + 1) * P], ctxs[:, t, :],
                                         cm.ident[:, :])
                        if t % 4 == 3:
                            m.then_inc(ctx_turned, 1)
                    for z in range(2):
                        m = pe.transpose(bank[6][0:64, z * 64:(z + 1) * 64], gw[:, z, :], cm.ident[0:64, 0:64])
                    m.then_inc(w_turned, 1)
                    pe.wait_ge(gw_ready, 1)
                    pe.wait_ge(ctxT_ready, 2)
                    for z in range(2):
                        for ht in range(2):
                            m = pe.matmul(bank[4 + ht if z == 0 else 6 + ht][0:64, :], gwT[:, z, :],
                                          ctxT[:, ht * 512:(ht + 1) * 512], start=True, stop=True)
                            m.then_inc(gq_done, 1)
                    pe.wait_ge(gq_ready, 4)
                    for b in range(B):
                        for i in range(TPB):
                            m = pe.matmul(bank[b][:, i * T:(i + 1) * T], gqT[:, 0, b * T + i * P:b * T + (i + 1) * P],
                                          gqT[:, 1, b * T:(b + 1) * T], start=True, stop=True, skip_group_check=True)
                        m.then_inc(similar, 1)
                    pe.wait_ge(bias_loaded, 4 * 16)
                    pe.wait_ge(ones_ready, 1)
                    for c in range(NBIAS):
                        if c >= 4:
                            pe.wait_ge(bias_read, c - 3)
                        n = min(512, 3072 + C - 512 * c)
                        pe.matmul(bank[4 + c % 4][:, 0:n], ones1[:, :], bias1[:, 512 * c:512 * c + n],
                                  start=True, stop=True).then_inc(bias_spread, 1)

            tmp0.close()
            w0.wqkv, w0.wo, w0.bo = wqkv0, wo0, brow[:, 3072:3072 + C]
            w0.bias = brow
            w0.cosw = lambda qk, i: rope[:, 0, i, :]
            w0.sinw = lambda qk, i: rope[:, 1, i, :]
            w0.prefetch = lambda sp: None
            w0.wait_x = lambda pe: pe.wait_ge(x_loaded, 16)
            w0.wait_qk = lambda pe: pe.wait_ge(w0_loaded, 6 * 16)
            w0.wait_v = lambda pe: pe.wait_ge(wv0_loaded, 16)
            w0.wait_o = lambda pe: pe.wait_ge(wo0_loaded, 16)
            attention_stage(nc, 0, cm, w0, A)
        release_semaphores(nc, cm)
        if stages >= 2:
            raw = [{n: moe.enter_context(nc.sbuf_tensor(f"raw_{n}{s}", [P, GCH if n == "d" else KC,
                                                                        C if n == "d" else GW], F32)) for n in "gud"}
                   for s in range(RAW)]
            raw_loaded = [sem(f"raw_loaded{s}") for s in range(RAW)]
            cross_attention_stage(nc, cm, kstack, vstack,
                                  lambda sp: [moe_load(sp, A, q, raw, raw_loaded) for q in range(RAW)])
        w1_loaded = sem("w1_loaded")
        if stages >= 3:
            def prefetch1(sp):
                for r in range(4):
                    sp.dma_start(wA[:, 2560 * r:2560 * (r + 1)].rearrange("p (r c) -> p r c", c=C),
                                 A["L1_attn_w_qkv"][1280 * r:1280 * (r + 1), :].rearrange("(r p) c -> p r c", p=P))\
                        .then_inc(w1_loaded, 16)

            moe_stage(nc, cm, A, raw, raw_loaded, sim, kth, kstack, prefetch1)
        moe.close()
        l0x.close()
        if stages >= 4:
            w1, keep1 = prepare_layer1(nc, cm, A, wA, sim, kth, w1_loaded)
            attention_stage(nc, 1, cm, w1, A)
            keep1.close()
            release_semaphores(nc, cm)
        if stages >= 6:
            dense_stage(nc, cm, A, wA, w1.ffn_loaded)

        with nc.Block("store") as block:
            @block.sync
            def _(sp):
                sp.dma_start(out.rearrange("b (i p) c -> p (b i) c", p=P), X[:, :, :]).then_inc(stored, 16)
                sp.wait_ge(stored, 16)


def constants():
    bf = np.dtype("bfloat16")
    k = {"c_ident": np.eye(P, dtype=np.float32), "c_identb": np.eye(P, dtype=np.float32).astype(bf),
         "c_maskb": np.triu(np.full((P, P), MASKED, np.float32), 1).astype(bf)}
    k["c_center"] = (np.eye(P) - 1.0 / P).astype(np.float32)
    had = np.ones((1, 1), np.float32)
    while len(had) < P:
        had = np.block([[had, had], [had, -had]])
    k["c_hadamard"] = had.astype(np.float32)
    sel = np.zeros((3 * NE, NCH * P), np.float32)
    for z in range(3):
        sel[z * NE + np.arange(NCH * P) // FE, np.arange(NCH * P)] = 1
    k["c_sel"] = sel.astype(bf)
    k["c_headmask"] = np.repeat(np.eye(4, dtype=np.float32), 32, axis=0)
    for layer, base in ((0, 10000.0), (1, 1000000.0)):
        inv = (1.0 / np.float32(base) ** (np.arange(0, HD, 2, dtype=np.float32) / np.float32(HD))).astype(np.float32)
        f = (np.arange(T, dtype=np.float32)[:, None] * inv[None, :]).astype(np.float32)
        c, s = np.cos(f), np.sin(f)
        cc = np.repeat(c, 2, axis=1)
        ss = np.stack([-s, s], axis=-1).reshape(T, HD)
        k[f"c_rope{layer}"] = np.stack([cc, ss]).astype(np.float32)
    return k


_INS = ['x', 'ctx_512', 'L0_attn_Wq', 'L0_attn_bq', 'L0_attn_Wk', 'L0_attn_bk', 'L0_attn_Wv', 'L0_attn_bv',
        'L0_attn_Wo', 'L0_attn_bo', 'L0_ffn_gate_w', 'L0_ffn_wg', 'L0_ffn_wu', 'L0_ffn_wd', 'L0_ffn_sg',
        'L0_ffn_su', 'L0_ffn_sd', 'L1_attn_w_qkv', 'L1_attn_w_o', 'L1_attn_q_norm_w', 'L1_attn_q_norm_b',
        'L1_attn_k_norm_w', 'L1_attn_k_norm_b', 'L1_xattn_Wq', 'L1_xattn_Wk', 'L1_xattn_gamma_raw', 'L1_ffn_W1',
        'L1_ffn_W2', 'L1_ffn_W3']


def kernel(**inputs):
    import numpy as _np
    import concourse.bacc as _bacc
    from concourse import mybir as _mybir
    from concourse.bass_utils import run_bass_kernel_spmd as _run

    nc = _bacc.Bacc("TRN2", target_bir_lowering=False, num_devices=1)
    arrays, A = {}, {}
    for name in _INS:
        a = _np.ascontiguousarray(inputs[name])
        if name == "L1_xattn_gamma_raw":
            a = a.reshape(1)
        arrays[f"in_{name}"] = a
    for name, a in constants().items():
        arrays[f"in_{name}"] = a
    for name, a in arrays.items():
        A[name[3:]] = nc.dram_tensor(name, a.shape, _mybir.dt.from_np(a.dtype), kind="ExternalInput").ap()
    out = nc.dram_tensor("out", (B, T, C), F32, kind="ExternalOutput").ap()
    decoder(nc, A, out)
    r = _run(nc, [arrays], core_ids=[0])
    return r.results[0]["out"]
```

```python
from contextlib import ExitStack

import numpy as np

import concourse.bass as bass
from concourse import mybir

F32 = mybir.dt.float32
F32R = mybir.dt.float32r
BF16 = mybir.dt.bfloat16
ALU = mybir.AluOpType
ACT = mybir.ActivationFunctionType
AX = mybir.AxisListType.X

P = 128
B, T, C = 4, 256, 256
NT = B * T // P
TPB = T // P
KC = C // P
HQ, HKV, HD = 16, 4, 128
LN_EPS = 1e-5
QK_EPS = 1e-6
MASKED = -1e30


class Count:

    def __init__(self, sem):
        self.sem, self.n = sem, 0

    def up(self, ins):
        ins.then_inc(self.sem, 1)
        self.n += 1
        return self.n


def stage_semaphore(nc, cm, name):
    s = nc.alloc_semaphore(name)
    cm.stage_sems.append(s)
    return s


def next_address(nc):
    return -(-nc.sbuf_base // 32) * 32


def bcast(ap, n, axis=1):
    shape = list(ap.shape)
    return ap.unsqueeze(axis).broadcast_to(shape[:axis] + [n] + shape[axis:])


class Common:
    pass


def attention_stage(nc, layer, cm, w, inputs):
    gated = layer == 1
    X, bank = cm.X, cm.bank
    NH = B * HQ
    ident, identb, maskb = cm.ident, cm.identb, cm.maskb
    scale = 0.25 if layer == 0 else HD ** -0.5
    kv_of = (lambda h: h // (HQ // HKV)) if gated else (lambda h: h % HKV)
    QW = HQ * HD
    KG, VG = HQ * HD // 512, HQ * HD // 512 + 1
    col0 = {g: 512 * g for g in range(KG)}
    if gated:
        col0[KG], col0[VG] = 2 * QW, 2 * QW + HKV * HD
    else:
        col0[KG], col0[VG] = QW, QW + HKV * HD
    turned = [(g, i) for g in (KG, 0, 1, 2, 3) for i in range(TPB)]
    NQ = len(turned)
    units = [("turned", g, i) for g, i in turned] + [("value", VG, i) for i in range(TPB)]
    NU = len(units)
    QLAG = 3 if gated else 2
    NSTEP = NU + QLAG
    PROJ_HEADS = 12 if gated else HQ - 1
    GATE_PAIRS = 10

    def steps_at(n):
        b, r = n // HQ + 1, n % HQ
        if b >= B or n >= NH:
            return []
        return [(b, k) for k in range(NSTEP) if k * PROJ_HEADS // NSTEP == r]

    def early(n):
        return [(b, k) for b, k in steps_at(n)[:1] if k]

    def late(n):
        return [(b, k) for b, k in steps_at(n) if (b, k) not in early(n)]

    def x_at(n):
        return [b for b, k in steps_at(n) if k == 0]

    def gates_at(n):
        b, r = n // HQ + 1, n % HQ - PROJ_HEADS
        if not gated or b >= B or n >= NH or r < 0:
            return []
        return [b * HQ // 2 + m for m in range(HQ // 2) if m * (HQ - PROJ_HEADS) // (HQ // 2) == r]

    first_gates = lambda k: [k - 2] if gated and 2 <= k < HQ // 2 + 2 else []
    uses = []
    for k in range(NSTEP):
        uses += [("project", 0, k)] if k < NU else []
        uses += [("gate", m) for m in first_gates(k)]
    for n in range(NH):
        uses += [("project", b, k) for b, k in steps_at(n) if k < NU]
        uses += [("gate", m) for m in gates_at(n)]
    use = {item: k for k, item in enumerate(uses)}

    with ExitStack() as ctx:
        def sb(name, shape, dt=F32):
            return ctx.enter_context(nc.sbuf_tensor(f"L{layer}_{name}", shape, dt))

        def sem(name):
            return stage_semaphore(nc, cm, f"L{layer}_{name}")

        xT = sb("xT", [P, KC, T]) if gated else None
        xh = sb("xh", [P, KC, T], F32R)
        xl = sb("xl", [P, KC, T], F32R)
        QT = sb("QT", [P, 2, HQ, T])
        KT = sb("KT", [P, 2, HKV, T])
        V = sb("V", [P, 2, TPB, HKV * HD])
        NSIN = 1 if gated else 2
        t_cos = sb("t_cos", [P, 2, 512])
        t_sin = sb("t_sin", [P, NSIN, 512])
        q_rot = sb("q_rot", [P, 3, 512])
        prob = sb("prob", [P, 3, 384])
        probT = sb("probT", [P, 2, 384])
        outT = sb("outT", [P, 2, T])
        mx = sb("mx", [P, 4, 2])
        nmx = sb("nmx", [P, 4, 2])
        rsum = sb("rsum", [P, 4, 2])
        rinv = sb("rinv", [P, 4, 2])
        ln = LayerNorm(sb, sem)
        if gated:
            gateT_at = next_address(nc)
            gateT = sb("gateT", [P, GATE_PAIRS, 2, T])
            ln_graph = LayerNorm(lambda n, s, dt=F32: sb("g" + n, s, dt), lambda n: sem("g" + n), ln.r, 1)
            r_scaled = Count(sem("r_scaled"))
            ssum = sb("ssum", [P, 2, 4])
            eps = sb("eps", [P, 1])
            lnv = sb("lnv", [P, 2, 4])
            rstd = sb("rstd", [P, 2, 4])
        cosw, sinw = w.cosw, w.sinw
        if gated:
            rotb = w.rotb
        qb = w.qb if gated else sb("qb", [P, 2, 512])

        x_turned = sem("x_turned")
        xh_ready = sem("xh_ready")
        xl_ready = sem("xl_ready")
        projected = sem("projected")
        proj_read = [sem("proj_read0"), sem("proj_read1")]
        rope_ready = sem("rope_ready")
        rope_read = sem("rope_read")
        q_ready = sem("q_ready")
        q_turned = sem("q_turned")
        qT_ready = sem("qT_ready")
        v_ready = sem("v_ready")
        scored = sem("scored")
        max_ready = sem("max_ready")
        exp_done = sem("exp_done")
        prob_ready = sem("prob_ready")
        prob_turned = sem("prob_turned")
        probT_ready = sem("probT_ready")
        out_done = sem("out_done")
        outT_ready = sem("outT_ready")
        y_done = sem("y_done")
        y_read = sem("y_read")
        copied = sem("copied")
        squared = sem("squared")
        log_done = sem("log_done")
        eps_ready = sem("eps_ready")
        rstd_ready = sem("rstd_ready")
        gate_kept = sem("gate_kept")
        xT_ready = sem("xT_ready")
        gate_ready = sem("gate_ready")
        vown = Count(sem("vector_own"))
        pown = Count(sem("pool_own"))
        aown = Count(sem("scalar_own"))

        b_score = [bank[0], bank[1]]
        b_proj = [bank[2], bank[3]]
        b_pT, b_out, b_turn, b_y = bank[4], bank[5], bank[6], bank[7]

        if gated:
            free = NH // 2 - GATE_PAIRS
            w.dense = dense = DensePreparation(
                nc, sem, w.wqkv, w.wqkv_at, w.ffn_raw, w.ffn_raw_at, gateT[:, free % GATE_PAIRS, 0, 0:P],
                gateT_at + 4 * 2 * T * (free % GATE_PAIRS), b_proj, len(uses))
        LAST = NH - HQ

        def normed_at(n, r):
            return n >= HQ + r and (n - HQ - r) % HQ == 0 and (not gated or n < NH)

        with nc.Block(f"attention{layer}") as block:

            @block.sync
            def _(sp):
                if gated:
                    sp.wait_ge(projected, use["project", B - 1, NU - 1] + 1)
                w.prefetch(sp)
                if gated:
                    sp.wait_ge(outT_ready, 2 * free + 2)
                    sp.dma_start(dense.had, inputs["c_hadamard"]).then_inc(dense.had_loaded, 16)

            @block.tensor
            def _(pe):
                def turn(b):
                    if b >= 1:
                        pe.wait_ge(qT_ready, NQ * b)
                    for kc in range(KC):
                        for i in range(TPB):
                            m = pe.transpose(b_turn[:, kc * T + i * P:kc * T + (i + 1) * P],
                                             X[:, TPB * b + i, kc * P:(kc + 1) * P], ident[:, :])
                    m.then_inc(x_turned, 1)

                def project(b, k):
                    if k == 0:
                        pe.wait_ge(xl_ready, b + 1)
                    if k < NU:
                        kind, g, i = units[k]
                        if b == 0 and i == 0:
                            w.wait_split(pe, g)
                        u = use["project", b, k]
                        if u >= 2:
                            pe.wait_ge(proj_read[u % 2], u // 2)
                        for kc in range(KC):
                            wh, wl = w.split(kc, g)
                            for z, (x, ww) in enumerate(((xh, wh), (xh, wl), (xl, wh))):
                                m = pe.matmul(b_proj[u % 2][:, :], x[:, kc, i * P:(i + 1) * P], ww,
                                              start=(kc == 0 and z == 0), stop=(kc == KC - 1 and z == 2))
                        m.then_inc(projected, 1)
                    if QLAG <= k < NQ + QLAG:
                        a = NQ * b + k - QLAG
                        pe.wait_ge(q_ready, a + 1)
                        if a >= 1:
                            pe.wait_ge(qT_ready, a)
                        if gated and k == QLAG:
                            pe.wait_ge(xT_ready, b + 1)
                        for s in range(4):
                            m = pe.transpose(b_turn[:, s * P:(s + 1) * P], q_rot[:, a % 3, s * P:(s + 1) * P],
                                             ident[:, :])
                        m.then_inc(q_turned, 1)

                def gates(m):
                    pe.wait_ge(xT_ready, 2 * m // HQ + 1)
                    u = use["gate", m]
                    pe.wait_ge(proj_read[u % 2], u // 2)
                    for s in range(2):
                        for kc in range(KC):
                            c0 = QW + (2 * m % HQ + s) * HD
                            ins = pe.matmul(b_proj[u % 2][:, s * T:(s + 1) * T], w.wqkv[:, kc, c0:c0 + HD],
                                            xT[:, kc, :], start=(kc == 0 and s == 0),
                                            stop=(kc == KC - 1), skip_group_check=True)
                    ins.then_inc(projected, 1)

                def scores(n):
                    b, h = n // HQ, n % HQ
                    j, par, ps = kv_of(h), b % 2, b_score[n % 2]
                    pe.wait_ge(qT_ready, NQ * b + TPB * (h // 4 + 2))
                    if n >= 2:
                        pe.wait_ge(exp_done, n - 1)
                    pe.matmul(ps[:, 0:P], QT[:, par, h, 0:P], KT[:, par, j, P:T], start=True, stop=False,
                              skip_group_check=True)
                    pe.matmul(ps[:, P:3 * P], QT[:, par, h, P:T], KT[:, par, j, :], start=False, stop=False,
                              skip_group_check=True)
                    pe.matmul(ps[:, 0:2 * P], identb[:, :], bcast(maskb[:, :], 2), start=False, stop=True,
                              skip_group_check=True).then_inc(scored, 1)

                def turn_prob(n):
                    pe.wait_ge(prob_ready, n + 1)
                    if n >= 1:
                        pe.wait_ge(probT_ready, n)
                    for s, to in enumerate((0, 2, 1)):
                        m = pe.transpose(b_pT[:, to * P:(to + 1) * P], prob[:, n % 3, s * P:(s + 1) * P],
                                         ident[:, :])
                    m.then_inc(prob_turned, 1)

                def values(n):
                    b, j = n // HQ, kv_of(n % HQ)
                    pe.wait_ge(probT_ready, n + 1)
                    pe.wait_ge(v_ready, TPB * (b + 1))
                    if n >= 1:
                        pe.wait_ge(outT_ready, n)
                    pe.matmul(b_out[:, 0:T], V[:, b % 2, 0, j * HD:(j + 1) * HD], probT[:, n % 2, 0:T],
                              start=True, stop=False, skip_group_check=True)
                    pe.matmul(b_out[:, P:T], V[:, b % 2, 1, j * HD:(j + 1) * HD], probT[:, n % 2, T:T + P],
                              start=False, stop=True, skip_group_check=True).then_inc(out_done, 1)

                def output(n):
                    b, h = n // HQ, n % HQ
                    pe.wait_ge(outT_ready, n + 1)
                    if n == 0:
                        w.wait_o(pe)
                    if h == 0 and b >= 1:
                        pe.wait_ge(y_read, b)
                    for i in range(TPB):
                        m = pe.matmul(b_y[:, i * C:(i + 1) * C], outT[:, n % 2, i * P:(i + 1) * P], w.wo[:, h, :],
                                      start=(h == 0 and i == 0), stop=(h == HQ - 1), skip_group_check=True)
                    m.then_inc(y_done, 1)

                w.wait_x(pe)
                turn(0)
                for k in range(NSTEP):
                    project(0, k)
                    for m in first_gates(k):
                        gates(m)
                for n in range(NH + 5):
                    if n < NH:
                        scores(n)
                    for b in x_at(n):
                        turn(b)
                    for b, k in early(n):
                        project(b, k)
                    for m in gates_at(n)[:1]:
                        gates(m)
                    if 2 <= n < NH + 2:
                        turn_prob(n - 2)
                    if 3 <= n < NH + 3:
                        values(n - 3)
                    for b, k in late(n):
                        project(b, k)
                    for m in gates_at(n)[1:]:
                        gates(m)
                    if 4 <= n < NH + 4:
                        output(n - 4)
                    if gated and LAST <= n < NH:
                        dense.tensor(pe, n - LAST, proj_read, w.ffn_loaded, ident)

            @block.scalar
            def _(act):
                def high_part(b):
                    act.wait_ge(x_turned, b + 1)
                    act.activation(xh[:, :, :].rearrange("p k t -> p (k t)"), b_turn[:, :], ACT.Copy)\
                       .then_inc(xh_ready, 1)

                def project(b, k):
                    if gated and k == 0:
                        act.wait_ge(xl_ready, b + 1)
                        act.activation(xT[:, :, :].rearrange("p k t -> p (k t)"), b_turn[:, :], ACT.Copy)\
                           .then_inc(xT_ready, 1)
                    if gated and k < NU:
                        kind, g, i = units[k]
                        if kind == "turned":
                            u = use["project", b, k]
                            a = NQ * b + k
                            act.wait_ge(projected, u + 1)
                            if a >= 2:
                                act.wait_ge(rope_ready, a - 1)
                            act.activation(qb[:, a % 2, :], b_proj[u % 2][:, :], ACT.Copy).then_inc(copied, 1)
                            act.wait_ge(copied, a + 1)
                            if a == 0:
                                act.wait_ge(eps_ready, 1)
                            if a >= 2:
                                act.wait_ge(log_done, a - 1)
                            for s in range(4):
                                m = act.activation(b_proj[u % 2][:, s * P:(s + 1) * P],
                                                   qb[:, a % 2, s * P:(s + 1) * P],
                                                   ACT.Square, accum_out=ssum[:, a % 2, s:s + 1])
                            m.then_inc(squared, 1)
                            act.wait_ge(squared, a + 1)
                            act.sem_inc(proj_read[u % 2], 1)
                    if gated and 1 <= k <= NQ:
                        a = NQ * b + k - 1
                        act.wait_ge(squared, a + 1)
                        if a >= 2:
                            act.wait_ge(rstd_ready, a - 1)
                        act.activation(lnv[:, a % 2, :], ssum[:, a % 2, :], ACT.Ln, bias=eps[:, 0:1], scale=1.0 / HD)\
                           .then_inc(log_done, 1)
                        act.wait_ge(log_done, a + 1)
                        if a >= 2:
                            act.wait_ge(q_ready, a - 1)
                        act.activation(rstd[:, a % 2, :], lnv[:, a % 2, :], ACT.Exp, scale=-0.5)\
                           .then_inc(rstd_ready, 1)
                    if QLAG <= k < NQ + QLAG:
                        a = NQ * b + k - QLAG
                        g, i = turned[k - QLAG]
                        act.wait_ge(q_turned, a + 1)
                        if b >= 2:
                            act.wait_ge(scored, HQ * (b - 1))
                        dst = KT if g == KG else QT
                        h0 = 0 if g == KG else 4 * g
                        t = TPB - 1 - i if g == KG else i
                        act.activation(dst[:, b % 2, h0:h0 + 4, t * P:(t + 1) * P],
                                       b_turn[:, :].rearrange("p (s t) -> p s t", s=4), ACT.Copy).then_inc(qT_ready, 1)

                def gates(m):
                    u = use["gate", m]
                    act.wait_ge(projected, u + 1)
                    if m >= GATE_PAIRS:
                        act.wait_ge(outT_ready, 2 * (m - GATE_PAIRS) + 2)
                    act.activation(gateT[:, m % GATE_PAIRS, :, :].rearrange("p s t -> p (s t)"), b_proj[u % 2][:, :],
                                   ACT.Tanh, scale=0.5).then_inc(gate_ready, 1)
                    act.wait_ge(gate_ready, m + 1)
                    act.sem_inc(proj_read[u % 2], 1)

                def exps(n):
                    act.wait_ge(max_ready, n + 1)
                    if n >= 3:
                        act.wait_ge(prob_turned, n - 2)
                    for i, (c0, c1) in enumerate(((0, P), (P, 3 * P))):
                        m = act.activation(prob[:, n % 3, c0:c1], b_score[n % 2][:, c0:c1], ACT.Exp,
                                           bias=nmx[:, n % 4, i:i + 1], scale=scale,
                                           accum_out=rsum[:, n % 4, i:i + 1])
                    m.then_inc(exp_done, 1)

                high_part(0)
                for k in range(NSTEP):
                    if not gated and k % 2 == 0 and k // 2 < len(w.late):
                        w.high(act, w.late[k // 2])
                    project(0, k)
                    for m in first_gates(k):
                        u = use["gate", m]
                        act.wait_ge(projected, u + 1)
                        act.activation(gateT[:, m, :, :].rearrange("p s t -> p (s t)"), b_proj[u % 2][:, :], ACT.Copy)\
                           .then_inc(gate_kept, 1)
                        act.wait_ge(gate_kept, m + 1)
                        act.sem_inc(proj_read[u % 2], 1)
                if gated:
                    act.preload_act_table_set("exp_and_others")
                    m = HQ // 2
                    first = gateT[:, 0:m, :, :].rearrange("p m s t -> p (m s t)")
                    act.activation(first, first, ACT.Tanh, scale=0.5).then_inc(gate_ready, m)
                    act.preload_act_table_set("natural_log_exp_and_others")
                for n in range(NH + 8):
                    for b in x_at(n):
                        high_part(b)
                    for b, k in early(n):
                        project(b, k)
                    if gates_at(n) and n % HQ == PROJ_HEADS:
                        act.preload_act_table_set("exp_and_others")
                    for m in gates_at(n)[:1]:
                        gates(m)
                    if 2 <= n < NH + 2:
                        act.wait_ge(prob_turned, n - 1)
                        if n >= 4:
                            act.wait_ge(out_done, n - 3)
                        act.activation(probT[:, n % 2, :], b_pT[:, 0:384], ACT.Copy).then_inc(probT_ready, 1)
                    if not gated and 3 <= n < NH + 3:
                        act.wait_ge(out_done, n - 2)
                        if n >= 5:
                            act.wait_ge(y_done, n - 4)
                        act.activation(outT[:, (n - 3) % 2, :], b_out[:, 0:T], ACT.Copy).then_inc(outT_ready, 1)
                    if n < NH:
                        exps(n)
                    for b, k in late(n):
                        project(b, k)
                    for m in gates_at(n)[1:]:
                        gates(m)
                    if gated and LAST <= n < NH:
                        dense.scalar(act, n - LAST)
                    if gates_at(n) and n % HQ == HQ - 1:
                        act.preload_act_table_set("natural_log_exp_and_others")
                    if normed_at(n, 4):
                        ln.rstd(act, (n - HQ - 4) // HQ)
                    if gated and normed_at(n, 6):
                        ln_graph.rstd(act, (n - HQ - 6) // HQ)

            @block.vector
            def _(dve):
                def low_part(b):
                    dve.wait_ge(xh_ready, b + 1)
                    dve.tensor_tensor(xl[:, :, :].rearrange("p k t -> p (k t)"), b_turn[:, :],
                                      xh[:, :, :].bitcast(F32).rearrange("p k t -> p (k t)"), ALU.subtract)\
                        .then_inc(xl_ready, 1)

                def project(b, k):
                    if k >= NU:
                        return
                    kind, g, i = units[k]
                    u = use["project", b, k]
                    if kind == "turned":
                        a = NQ * b + k
                        qk = 1 if g == KG else 0
                        if gated:
                            dve.wait_ge(copied, a + 1)
                        else:
                            dve.wait_ge(projected, u + 1)
                            c0 = col0[g]
                            v = vown.up(dve.tensor_tensor(qb[:, a % 2, :], b_proj[u % 2][:, :],
                                                          w.bias[:, c0:c0 + 512], ALU.add))
                            dve.wait_ge(vown.sem, v)
                            dve.sem_inc(proj_read[u % 2], 1)
                        x = qb[:, a % 2, :]
                        ps4 = x.rearrange("p (s d) -> p s d", s=4)
                        pairs = x.rearrange("p (s e two) -> p s e two", s=4, two=2)
                        if a >= 2:
                            dve.wait_ge(rope_read if gated else q_ready, a - 1)
                        dve.tensor_tensor(t_cos[:, a % 2, :].rearrange("p (s d) -> p s d", s=4), ps4,
                                          bcast(cosw(qk, i), 4), ALU.mult)
                        v = vown.up(dve.tensor_tensor(
                            t_sin[:, a % NSIN, :].rearrange("p (s e two) -> p s e two", s=4, two=2),
                            pairs[:, :, :, ::-1],
                            bcast(sinw(qk, i).rearrange("p (e two) -> p e two", two=2), 4), ALU.mult))
                        dve.wait_ge(vown.sem, v)
                        if gated:
                            v = vown.up(dve.tensor_tensor(t_cos[:, a % 2, :], t_cos[:, a % 2, :], t_sin[:, a % NSIN, :],
                                                          ALU.add))
                            dve.wait_ge(vown.sem, v)
                        dve.sem_inc(rope_ready, 1)
                    elif kind == "value":
                        dve.wait_ge(projected, u + 1)
                        if b >= 2:
                            dve.wait_ge(out_done, HQ * (b - 1))
                        if gated:
                            v = vown.up(dve.tensor_copy(V[:, b % 2, i, :], b_proj[u % 2][:, :]))
                        else:
                            v = vown.up(dve.tensor_tensor(V[:, b % 2, i, :], b_proj[u % 2][:, :],
                                                          w.bias[:, col0[VG]:col0[VG] + 512], ALU.add))
                        dve.wait_ge(vown.sem, v)
                        dve.sem_inc(proj_read[u % 2], 1)
                        dve.sem_inc(v_ready, 1)

                def maxima(n):
                    ps = b_score[n % 2]
                    dve.wait_ge(scored, n + 1)
                    if n >= 4:
                        dve.wait_ge(exp_done, n - 3)
                    dve.tensor_reduce(mx[:, n % 4, 0:1], ps[:, 0:P], AX, ALU.max)
                    v = vown.up(dve.tensor_reduce(mx[:, n % 4, 1:2], ps[:, P:3 * P], AX, ALU.max))
                    dve.wait_ge(vown.sem, v)
                    dve.tensor_scalar(nmx[:, n % 4, :], mx[:, n % 4, :], -scale, None, ALU.mult).then_inc(max_ready, 1)

                def normalise(n):
                    dve.wait_ge(exp_done, n + 1)
                    v = vown.up(dve.reciprocal(rinv[:, n % 4, :], rsum[:, n % 4, :]))
                    dve.wait_ge(vown.sem, v)
                    for i, (c0, c1) in enumerate(((0, P), (P, 3 * P))):
                        m = dve.tensor_scalar(prob[:, n % 3, c0:c1], prob[:, n % 3, c0:c1], rinv[:, n % 4, i:i + 1],
                                              None, ALU.mult)
                    m.then_inc(prob_ready, 1)

                low_part(0)
                for k in range(NSTEP):
                    project(0, k)
                for n in range(NH + 8):
                    if normed_at(n, 4):
                        b = (n - HQ - 4) // HQ
                        dve.wait_ge(y_done, HQ * (b + 1))
                        if gated and b:
                            dve.wait_ge(ln_graph.x_new, b)
                        ln.sums(dve, b, b_y[:, :].rearrange("p (i c) -> p i c", i=TPB), X, vown, y_read,
                                None if gated else w.bo)
                    if normed_at(n, 5):
                        ln.scale(dve, (n - HQ - 5) // HQ, X)
                    if gated and normed_at(n, 6):
                        b = (n - HQ - 6) // HQ
                        Xb = X[:, TPB * b:TPB * (b + 1), :]
                        dve.wait_ge(ln.x_new, b + 1)
                        v = r_scaled.up(dve.tensor_scalar(Xb, Xb, w.two_minus_gamma, None, ALU.mult))
                        dve.wait_ge(r_scaled.sem, v)
                        ln_graph.sums(dve, b, w.graph[:, TPB * b:TPB * (b + 1), :], X, vown, None, None)
                    if gated and normed_at(n, 7):
                        ln_graph.scale(dve, (n - HQ - 7) // HQ, X)
                    if n < NH:
                        maxima(n)
                    for b in x_at(n):
                        low_part(b)
                    if gated and 3 <= n < NH + 3:
                        a = n - 3
                        dve.wait_ge(out_done, a + 1)
                        if a >= 2:
                            dve.wait_ge(y_done, a - 1)
                        dve.wait_ge(gate_ready, a // 2 + 1)
                        dve.scalar_tensor_tensor(outT[:, a % 2, :], gateT[:, a // 2 % GATE_PAIRS, a % 2, :], 1.0,
                                                 b_out[:, 0:T], ALU.add, ALU.mult).then_inc(outT_ready, 1)
                    if 1 <= n < NH + 1:
                        normalise(n - 1)
                    for b, k in early(n):
                        project(b, k)
                    for b, k in late(n):
                        project(b, k)
                    if gated and LAST <= n < NH:
                        dense.vector(dve, n - LAST)

            @block.gpsimd
            def _(pool):
                if gated:
                    pool.memset(eps[:, :], QK_EPS).then_inc(eps_ready, 1)
                for b in range(B):
                    for k in range(NQ):
                        g, i = turned[k]
                        a = NQ * b + k
                        qk = 1 if g == KG else 0
                        pool.wait_ge(rope_ready, a + 1)
                        if a >= 3:
                            pool.wait_ge(q_turned, a - 2)
                        q = q_rot[:, a % 3, :]
                        if gated:
                            q4 = q.rearrange("p (s d) -> p s d", s=4)
                            pool.wait_ge(rstd_ready, a + 1)
                            v = pown.up(pool.tensor_tensor(
                                q4, t_cos[:, a % 2, :].rearrange("p (s d) -> p s d", s=4),
                                rstd[:, a % 2, :].unsqueeze(2).broadcast_to([P, 4, HD]), ALU.mult))
                            pool.wait_ge(pown.sem, v)
                            pool.sem_inc(rope_read, 1)
                            pool.tensor_tensor(q4, q4, rotb(qk, i), ALU.add).then_inc(q_ready, 1)
                        else:
                            pool.tensor_tensor(q, t_cos[:, a % 2, :], t_sin[:, a % NSIN, :], ALU.add)\
                                .then_inc(q_ready, 1)
                            if a % 2 and a // 2 < len(w.late):
                                w.low(pool, w.late[a // 2])
                if gated:
                    dense.butterflies(pool)


def cross_attention_stage(nc, cm, kstack, vstack, prefetch, pad):
    X, bank, ident = cm.X, cm.bank, cm.ident
    G, D, J, SW = 4, 8, 4, 32
    scale = D ** -0.5
    NUNIT = 2 * B

    order = [("keys", 0, 0), ("queries", 0, 0)]
    for u in range(NUNIT + 3):
        for k in range(2 * J):
            if u < NUNIT:
                order.append(("maxima", u, k))
            if k < 2 and 2 <= u < NUNIT + 2:
                order.append(("scores", u - 2, 2 * J - 2 + k))
            if k >= 2 and 1 <= u < NUNIT + 1:
                order.append(("scores", u - 1, k - 2))
            if k == 1 and 1 <= u < NUNIT + 1:
                order.append(("queries_shifted", u - 1, 0))
            if k == 4 and u + 1 < NUNIT:
                order += [("keys", u + 1, 0), ("queries", u + 1, 0)]
            if k == 2 and u >= 4 and u % 2 == 0:
                order.append(("normalise", u // 2 - 2, 0))
            if k == 3 and 2 <= u < NUNIT + 2:
                order.append(("values", u - 2, 1))
            if k == 6 and 2 <= u < NUNIT + 2:
                order.append(("outputs", u - 2, 0))
            if k == 7 and 1 <= u < NUNIT + 1:
                order.append(("values", u - 1, 0))
    RING, FILLS = 6, {"queries_shifted": 2, "keys": 1, "queries": 2, "scores": 2, "maxima": 2, "outputs": 2}
    turn, n_fill = {}, 0
    for item in order:
        for h in range(FILLS.get(item[0], 0)):
            turn[item + (h,)] = (n_fill % RING, n_fill // RING)
            n_fill += 1

    with ExitStack() as ctx:
        def sb(name, shape, dt=F32):
            return ctx.enter_context(nc.sbuf_tensor(f"X0_{name}", shape, dt))

        def sem(name):
            return stage_semaphore(nc, cm, f"X0_{name}")

        x_hi = sb("x_hi", [P, TPB, C], F32R)
        qstack = sb("qstack", [P, 2, TPB, G, 2 * J, SW])
        qT = sb("qT", [P, 2, G * T], F32R)
        qTs = sb("qTs", [P, 2, G * T], F32R)
        kT = sb("kT", [P, 3, J, T], F32R)
        probT = sb("probT", [P, 2 * J, G * T])
        outT = sb("outT", [P, 2, G * T])
        mx = sb("mx", [P, 2, TPB, G, J])
        rden = sb("rden", [P, 2, G, J])
        att = sb("att", [P, 2, TPB, C])
        ln = LayerNorm(sb, sem)

        filled = [sem(f"bank_filled{s}") for s in range(RING)]
        read = [sem(f"bank_read{s}") for s in range(RING)]
        stack_zero = sem("stack_zero")
        hi_ready = sem("hi_ready")
        stack_ready = sem("stack_ready")
        maxima_in = sem("maxima_in")
        summed = sem("summed")
        outT_ready = sem("outT_ready")
        vown = Count(sem("vector_own"))

        acc = (bank[6], bank[7])
        tile_of = lambda k: (k // G, k % G)
        chunk_of = lambda k: (k // J, k % J)

        def wait_filled(eng, *fill):
            s, r = turn[fill]
            eng.wait_ge(filled[s], r + 1)
            return bank[s]

        def wait_free(eng, *fill):
            s, r = turn[fill]
            if r:
                eng.wait_ge(read[s], r)
            return bank[s]

        def wait_read(eng, kind, u, ks):
            last = {}
            for k in ks:
                for h in range(FILLS[kind]):
                    s, r = turn[kind, u, k, h]
                    last[s] = r + 1
            for s, r in last.items():
                eng.wait_ge(read[s], r)

        with nc.Block("cross_attention") as block:

            @block.sync
            def _(sp):
                prefetch(sp)

            @block.tensor
            def _(pe):
                for kind, u, k in order:
                    b, half = u // 2, u % 2
                    if kind == "keys":
                        to = wait_free(pe, kind, u, k, 0)
                        for i in range(TPB):
                            m = pe.transpose(to[:, i * P:(i + 1) * P],
                                             kstack[:, TPB * b + i, half * P:(half + 1) * P], ident[:, :])
                        m.then_inc(filled[turn[kind, u, k, 0][0]], 1)
                    elif kind in ("queries", "queries_shifted"):
                        if kind == "queries":
                            pe.wait_ge(stack_ready, b + 1)
                        else:
                            pe.wait_ge(maxima_in, u + 1)
                        for h in range(2):
                            to = wait_free(pe, kind, u, k, h)
                            for g in (2 * h, 2 * h + 1):
                                for i in range(TPB):
                                    c = (g % 2) * T + i * P
                                    m = pe.transpose(to[:, c:c + P],
                                                     qstack[:, b % 2, i, g, J * half:J * (half + 1), :]
                                                     .rearrange("p j w -> p (j w)"), ident[:, :])
                            m.then_inc(filled[turn[kind, u, k, h][0]], 1)
                    elif kind == "maxima":
                        i, g = tile_of(k)
                        if k == 0:
                            wait_read(pe, "keys", u, [0])
                            wait_read(pe, "queries", u, [0])
                        for h in range(2):
                            to = wait_free(pe, kind, u, k, h)
                            pe.matmul(to[:, :], qT[:, u % 2, g * T + i * P:g * T + (i + 1) * P],
                                      kT[:, u % 3, 2 * h:2 * h + 2, :].rearrange("p j t -> p (j t)"),
                                      start=True, stop=True).then_inc(filled[turn[kind, u, k, h][0]], 1)
                    elif kind == "scores":
                        c, j = chunk_of(k)
                        if k == 0:
                            wait_read(pe, "queries_shifted", u, [0])
                        for h in range(2):
                            to = wait_free(pe, kind, u, k, h)
                            pe.matmul(to[:, :], kT[:, u % 3, j, c * P:(c + 1) * P],
                                      qTs[:, u % 2, h * 512:(h + 1) * 512], start=True, stop=True)                              .then_inc(filled[turn[kind, u, k, h][0]], 1)
                    elif kind == "values":
                        wait_read(pe, "scores", u, range(J * k, J * (k + 1)))
                        if k == 0 and u >= 1:
                            pe.wait_ge(outT_ready, u)
                        for h in range(2):
                            for j in range(J):
                                m = pe.matmul(acc[h][SW * j:SW * (j + 1), :], vstack[:, TPB * b + k, J * half + j, :],
                                              probT[:, J * k + j, h * 512:(h + 1) * 512],
                                              start=(k == 0), stop=(k == 1))
                        m.then_inc(summed, 1)
                    elif kind == "outputs":
                        pe.wait_ge(outT_ready, u + 1)
                        for i in range(TPB):
                            to = wait_free(pe, kind, u, k, i)
                            for g in range(G):
                                m = pe.transpose(to[:, g * P:(g + 1) * P],
                                                 outT[:, u % 2, g * T + i * P:g * T + (i + 1) * P], ident[:, :])
                            m.then_inc(filled[turn[kind, u, k, i][0]], 1)

            @block.scalar
            def _(act):
                for kind, u, k in order:
                    if kind in ("queries", "queries_shifted"):
                        dst = qT if kind == "queries" else qTs
                        for h in range(2):
                            src = wait_filled(act, kind, u, k, h)
                            act.activation(dst[:, u % 2, h * 512:(h + 1) * 512], src[:, :], ACT.Copy)                               .then_inc(read[turn[kind, u, k, h][0]], 1)
                    elif kind == "keys":
                        src = wait_filled(act, kind, u, k, 0)
                        for j in range(J):
                            m = act.activation(kT[:, u % 3, j, :], src[:, 0:T], ACT.Copy,
                                               scale=cm.headmask[:, j:j + 1])
                        m.then_inc(read[turn[kind, u, k, 0][0]], 1)
                    elif kind == "scores":
                        c, j = chunk_of(k)
                        if u >= 1:
                            act.wait_ge(summed, 2 * (u - 1) + c + 1)
                        for h in range(2):
                            src = wait_filled(act, kind, u, k, h)
                            act.activation(probT[:, k, h * 512:(h + 1) * 512], src[:, :], ACT.Exp, scale=scale)                               .then_inc(read[turn[kind, u, k, h][0]], 1)
                    elif kind == "normalise":
                        ln.rstd(act, u)

            @block.vector
            def _(dve):
                def high(b):
                    if b >= 1:
                        dve.wait_ge(stack_ready, b)
                    dve.tensor_copy(x_hi[:, :, :], X[:, TPB * b:TPB * (b + 1), :]).then_inc(hi_ready, 1)

                high(0)
                for kind, u, k in order:
                    b, half = u // 2, u % 2
                    if kind == "maxima":
                        i, g = tile_of(k)
                        for h in range(2):
                            src = wait_filled(dve, kind, u, k, h)
                            dve.tensor_reduce(mx[:, u % 2, i, g, 2 * h:2 * h + 2],
                                              src[:, :].rearrange("p (j t) -> p j t", j=2), AX, ALU.max)                               .then_inc(read[turn[kind, u, k, h][0]], 1)
                        if k == 2 * J - 1:
                            wait_read(dve, kind, u, range(2 * J))
                            dve.tensor_scalar(
                                qstack[:, b % 2, :, :, J * half:J * (half + 1), 3 * D].rearrange("p i g j -> p (i g) j"),
                                mx[:, u % 2].rearrange("p i g j -> p (i g) j"), -1.0, None, ALU.mult)                               .then_inc(maxima_in, 1)
                            if half == 0 and b + 1 < B:
                                high(b + 1)
                    elif kind == "values" and k == 1:
                        dve.wait_ge(summed, 2 * u + 2)
                        for h in range(2):
                            m = dve.tensor_copy(outT[:, u % 2, h * 512:(h + 1) * 512], acc[h][:, :])
                        m.then_inc(outT_ready, 1)
                    elif kind == "outputs":
                        for i in range(TPB):
                            o = wait_filled(dve, kind, u, k, i)[:, :].rearrange("p (g j w) -> p g j w", g=G, j=J)
                            v = vown.up(dve.reciprocal(rden[:, i], o[:, :, :, D]))
                        dve.wait_ge(vown.sem, v)
                        for i in range(TPB):
                            s, r = turn[kind, u, k, i]
                            o = bank[s][:, :].rearrange("p (g j w) -> p g j w", g=G, j=J)
                            to = att[:, b % 2, i, half * P:(half + 1) * P].rearrange("p (j g d) -> p g j d", g=G, d=D)
                            dve.tensor_tensor(to, o[:, :, :, 0:D], rden[:, i].unsqueeze(3).broadcast_to([P, G, J, D]),
                                              ALU.mult).then_inc(read[s], 1)
                        if half == 1:
                            wait_read(dve, kind, u - 1, [0])
                            wait_read(dve, kind, u, [0])
                            ln.sums(dve, b, att[:, b % 2], X, vown, None, None)
                    elif kind == "normalise":
                        ln.scale(dve, u, X)

            @block.gpsimd
            def _(pool):
                for b in range(B):
                    if b < 2:
                        pool.memset(qstack[:, b], 0.0).then_inc(stack_zero, 1)
                        pool.wait_ge(stack_zero, b + 1)
                    pool.wait_ge(hi_ready, b + 1)
                    if b >= 2:
                        wait_read(pool, "queries_shifted", 2 * b - 3, [0])
                    for i in range(TPB):
                        hi = x_hi[:, i, :].bitcast(F32).rearrange("p (j g d) -> p g j d", g=G, d=D)
                        xx = X[:, TPB * b + i, :].rearrange("p (j g d) -> p g j d", g=G, d=D)
                        to = qstack[:, b % 2, i]
                        pool.tensor_copy(to[:, :, :, 0:D], hi)
                        pool.tensor_copy(to[:, :, :, D:2 * D], hi)
                        m = pool.tensor_tensor(to[:, :, :, 2 * D:3 * D], xx, hi, ALU.subtract)
                    m.then_inc(stack_ready, 1)
                pad(pool)


HT = 512


class GatedUnits:

    DLAG = 2

    def __init__(self, sb, sem, n_chunks, weighted_from, bank, xh, xl, w_up, w_down, own, by_half=False):
        self.bank, self.xh, self.xl, self.w_up, self.w_down, self.own = bank, xh, xl, w_up, w_down, own
        self.n_chunks, self.NU = n_chunks, 2 * n_chunks
        self.unit = (lambda n: (n % n_chunks, n // n_chunks)) if by_half else (lambda n: (n // 2, n % 2))
        self.half_done = [n_chunks, 2 * n_chunks] if by_half else [2 * n_chunks] * 2
        self.turn, k = {}, 0
        for n in range(self.NU):
            weighted = weighted_from is not None and n >= weighted_from
            for kind in ("p", "g", "u", "w")[0 if n == weighted_from else 1:4 if weighted else 3]:
                self.turn[kind, n] = (k % 4, k // 4)
                k += 1
        self.silu = sb("silu", [P, 2, HT])
        self.act_f = sb("act_f", [P, 2, HT])
        self.act_c = sb("act_c", [P, 3, HT])
        self.act_h = sb("act_h", [P, 3, HT], F32R)
        self.act_l = sb("act_l", [P, 3, HT], F32R)
        self.yT = sb("yT", [P, KC, NT * P])
        self.filled = [sem(f"filled{s}") for s in range(4)]
        self.read = [sem(f"read{s}") for s in range(4)]
        self.silu_ready = sem("silu_ready")
        self.act_ready = sem("act_ready")
        self.act_hi_ready = sem("act_hi_ready")
        self.act_lo_ready = sem("act_lo_ready")
        self.down_done = sem("down_done")
        self.yT_ready = sem("yT_ready")
        self.y_turned = sem("y_turned")

    def hidden(self, pe, n, weights):
        c, ht = self.unit(n)
        tok = slice(HT * ht, HT * (ht + 1))
        for kind in "gu":
            s, rd = self.turn[kind, n]
            if rd:
                pe.wait_ge(self.read[s], rd)
            for kc in range(KC):
                H, L = self.w_up(kind, c, kc)
                for z, (a, x) in enumerate(((H, self.xh), (H, self.xl), (L, self.xh))):
                    m = pe.matmul(self.bank[s][:, :], a, x[:, kc, tok], start=(kc == 0 and z == 0),
                                  stop=(kc == KC - 1 and z == 2))
            m.then_inc(self.filled[s], 1)
        if ("w", n) in self.turn:
            s, rd = self.turn["w", n]
            if rd:
                pe.wait_ge(self.read[s], rd)
            weights(pe, n, self.bank[s], tok).then_inc(self.filled[s], 1)

    def down(self, pe, n):
        c, ht = self.unit(n)
        pe.wait_ge(self.act_lo_ready, n + 1)
        for dc in range(KC):
            H, L = self.w_down(c, dc)
            for z, (w, a) in enumerate(((H, self.act_h), (L, self.act_h), (H, self.act_l))):
                m = pe.matmul(self.bank[4 + 2 * ht + dc][:, :], w, a[:, n % 3, :], start=(c == 0 and z == 0),
                              stop=(c == self.n_chunks - 1 and z == 2))
        m.then_inc(self.down_done, 1)

    def turn_back(self, pe, b, to, ident):
        pe.wait_ge(self.yT_ready, b // 2 + 1)
        for i in range(TPB):
            for dc in range(KC):
                t = TPB * b + i
                m = pe.transpose(to[:, i * C + dc * P:i * C + (dc + 1) * P],
                                 self.yT[:, dc, t * P:(t + 1) * P], ident[:, :])
        m.then_inc(self.y_turned, 1)

    def gate(self, act, n):
        s, rd = self.turn["g", n]
        act.wait_ge(self.filled[s], rd + 1)
        if n >= 2:
            act.wait_ge(self.act_ready, n - 1)
        act.activation(self.silu[:, n % 2, :], self.bank[s][:, :], ACT.Silu).then_inc(self.silu_ready, 1)
        act.wait_ge(self.silu_ready, n + 1)
        act.sem_inc(self.read[s], 1)

    def high(self, act, n):
        act.wait_ge(self.act_ready, n + 1)
        if n >= 3:
            act.wait_ge(self.down_done, n - 2)
        act.activation(self.act_h[:, n % 3, :], self.act_c[:, n % 3, :], ACT.Copy).then_inc(self.act_hi_ready, 1)

    def keep(self, act, ht):
        act.wait_ge(self.down_done, self.half_done[ht])
        for dc in range(KC):
            m = act.activation(self.yT[:, dc, HT * ht:HT * (ht + 1)], self.bank[4 + 2 * ht + dc][:, :], ACT.Copy)
        m.then_inc(self.yT_ready, 1)

    def product(self, dve, n):
        s, rd = self.turn["u", n]
        dve.wait_ge(self.silu_ready, n + 1)
        dve.wait_ge(self.filled[s], rd + 1)
        if n >= 3:
            dve.wait_ge(self.act_lo_ready, n - 2)
        if ("w", n) in self.turn:
            v = self.own.up(dve.tensor_tensor(self.act_f[:, n % 2, :], self.bank[s][:, :], self.silu[:, n % 2, :],
                                              ALU.mult))
            dve.wait_ge(self.own.sem, v)
            dve.sem_inc(self.read[s], 1)
            s, rd = self.turn["w", n]
            dve.wait_ge(self.filled[s], rd + 1)
            dve.tensor_tensor(self.act_c[:, n % 3, :], self.bank[s][:, :], self.act_f[:, n % 2, :], ALU.mult)\
                .then_inc(self.act_ready, 1)
        else:
            dve.tensor_tensor(self.act_c[:, n % 3, :], self.bank[s][:, :], self.silu[:, n % 2, :], ALU.mult)\
                .then_inc(self.act_ready, 1)
        dve.wait_ge(self.act_ready, n + 1)
        dve.sem_inc(self.read[s], 1)

    def low(self, dve, n):
        dve.wait_ge(self.act_hi_ready, n + 1)
        dve.tensor_tensor(self.act_l[:, n % 3, :], self.act_c[:, n % 3, :], self.act_h[:, n % 3, :].bitcast(F32),
                          ALU.subtract).then_inc(self.act_lo_ready, 1)


def turn_x(pe, X, to, ident, x_turned, ht):
    for kc in range(KC):
        for i in range(4):
            m = pe.transpose(to[2 * ht + kc][:, i * P:(i + 1) * P],
                             X[:, 4 * ht + i, kc * P:(kc + 1) * P], ident[:, :])
        m.then_inc(x_turned, 1)


def high_x(act, bank, xh, x_turned, xh_ready, ht):
    for kc in range(KC):
        act.wait_ge(x_turned, 2 * ht + kc + 1)
        act.activation(xh[:, kc, HT * ht:HT * (ht + 1)], bank[2 * ht + kc][:, :], ACT.Copy).then_inc(xh_ready, 1)


def low_x(dve, bank, xh, xl, xh_ready, xl_ready, ht):
    for kc in range(KC):
        dve.wait_ge(xh_ready, 2 * ht + kc + 1)
        dve.tensor_tensor(xl[:, kc, HT * ht:HT * (ht + 1)], bank[2 * ht + kc][:, :],
                          xh[:, kc, HT * ht:HT * (ht + 1)].bitcast(F32), ALU.subtract).then_inc(xl_ready, 1)


NE, FE, TOPK, FS = 32, 96, 6, 192
NCH = NE * FE // P
NSH = -(-FS // P)
GCH = 3
NGRP = NCH // GCH + 1
GW = GCH * P
RAW, SPLIT = 3, 2


def moe_loads(A, q):
    q -= 1
    e0 = 4 * q
    for kc in range(KC):
        for name, n in (("g", "L0_ffn_wg"), ("u", "L0_ffn_wu")):
            yield (name, kc), A[n][e0:e0 + 4, kc * P:(kc + 1) * P, :].rearrange("e p f -> p e f")
    yield ("d", 0), A["L0_ffn_wd"].rearrange("e f d -> (e f) d")[GW * q:GW * (q + 1), :]\
        .rearrange("(c p) d -> p c d", p=P)


def pad_shared(pool, raw, own):
    for name in "gu":
        pool.memset(raw[0][name][:, :, FS:GW], 0.0)
    v = own.up(pool.memset(raw[0]["d"][:, 2:GCH, :], 0.0))
    pool.wait_ge(own.sem, v)
    pool.memset(raw[0]["d"][FS - P:P, 1, :], 0.0)


def moe_load(sp, A, q, raw, loaded):
    s = q % RAW
    if q:
        for (name, kc), src in moe_loads(A, q):
            if name == "d":
                dst = raw[s]["d"][:, :, :]
            else:
                dst = raw[s][name][:, kc, :].rearrange("p (e f) -> p e f", f=FE)
            sp.dma_start(dst, src).then_inc(loaded[s], 16)
        return
    for name, n in (("g", "L0_ffn_sg"), ("u", "L0_ffn_su")):
        sp.dma_start(raw[s][name][:, :, 0:FS], A[n].rearrange("(k p) f -> p k f", p=P)).then_inc(loaded[s], 16)
    sp.dma_start(raw[s]["d"][:, 0, :], A["L0_ffn_sd"][0:P, :]).then_inc(loaded[s], 16)
    sp.dma_start(raw[s]["d"][0:FS - P, 1, :], A["L0_ffn_sd"][P:FS, :]).then_inc(loaded[s], 16)


def moe_stage(nc, cm, A, raw, loaded, gate_w, sel, small_loaded, sim, kth, unranked, prefetch):
    X, bank, ident, identb = cm.X, cm.bank, cm.ident, cm.identb
    first_chunk = lambda q: NSH + GCH * (q - 1) if q else 0
    last_unit = lambda q: 2 * first_chunk(q + 1) - 1

    def place(c):
        return (0, c) if c < NSH else (1 + (c - NSH) // GCH, (c - NSH) % GCH)

    with ExitStack() as ctx:
        def sb(name, shape, dt=F32):
            return ctx.enter_context(nc.sbuf_tensor(f"M_{name}", shape, dt))

        def sem(name):
            return stage_semaphore(nc, cm, f"M_{name}")

        xh = sb("xh", [P, KC, NT * P], F32R)
        xl = sb("xl", [P, KC, NT * P], F32R)
        hi = [{n: sb(f"hi_{n}{s}", [P, GCH if n == "d" else KC, C if n == "d" else GW], F32R) for n in "gud"}
              for s in range(SPLIT)]
        lo = [{n: sb(f"lo_{n}{s}", [P, GCH if n == "d" else KC, C if n == "d" else GW], F32R) for n in "gud"}
              for s in range(SPLIT)]
        gate_h = sb("gate_h", [P, KC, NE], F32R)
        gate_l = sb("gate_l", [P, KC, NE], F32R)
        score = sb("score", [P, NT, NE + 8])
        e_neg = sb("e_neg", [P, NT, NE])
        top = sb("top", [P, NT, 8])
        rest = sb("rest", [P, NT, NE + 8])
        den = sb("den", [P, NT])
        comb = sb("comb", [P, NT, NE])
        parts = sb("parts", [P, NT, 3, NE], BF16)
        combT = sb("combT", [3 * NE, NT * P], BF16)

        x_turned = sem("x_turned")
        xh_ready = sem("xh_ready")
        xl_ready = sem("xl_ready")
        logitsT_done = sem("logitsT_done")
        logitsT_ready = sem("logitsT_ready")
        logits_done = sem("logits_done")
        exp_ready = sem("exp_ready")
        parts_ready = sem("parts_ready")
        combT_ready = sem("combT_ready")
        gate_ready = sem("gate_ready")
        hi_ready = sem("hi_ready")
        lo_ready = sem("lo_ready")
        vown = Count(sem("vector_own"))

        def w_up(kind, c, kc):
            q, r = place(c)
            return (hi[q % SPLIT][kind][:, kc, r * P:(r + 1) * P], lo[q % SPLIT][kind][:, kc, r * P:(r + 1) * P])

        def w_down(c, dc):
            q, r = place(c)
            return (hi[q % SPLIT]["d"][:, r, dc * P:(dc + 1) * P], lo[q % SPLIT]["d"][:, r, dc * P:(dc + 1) * P])

        un = GatedUnits(sb, sem, NCH + NSH, 2 * NSH, bank, xh, xl, w_up, w_down, vown)
        NU = un.NU
        logitsT = un.yT[0:NE, 0, :]

        NLOAD = [4] + [5] * (NGRP - 1)

        def group_loaded(q):
            return 16 * sum(NLOAD[p] for p in range(q % RAW, q + 1, RAW))

        with nc.Block("experts") as block:

            @block.sync
            def _(sp):
                prefetch(sp)
                for q in range(RAW, NGRP):
                    sp.wait_ge(lo_ready, q - RAW + 1)
                    sp.wait_ge(hi_ready, q - RAW + 1)
                    moe_load(sp, A, q, raw, loaded)

            @block.tensor
            def _(pe):
                for ht in range(2):
                    turn_x(pe, X, bank, ident, x_turned, ht)
                pe.wait_ge(gate_ready, 2)
                pe.wait_ge(xl_ready, 4)
                for ht in range(2):
                    tok = slice(HT * ht, HT * (ht + 1))
                    for kc in range(KC):
                        for n, (g, a) in enumerate(((gate_h, xh), (gate_l, xh), (gate_h, xl))):
                            m = pe.matmul(bank[4 + ht][0:NE, :], g[:, kc, :], a[:, kc, tok],
                                          start=(kc == 0 and n == 0), stop=(kc == KC - 1 and n == 2))
                    m.then_inc(logitsT_done, 1)
                for t in range(NT):
                    if t % 4 == 0:
                        pe.wait_ge(logitsT_ready, t // 4 + 1)
                    m = pe.transpose(bank[6][:, NE * t:NE * (t + 1)], logitsT[:, t * P:(t + 1) * P],
                                     ident[0:NE, 0:NE])
                m.then_inc(logits_done, 1)

                def weights(pe, n, to, tok):
                    if n == 2 * NSH:
                        pe.wait_ge(combT_ready, 1)
                    c = n // 2 - NSH
                    return pe.matmul(to[:, :], sel[:, c * P:(c + 1) * P], combT[:, tok], start=True, stop=True)

                for n in range(NU + un.DLAG):
                    if n < NU:
                        q, r = place(n // 2)
                        if r == 0 and n % 2 == 0:
                            pe.wait_ge(hi_ready, q + 1)
                            pe.wait_ge(lo_ready, q + 1)
                        if n == 2 * NSH:
                            s, rd = un.turn["p", n]
                            pe.wait_ge(un.read[s], rd)
                            pe.wait_ge(parts_ready, 1)
                            for t in range(NT):
                                m = pe.transpose(bank[s][0:3 * NE, :].bitcast(BF16)[:, t * P:(t + 1) * P],
                                                 parts[:, t].rearrange("p z e -> p (z e)"), identb[:, :])
                            m.then_inc(un.filled[s], 1)
                        un.hidden(pe, n, weights)
                    if n == 0:
                        pe.wait_ge(exp_ready, 1)
                    if n >= un.DLAG:
                        un.down(pe, n - un.DLAG)
                for b in range(B):
                    un.turn_back(pe, b, bank[b], ident)

            @block.scalar
            def _(act):
                for ht in range(2):
                    high_x(act, bank, xh, x_turned, xh_ready, ht)
                for ht in range(2):
                    act.wait_ge(logitsT_done, ht + 1)
                    act.activation(logitsT[:, HT * ht:HT * (ht + 1)], bank[4 + ht][0:NE, :], ACT.Copy)\
                       .then_inc(logitsT_ready, 1)
                act.wait_ge(logits_done, 1)
                act.activation(e_neg[:, :, :].rearrange("p t e -> p (t e)"), bank[6][:, 0:NT * NE], ACT.Exp,
                               scale=-1.0).then_inc(exp_ready, 1)
                for n in range(NU + 1):
                    if n < NU:
                        un.gate(act, n)
                    if n >= 1:
                        un.high(act, n - 1)
                for ht in range(2):
                    un.keep(act, ht)

            @block.vector
            def _(dve):
                def split_hi(q):
                    dve.wait_ge(loaded[q % RAW], group_loaded(q))
                    if q >= SPLIT:
                        dve.wait_ge(un.down_done, last_unit(q - SPLIT) + 1)
                    for name in "gud":
                        m = dve.tensor_copy(hi[q % SPLIT][name][:, :, :], raw[q % RAW][name][:, :, :])
                    m.then_inc(hi_ready, 1)

                dve.wait_ge(small_loaded, 32)
                dve.tensor_copy(gate_h[:, :, :], gate_w[:, :, :]).then_inc(gate_ready, 1)
                dve.wait_ge(gate_ready, 1)
                dve.tensor_tensor(gate_l[:, :, :], gate_w[:, :, :], gate_h[:, :, :].bitcast(F32), ALU.subtract)\
                    .then_inc(gate_ready, 1)
                split_hi(0)
                for ht in range(2):
                    low_x(dve, bank, xh, xl, xh_ready, xl_ready, ht)

                def route_scores():
                    v = vown.up(dve.memset(score[:, :, :], -1.0))
                    dve.wait_ge(exp_ready, 1)
                    dve.wait_ge(vown.sem, v)
                    v = vown.up(dve.tensor_scalar(e_neg[:, :, :], e_neg[:, :, :], 1.0, None, ALU.add))
                    dve.wait_ge(vown.sem, v)
                    v = vown.up(dve.reciprocal(score[:, :, 0:NE], e_neg[:, :, :]))
                    dve.wait_ge(vown.sem, v)

                def route_top():
                    for t in range(NT):
                        v = vown.up(dve.max(top[:, t, :], score[:, t, :]))
                    dve.wait_ge(vown.sem, v)
                    v = vown.up(dve.memset(top[:, :, TOPK:8], -1.0))
                    dve.wait_ge(vown.sem, v)
                    for t in range(NT):
                        v = vown.up(dve.match_replace(rest[:, t, :], top[:, t, :], score[:, t, :], 0.0))
                    dve.wait_ge(vown.sem, v)

                def route_weights():
                    v = vown.up(dve.tensor_tensor(comb[:, :, :], score[:, :, 0:NE], rest[:, :, 0:NE], ALU.subtract))
                    dve.wait_ge(vown.sem, v)
                    v = vown.up(dve.tensor_reduce(den[:, :], comb[:, :, :], AX, ALU.add))
                    dve.wait_ge(vown.sem, v)
                    v = vown.up(dve.tensor_scalar(den[:, :], den[:, :], 1e-20, None, ALU.add))
                    dve.wait_ge(vown.sem, v)
                    v = vown.up(dve.reciprocal(den[:, :], den[:, :]))
                    dve.wait_ge(vown.sem, v)
                    v = vown.up(dve.tensor_tensor(comb[:, :, :], comb[:, :, :],
                                                  den[:, :].unsqueeze(2).broadcast_to([P, NT, NE]), ALU.mult))
                    for z in range(3):
                        dve.wait_ge(vown.sem, v)
                        v = vown.up(dve.tensor_copy(parts[:, :, z, :], comb[:, :, :]))
                        dve.wait_ge(vown.sem, v)
                        if z < 2:
                            v = vown.up(dve.tensor_tensor(comb[:, :, :], comb[:, :, :], parts[:, :, z, :], ALU.subtract))
                    dve.sem_inc(parts_ready, 1)

                def route_turned():
                    s, rd = un.turn["p", 2 * NSH]
                    dve.wait_ge(un.filled[s], rd + 1)
                    dve.tensor_copy(combT[:, :], bank[s][0:3 * NE, :].bitcast(BF16)).then_inc(combT_ready, 1)
                    dve.wait_ge(combT_ready, 1)
                    dve.sem_inc(un.read[s], 1)

                routing = [route_scores, route_top, route_weights, lambda: None, route_turned]
                assert len(routing) == 2 * NSH + 1
                KTH = int(T * 0.3)
                rounds = -(-KTH // 8)
                assert KTH - 8 * (rounds - 1) == 4
                ranked = {}

                def rank(r, t, replace):
                    src = sim if r == 0 else unranked
                    if replace:
                        dve.wait_ge(vown.sem, ranked[t])
                        ranked[t] = vown.up(dve.match_replace(unranked[:, t, :], kth[:, t, :], src[:, t, :], -3e38))
                    else:
                        if r:
                            dve.wait_ge(vown.sem, ranked[t])
                        ranked[t] = vown.up(dve.max(kth[:, t, :], src[:, t, :]))

                ranking = [(r, t, replace) for r in range(rounds) for replace in (False, True)[:2 if r < rounds - 1 else 1]
                           for t in range(NT)]
                n0 = len(routing)
                per_unit = -(-len(ranking) // (NU - n0))
                for n in range(NU + 1):
                    if n >= n0:
                        for item in ranking[per_unit * (n - n0):per_unit * (n - n0 + 1)]:
                            rank(*item)
                    if n < n0:
                        routing[n]()
                    if n < NU:
                        for q in range(1, NGRP):
                            if n == 2 * first_chunk(q) - 4:
                                split_hi(q)
                        un.product(dve, n)
                    if n >= 1:
                        un.low(dve, n - 1)

            @block.gpsimd
            def _(pool):
                for q in range(NGRP):
                    pool.wait_ge(hi_ready, q + 1)
                    for name in "gud":
                        m = pool.tensor_tensor(lo[q % SPLIT][name][:, :, :], raw[q % RAW][name][:, :, :],
                                               hi[q % SPLIT][name][:, :, :].bitcast(F32), ALU.subtract)
                    m.then_inc(lo_ready, 1)


def early_loads(sp, A, early, gam, loaded):
    sp.dma_start(early[:, 0:512].rearrange("p (s i d) -> p s i d", s=2, i=TPB),
                 A["c_rope1"].rearrange("s (i p) d -> p s i d", p=P)).then_inc(loaded, 16)
    for z, name in enumerate(("q_norm_w", "k_norm_w", "q_norm_b", "k_norm_b")):
        sp.dma_start(early[:, 512 + HD * z:512 + HD * (z + 1)], A["L1_attn_" + name].partition_broadcast(P))\
            .then_inc(loaded, 16)
    sp.dma_start(gam[:, 0:1], A["L1_xattn_gamma_raw"].partition_broadcast(P)).then_inc(loaded, 16)


N_EARLY = 6


def prepare_layer1(nc, cm, A, wA, sim, kth, w1_loaded, early, gam, loaded):
    X, bank, ident = cm.X, cm.bank, cm.ident
    NR = (2 * HQ + 2 * HKV)
    centered = lambda r: r < HQ or 2 * HQ <= r < 2 * HQ + HKV
    keep = ExitStack()

    def sb(name, shape, dt=F32):
        return keep.enter_context(nc.sbuf_tensor(f"P1_{name}", shape, dt))

    def sem(name):
        return keep.enter_context(nc.semaphore(f"P1_{name}"))

    w = Weights()
    w.wqkv_at = next_address(nc)
    wT = sb("wT", [P, KC, NR * P])
    tab = sb("tab", [P, 3, 2, TPB, HD])
    raw = wA[:, :].rearrange("p (r c) -> p r c", c=C)
    wo = wA[:, 0:HQ * C].rearrange("p (h n) -> p h n", h=HQ)
    with ExitStack() as ctx:
        def tmp(name, shape, dt=F32):
            return ctx.enter_context(nc.sbuf_tensor(f"P1_{name}", shape, dt))

        center = tmp("center", [P, P])
        wo_raw = tmp("wo_raw", [P, KC, HQ * HD])
        rope = early[:, 0:512].rearrange("p (s i d) -> p s i d", s=2, i=TPB)
        norm = early[:, 512:1024].rearrange("p (z d) -> p z d", z=4)
        swapped = tmp("swapped", [P, 4, HD])
        sig = tmp("sig", [P, NT, T])
        ln = LayerNorm(lambda name, shape, dt=F32: tmp(name, shape, dt), sem)
        filled, wo_loaded, center_ready = sem("filled"), sem("wo_loaded"), sem("center_ready")
        copied = [sem(f"copied{s}") for s in range(4)]
        sig_tanh, a_ready, a_turned, gam_tanh = sem("sig_tanh"), sem("a_ready"), sem("a_turned"), sem("gam_tanh")
        sig_scaled = sem("sig_scaled")
        pown = Count(sem("pool_own"))
        own = Count(sem("vector_own"))
        NG = NR // 4
        NF = KC * NG + HQ // 2
        groups = (4, 5, 6, 7, 8, 9, 0, 1, 2, 3)
        n_gate = 4 * KC
        w_hi = nc.alloc_sbuf_tensor_at("w1_hi", [P, KC, NR * P], F32R, offset=w.wqkv_at)
        w_lo = nc.alloc_sbuf_tensor_at("w1_lo", [P, 6, KC, 512], F32R, offset=cm.wA_at + 4 * HQ * C)
        hi_copied = sem("hi_copied")

        with nc.Block("prepare1") as block:

            @block.sync
            def _(sp):
                sp.dma_start(wo_raw[:, :, :], A["L1_attn_w_o"].rearrange("(k p) n -> p k n", p=P))\
                    .then_inc(wo_loaded, 16)

            def turn_graph(pe):
                pe.wait_ge(ln.x_new, B)
                for b in range(B):
                    pe.wait_ge(a_ready, TPB * (b + 1))
                    for i in range(TPB):
                        for j in range(TPB):
                            m = pe.transpose(bank[b][:, i * T + j * P:i * T + (j + 1) * P],
                                             sig[:, TPB * b + j, i * P:(i + 1) * P], ident[:, :])
                    m.then_inc(a_turned, 1)

            @block.tensor
            def _(pe):
                pe.wait_ge(center_ready, 1)
                pe.wait_ge(w1_loaded, 4 * 16)
                for z in range(NF):
                    to = bank[4 + z % 4]
                    if z >= 4:
                        pe.wait_ge(copied[z % 4], z // 4)
                    if z < KC * NG:
                        kc = z % KC
                        for s in range(4):
                            r = 4 * groups[z // KC] + s
                            src, dst = raw[:, r, kc * P:(kc + 1) * P], to[:, s * P:(s + 1) * P]
                            if centered(r):
                                m = pe.matmul(dst, src, center[:, :], start=True, stop=True, skip_group_check=True)
                            else:
                                m = pe.transpose(dst, src, ident[:, :])
                    else:
                        if z == KC * NG:
                            turn_graph(pe)
                            pe.wait_ge(wo_loaded, 16)
                        h0 = 2 * (z - KC * NG)
                        for s in range(4):
                            h, nch = h0 + s // 2, s % 2
                            m = pe.transpose(to[:, s * P:(s + 1) * P], wo_raw[:, nch, h * HD:(h + 1) * HD], ident[:, :])
                    m.then_inc(filled, 1)

            split = lambda z: n_gate <= z < KC * NG
            by_scalar = lambda z: z < n_gate or z % 2 == 0
            cols = lambda z: slice(512 * groups[z // KC], 512 * (groups[z // KC] + 1))

            def copy_out(eng, copy, halve, z):
                eng.wait_ge(filled, z + 1)
                if z < n_gate:
                    dst = wT[:, z % KC, cols(z)]
                else:
                    copy = halve
                    h0 = 2 * (z - KC * NG)
                    dst = wo[:, h0:h0 + 2, :].rearrange("p h n -> p (h n)")
                copy(dst, bank[4 + z % 4][:, :]).then_inc(copied[z % 4], 1)

            rstd_before = (1, 2, 4, 6)

            @block.scalar
            def _(act):
                act.preload_act_table_set("natural_log_exp_and_others")
                for z in (z for z in range(NF) if by_scalar(z) or split(z)):
                    if z in rstd_before:
                        ln.rstd(act, rstd_before.index(z))
                    if split(z):
                        act.wait_ge(filled, z + 1)
                        act.activation(w_hi[:, z % KC, cols(z)], bank[4 + z % 4][:, :], ACT.Copy)\
                           .then_inc(hi_copied, 1)
                        if z == KC * NG - 1:
                            act.preload_act_table_set("natural_log_exp_and_others")
                        continue
                    copy_out(act, lambda o, i: act.activation(o, i, ACT.Copy),
                             lambda o, i: act.activation(o, i, ACT.Copy, scale=0.5), z)
                    if z == n_gate - 1:
                        act.preload_act_table_set("exp_and_others")
                        act.wait_ge(loaded, N_EARLY * 16)
                        act.activation(gam[:, 1:2], gam[:, 0:1], ACT.Tanh, scale=0.5).then_inc(gam_tanh, 1)
                        act.activation(sig[:, :, :], sim[:, :, :], ACT.Tanh, scale=0.5).then_inc(sig_tanh, 1)

            @block.vector
            def _(dve):
                dve.tensor_scalar(center[:, :], ident[:, :], -1.0 / P, None, ALU.add).then_inc(center_ready, 1)
                for b in range(B):
                    ln.sums(dve, b, bank[b][:, :].rearrange("p (i c) -> p i c", i=TPB), X, own, None, None)
                    if b >= 1:
                        ln.scale(dve, b - 1, X)
                ln.scale(dve, B - 1, X)
                for z in (z for z in range(NF) if not by_scalar(z) or split(z)):
                    if split(z):
                        dve.wait_ge(hi_copied, z - n_gate + 1)
                        dve.tensor_tensor(w_lo[:, z // KC - 4, z % KC, :], bank[4 + z % 4][:, :],
                                          w_hi[:, z % KC, cols(z)].bitcast(F32), ALU.subtract)\
                           .then_inc(copied[z % 4], 1)
                    else:
                        copy_out(dve, lambda o, i: dve.tensor_copy(o, i),
                                 lambda o, i: dve.tensor_scalar(o, i, 0.5, None, ALU.mult), z)
                    if KC * NG - NT <= z < KC * NG:
                        t = z - (KC * NG - NT)
                        if t == 0:
                            dve.wait_ge(sig_scaled, 1)
                        dve.scalar_tensor_tensor(sig[:, t, :], sim[:, t, :], kth[:, t, 3:4], sig[:, t, :],
                                                 ALU.is_ge, ALU.mult).then_inc(a_ready, 1)
                    if z == KC * NG - 1:
                        for b in range(B):
                            dve.wait_ge(a_turned, b + 1)
                            own.up(dve.tensor_tensor(sim[:, TPB * b:TPB * (b + 1), :],
                                                     bank[b][:, :].rearrange("p (i m) -> p i m", i=TPB),
                                                     sig[:, TPB * b:TPB * (b + 1), :], ALU.add))

            @block.gpsimd
            def _(pool):
                pool.wait_ge(gam_tanh, 1)
                pown.up(pool.tensor_scalar(gam[:, 2:3], gam[:, 1:2], -0.5, 1.5, ALU.mult, ALU.add))
                v = pown.up(pool.tensor_scalar(gam[:, 3:4], gam[:, 1:2], 0.125, 0.125, ALU.mult, ALU.add))
                pool.wait_ge(pown.sem, v)
                pool.wait_ge(sig_tanh, 1)
                pool.tensor_scalar(sig[:, :, :], sig[:, :, :], 1.0, gam[:, 3:4], ALU.add, ALU.mult)\
                    .then_inc(sig_scaled, 1)
                pool.wait_ge(loaded, N_EARLY * 16)
                v = pown.up(pool.tensor_copy(swapped[:, :, :].rearrange("p z (e two) -> p (z e) two", two=2),
                                             norm.rearrange("p z (e two) -> p (z e) two", two=2)[:, :, ::-1]))
                pool.wait_ge(pown.sem, v)
                with nc.sbuf_tensor("P1_b_sin", [P, 2, TPB, HD], F32) as b_sin:
                    for qk in range(2):
                        pown.up(pool.tensor_tensor(tab[:, 0, qk], bcast(norm[:, qk, :], TPB), rope[:, 0], ALU.mult))
                        pown.up(pool.tensor_tensor(tab[:, 1, qk], bcast(swapped[:, qk, :], TPB), rope[:, 1], ALU.mult))
                        pown.up(pool.tensor_tensor(tab[:, 2, qk], bcast(norm[:, 2 + qk, :], TPB), rope[:, 0], ALU.mult))
                        v = pown.up(pool.tensor_tensor(b_sin[:, qk], bcast(swapped[:, 2 + qk, :], TPB), rope[:, 1],
                                                       ALU.mult))
                        pool.wait_ge(pown.sem, v)
                        pown.up(pool.tensor_tensor(tab[:, 2, qk], tab[:, 2, qk], b_sin[:, qk], ALU.add))

    w.wqkv, w.wo, w.bo = wT, wo, None

    def split_weights(kc, g):
        g = g if g < 4 else g + 4
        return w_hi[:, kc, 512 * g:512 * (g + 1)], w_lo[:, groups.index(g) - 4, kc, :]

    w.split = split_weights
    w.qb = early[:, :].rearrange("p (s n) -> p s n", s=2)
    w.cosw = lambda qk, i: tab[:, 0, qk, i, :]
    w.sinw = lambda qk, i: tab[:, 1, qk, i, :]
    w.rotb = lambda qk, i: bcast(tab[:, 2, qk, i, :], 4)
    w.wait_x = w.wait_o = lambda pe: None
    w.wait_split = lambda pe, g: None
    w.graph, w.two_minus_gamma = sim, gam[:, 2:3]
    w.ffn_raw, w.ffn_raw_at = wA[:, HQ * C:HQ * C + 3 * PART], cm.wA_at + 4 * HQ * C
    w.ffn_loaded = nc.alloc_semaphore("ffn_loaded")

    def prefetch(sp):
        for z, name in enumerate(("L1_ffn_W1", "L1_ffn_W3")):
            sp.dma_start(wA[:, 4096 + 2048 * z:6144 + 2048 * z].rearrange("p (r c) -> p r c", c=C),
                         A[name].rearrange("(r p) c -> p r c", p=P)).then_inc(w.ffn_loaded, 16)
        sp.dma_start(wA[:, 8192:10240].rearrange("p (k h) -> p k h", k=KC),
                     A["L1_ffn_W2"].rearrange("(k p) h -> p k h", p=P)).then_inc(w.ffn_loaded, 16)

    w.prefetch = prefetch
    return w, keep


HID = 1024
PART = KC * HID


class DensePreparation:

    def __init__(self, nc, sem, wT, wT_at, raw, raw_at, had, had_at, bank, uses):
        def rounded(name, columns, at):
            return nc.alloc_sbuf_tensor_at(f"dense_{name}", [P, columns], F32R, offset=at)[:, :]

        at = lambda i: wT_at + 4 * PART * i
        flat = wT[:, :, :].rearrange("p k n -> p (k n)")
        part = lambda i: flat[:, PART * i:PART * (i + 1)]
        ups = lambda ap: ap.rearrange("p (k h) -> p k h", k=KC)
        downs = lambda ap: ap.rearrange("p (c d) -> p c d", d=C)
        self.up_h = {n: ups(rounded(f"up_h_{n}", PART, at(2 * i))) for i, n in enumerate("gu")}
        self.up_l = {n: ups(rounded(f"up_l_{n}", PART, at(2 * i + 1))) for i, n in enumerate("gu")}
        self.down_h = downs(rounded("down_h", PART, at(4)))
        self.down_l = downs(rounded("down_l", PART, raw_at + 8 * PART))
        self.raw_up = {"g": raw[:, 0:PART].rearrange("p (r c) -> p r c", c=C),
                       "u": raw[:, PART:2 * PART].rearrange("p (r c) -> p r c", c=C)}
        self.raw_down = raw[:, 2 * PART:3 * PART].rearrange("p (k h) -> p k h", k=KC)
        self.mid = (downs(part(4)), downs(raw[:, 0:PART]))
        self.mid_h, self.mid_l = downs(rounded("mid_h", PART, raw_at + 4 * PART)), downs(rounded("mid_l", PART, raw_at))
        self.had, self.had_r = had, rounded("had_r", P, had_at + 4 * P)
        self.bank, self.uses = bank, uses
        self.fills = [("turn", z) for z in range(4)] + [("up", "g", kc, r) for kc in range(KC) for r in range(2)] + \
            [("up", "u", kc, r) for kc in range(KC) for r in range(2)] + [("had", z) for z in range(4)]
        self.filled = sem("dense_filled")
        self.hi_ready = sem("dense_hi_ready")
        self.read = sem("dense_read")
        self.mid_ready = sem("mid_ready")
        self.had_loaded = sem("had_loaded")
        self.had_ready = sem("had_ready")
        self.own = Count(sem("dense_pool_own"))

    def at(self, r):
        return [f for f in range(len(self.fills)) if (f // 2 if f < 12 else min(f, HQ - 1)) == r]

    def n_split(self, f):
        return sum(x[0] != "turn" for x in self.fills[:f + 1])

    def parts_of(self, f):
        if f[0] == "up":
            _, n, kc, r = f
            return self.up_h[n][:, kc, 512 * r:512 * (r + 1)], self.up_l[n][:, kc, 512 * r:512 * (r + 1)]
        z = f[1]
        return (self.down_h[:, 2 * z:2 * z + 2, :].rearrange("p k d -> p (k d)"),
                self.down_l[:, 2 * z:2 * z + 2, :].rearrange("p k d -> p (k d)"))

    def tensor(self, pe, r, proj_read, loaded, ident):
        for f in self.at(r):
            to = self.bank[f % 2]
            if f < 2:
                pe.wait_ge(proj_read[f % 2], (self.uses + 1 - f % 2) // 2)
                pe.wait_ge(loaded, 3 * 16)
            else:
                pe.wait_ge(self.read, f - 1)
            kind, *at = self.fills[f]
            if kind == "had":
                z = at[0]
                pe.wait_ge(self.mid_ready, 2)
                pe.wait_ge(self.had_ready, 1)
                for p, src in enumerate((self.mid_h, self.mid_l)):
                    m = pe.matmul(to[:, :], self.had_r, src[:, 2 * z:2 * z + 2, :].rearrange("p k d -> p (k d)"),
                                  start=(p == 0), stop=(p == 1))
            else:
                for s in range(4):
                    if kind == "turn":
                        c, dc = 2 * at[0] + s // 2, s % 2
                        src = self.raw_down[:, dc, c * P:(c + 1) * P]
                    else:
                        n, kc, half = at
                        src = self.raw_up[n][:, 4 * half + s, kc * P:(kc + 1) * P]
                    m = pe.transpose(to[:, s * P:(s + 1) * P], src, ident[:, :])
            m.then_inc(self.filled, 1)

    def scalar(self, act, r):
        for f in self.at(r):
            if self.fills[f][0] != "turn":
                act.wait_ge(self.filled, f + 1)
                act.activation(self.parts_of(self.fills[f])[0], self.bank[f % 2][:, :], ACT.Copy)\
                   .then_inc(self.hi_ready, 1)

    def vector(self, dve, r):
        if r == 0:
            dve.wait_ge(self.had_loaded, 16)
            dve.tensor_copy(self.had_r, self.had).then_inc(self.had_ready, 1)
        for f in self.at(r):
            dve.wait_ge(self.filled, f + 1)
            if self.fills[f][0] == "turn":
                z = self.fills[f][1]
                dve.tensor_scalar(self.mid[0][:, 2 * z:2 * z + 2, :].rearrange("p k d -> p (k d)"),
                                  self.bank[f % 2][:, :], HID ** -0.5, None, ALU.mult).then_inc(self.read, 1)
                continue
            hi, lo = self.parts_of(self.fills[f])
            dve.wait_ge(self.hi_ready, self.n_split(f))
            dve.tensor_tensor(lo, self.bank[f % 2][:, :], hi.bitcast(F32), ALU.subtract).then_inc(self.read, 1)

    def butterflies(self, pool):
        pool.wait_ge(self.read, 8)
        for z in range(3):
            a = self.mid[z % 2].rearrange("p (k two s) d -> p k two (s d)", two=2, s=1 << z)
            o = self.mid[(z + 1) % 2].rearrange("p (k two s) d -> p k two (s d)", two=2, s=1 << z)
            self.own.up(pool.tensor_tensor(o[:, :, 0], a[:, :, 0], a[:, :, 1], ALU.add))
            v = self.own.up(pool.tensor_tensor(o[:, :, 1], a[:, :, 0], a[:, :, 1], ALU.subtract))
            pool.wait_ge(self.own.sem, v)
        pool.wait_ge(self.read, 12)
        v = self.own.up(pool.tensor_copy(self.mid_h, self.mid[1]))
        pool.wait_ge(self.own.sem, v)
        pool.sem_inc(self.mid_ready, 1)
        pool.tensor_tensor(self.mid_l, self.mid[1], self.mid_h.bitcast(F32), ALU.subtract).then_inc(self.mid_ready, 1)


def dense_stage(nc, cm, w, A, out, stored):
    X, bank, ident = cm.X, cm.bank, cm.ident
    prep = w.dense
    NC_ = HID // P
    with ExitStack() as ctx:
        def sb(name, shape, dt=F32):
            return ctx.enter_context(nc.sbuf_tensor(f"D_{name}", shape, dt))

        def sem(name):
            return ctx.enter_context(nc.semaphore(f"D_{name}"))

        xh = sb("xh", [P, KC, NT * P], F32R)
        xl = sb("xl", [P, KC, NT * P], F32R)
        ln = LayerNorm(sb, sem)
        ln_attn = LayerNorm(lambda n, s, dt=F32: sb("a" + n, s, dt), lambda n: sem("a" + n), first=B - 1)
        ln_graph = LayerNorm(lambda n, s, dt=F32: sb("g" + n, s, dt), lambda n: sem("g" + n), first=B - 1)

        x_turned = sem("x_turned")
        xh_ready = sem("xh_ready")
        xl_ready = sem("xl_ready")
        vown = Count(sem("vector_own"))
        xbank = [bank[0], bank[1], bank[6], bank[7]]

        def w_up(kind, c, kc):
            return prep.up_h[kind][:, kc, c * P:(c + 1) * P], prep.up_l[kind][:, kc, c * P:(c + 1) * P]

        def w_down(c, dc):
            return prep.down_h[:, c, dc * P:(dc + 1) * P], prep.down_l[:, c, dc * P:(dc + 1) * P]

        un = GatedUnits(sb, sem, NC_, None, bank, xh, xl, w_up, w_down, vown, by_half=True)
        NU = un.NU
        SECOND = 4
        KEEP = NC_ + un.DLAG + 1
        BACK, SUMS, SCALE = KEEP + 1, KEEP + 2, KEEP + 3

        with nc.Block("dense") as block:

            @block.sync
            def _(sp):
                for b in range(B):
                    sp.wait_ge(ln.x_new, b + 1)
                    sp.dma_start(out[b].rearrange("(i p) c -> p i c", p=P), X[:, TPB * b:TPB * (b + 1), :])\
                      .then_inc(stored, 16)
                sp.wait_ge(stored, 16 * B)

            @block.tensor
            def _(pe):
                turn_x(pe, X, xbank, ident, x_turned, 0)
                pe.wait_ge(xl_ready, 2)
                for n in range(NU + un.DLAG):
                    if n == SECOND:
                        pe.wait_ge(ln_graph.x_new, 1)
                        turn_x(pe, X, xbank, ident, x_turned, 1)
                    if n == NC_:
                        pe.wait_ge(xl_ready, 4)
                    if n < NU:
                        un.hidden(pe, n, None)
                    if n >= un.DLAG:
                        un.down(pe, n - un.DLAG)
                    if n == BACK:
                        for b in range(2):
                            un.turn_back(pe, b, bank[4 + b], ident)
                for b in range(2, B):
                    un.turn_back(pe, b, bank[4 + b], ident)

            @block.scalar
            def _(act):
                act.preload_act_table_set("natural_log_exp_and_others")
                high_x(act, xbank, xh, x_turned, xh_ready, 0)
                ln_attn.rstd(act, 0)
                ln_graph.rstd(act, 0)
                for n in range(NU + 1):
                    if n < NU:
                        un.gate(act, n)
                    if n >= 1:
                        un.high(act, n - 1)
                    if n == SECOND:
                        high_x(act, xbank, xh, x_turned, xh_ready, 1)
                    if n == KEEP:
                        un.keep(act, 0)
                    if n == SCALE:
                        for b in range(2):
                            ln.rstd(act, b)
                act.preload_act_table_set("natural_log_exp_and_others")
                un.keep(act, 1)
                for b in range(2, B):
                    ln.rstd(act, b)

            @block.vector
            def _(dve):
                def sums(b):
                    dve.wait_ge(un.y_turned, b + 1)
                    ln.sums(dve, b, bank[4 + b][:, :].rearrange("p (i c) -> p i c", i=TPB), X, vown, None, None)

                low_x(dve, xbank, xh, xl, xh_ready, xl_ready, 0)
                last = slice(TPB * (B - 1), TPB * B)
                ln_attn.sums(dve, 0, bank[7][:, :].rearrange("p (i c) -> p i c", i=TPB), X, vown, None, None)
                ln_attn.scale(dve, 0, X)
                dve.wait_ge(ln_attn.x_new, 1)
                v = vown.up(dve.tensor_scalar(X[:, last, :], X[:, last, :], w.two_minus_gamma, None, ALU.mult))
                dve.wait_ge(vown.sem, v)
                ln_graph.sums(dve, 0, w.graph[:, last, :], X, vown, None, None)
                ln_graph.scale(dve, 0, X)
                for n in range(NU + 1):
                    if n < NU:
                        un.product(dve, n)
                    if n >= 1:
                        un.low(dve, n - 1)
                    if n == SECOND:
                        low_x(dve, xbank, xh, xl, xh_ready, xl_ready, 1)
                    if n == SUMS:
                        for b in range(2):
                            sums(b)
                    if n == SCALE:
                        for b in range(2):
                            ln.scale(dve, b, X)
                sums(2)
                sums(3)
                ln.scale(dve, 2, X)
                ln.scale(dve, 3, X)


class LayerNorm:

    def __init__(self, sb, sem, r=None, turn=0, first=0):
        self.first = first
        self.r, self.turn = r if r is not None else sb("ln_r", [P, 2, TPB, C]), turn
        self.stats = sb("ln_stats", [P, 2, TPB, 6])
        self.mv = sb("ln_mv", [P, 2, TPB, 2])
        self.ve = sb("ln_ve", [P, 2, TPB])
        self.lv = sb("ln_lv", [P, 2, TPB])
        self.rs = sb("ln_rs", [P, 2, TPB])
        self.var_ready = sem("ln_var_ready")
        self.log_ready = sem("ln_log_ready")
        self.rstd_ready = sem("ln_rstd_ready")
        self.x_new = sem("x_new")

    def sums(self, dve, n, y, X, own, y_read, bias):
        r = self.r[:, (n + self.turn) % 2]
        t0 = TPB * (self.first + n)
        Xb = X[:, t0:t0 + TPB, :]
        if n >= 2:
            dve.wait_ge(self.x_new, n - 1)
        v = own.up(dve.tensor_tensor(r, y, Xb, ALU.add))
        dve.wait_ge(own.sem, v)
        if y_read is not None:
            dve.sem_inc(y_read, 1)
        if bias is not None:
            v = own.up(dve.tensor_tensor(r, r, bcast(bias[:, :], TPB), ALU.add))
            dve.wait_ge(own.sem, v)
        for i in range(TPB):
            v = own.up(dve.bn_stats(self.stats[:, n % 2, i, :], r[:, i, :]))
        dve.wait_ge(own.sem, v)
        for i in range(TPB):
            v = own.up(dve.bn_aggr(self.mv[:, n % 2, i, :], self.stats[:, n % 2, i, :]))
        dve.wait_ge(own.sem, v)
        dve.tensor_scalar(self.ve[:, n % 2, :], self.mv[:, n % 2, :, 1], LN_EPS, None, ALU.add)\
            .then_inc(self.var_ready, 1)

    def rstd(self, act, n):
        act.wait_ge(self.var_ready, n + 1)
        act.activation(self.lv[:, n % 2, :], self.ve[:, n % 2, :], ACT.Ln).then_inc(self.log_ready, 1)
        act.wait_ge(self.log_ready, n + 1)
        act.activation(self.rs[:, n % 2, :], self.lv[:, n % 2, :], ACT.Exp, scale=-0.5).then_inc(self.rstd_ready, 1)

    def scale(self, dve, n, X):
        dve.wait_ge(self.rstd_ready, n + 1)
        for i in range(TPB):
            m = dve.tensor_scalar(X[:, TPB * (self.first + n) + i, :], self.r[:, (n + self.turn) % 2, i, :], self.mv[:, n % 2, i, 0:1],
                                  self.rs[:, n % 2, i:i + 1], ALU.subtract, ALU.mult)
        m.then_inc(self.x_new, 1)


NBIAS = -(-(3072 + C) // 512)


class Weights:
    pass


def release_semaphores(nc, cm):
    nc.clear_and_free_semaphores(cm.stage_sems)
    nc.all_engine_barrier()
    cm.stage_sems = []


def decoder(nc, A, out, stages=6):
    with ExitStack() as ctx:
        def sb(name, shape, dt=F32):
            return ctx.enter_context(nc.sbuf_tensor(name, shape, dt))

        def sem(name):
            return ctx.enter_context(nc.semaphore(name))

        cm = Common()
        cm.stage_sems = []
        cm.X = X = sb("X", [P, NT, C])
        cm.ident = sb("ident", [P, P])
        cm.identb = sb("identb", [P, P], BF16)
        cm.maskb = sb("maskb", [P, P], BF16)
        cm.headmask = sb("headmask", [P, 4])
        cm.bank = [ctx.enter_context(nc.psum_tensor(f"bank{i}", [P, 512], F32)) for i in range(8)]
        x_loaded = sem("x_loaded")
        ctx_loaded = sem("ctx_loaded")
        bias_loaded = sem("bias_loaded")
        wo0_loaded = sem("wo0_loaded")
        w0_loaded = [sem(f"w0_loaded{g}") for g in range(6)]
        rope_loaded = sem("rope_loaded")
        stored = sem("stored")
        cm.wA_at = next_address(nc)
        wA = sb("wA", [P, 10240])

        w0 = Weights()
        wqkv0 = wA[:, 0:6144].rearrange("p (k n) -> p k n", k=KC)
        wo0 = wA[:, 6144:10240].rearrange("p (h n) -> p h n", h=HQ)

        sim = sb("sim", [P, NT, T])
        kth = sb("kth", [P, NT, 8])
        early = sb("early", [P, 1024])
        gam = sb("gam", [P, 4])
        l0x = ExitStack()
        moe = ExitStack()
        kstack = l0x.enter_context(nc.sbuf_tensor("kstack", [P, NT, 256], F32))
        vstack = l0x.enter_context(nc.sbuf_tensor("vstack", [P, NT, 8, 32], F32))
        with ExitStack() as l0:
            brow = l0.enter_context(nc.sbuf_tensor("brow", [P, 3072 + C], F32))
            w0_hi = l0.enter_context(nc.sbuf_tensor("w0_hi", [P, KC, 3072], F32R))
            w0_lo = nc.alloc_sbuf_tensor_at("w0_lo", [P, KC, 3072], F32R, offset=cm.wA_at)
            w0_high, w0_low = [sem(f"w0_high{g}") for g in range(6)], [sem(f"w0_low{g}") for g in range(6)]
            rope = l0.enter_context(nc.sbuf_tensor("rope", [P, 2, TPB, HD], F32))
            ones1 = l0.enter_context(nc.sbuf_tensor("ones1", [1, P], F32))
            ctxs = l0.enter_context(nc.sbuf_tensor("ctxs", [P, NT, 64], F32))
            c_hi = l0.enter_context(nc.sbuf_tensor("c_hi", [P, NT, 64], F32R))
            gw = l0.enter_context(nc.sbuf_tensor("gw", [64, 2, 64], F32))
            gwT = l0.enter_context(nc.sbuf_tensor("gwT", [64, 2, 64], F32))
            stack_clear = sem("stack_clear")
            ctx_turned, w_turned, gw_ready, ctxT_ready = map(sem, ("ctx_turned", "w_turned", "gw_ready", "ctxT_ready"))
            bias_spread, bias_read, ones_ready = map(sem, ("bias_spread", "bias_read", "ones_ready"))
            gq_done, gq_ready, similar = map(sem, ("gq_done", "gq_ready", "similar"))
            bank = cm.bank
            tmp0 = ExitStack()
            bias1 = tmp0.enter_context(nc.sbuf_tensor("bias1", [1, 3072 + C], F32))
            ctxT = tmp0.enter_context(nc.sbuf_tensor("ctxT", [64, NT * P], F32))
            gqT = tmp0.enter_context(nc.sbuf_tensor("gqT", [64, 2, NT * P], F32))
            EARLY, w0.late = (4, 0, 1), (2, 3, 5)
            cols = lambda g: slice(512 * g, 512 * (g + 1))

            def high(eng, g):
                eng.wait_ge(w0_loaded[g], 16)
                eng.activation(w0_hi[:, :, cols(g)], wqkv0[:, :, cols(g)], ACT.Copy).then_inc(w0_high[g], 1)

            def low(eng, g):
                eng.wait_ge(w0_high[g], 1)
                eng.tensor_tensor(w0_lo[:, :, cols(g)], wqkv0[:, :, cols(g)], w0_hi[:, :, cols(g)].bitcast(F32),
                                  ALU.subtract).then_inc(w0_low[g], 1)

            def wait_split(pe, g):
                pe.wait_ge(w0_high[g], 1)
                pe.wait_ge(w0_low[g], 1)

            w0.high, w0.low = high, low
            w0.split = lambda kc, g: (w0_hi[:, kc, cols(g)], w0_lo[:, kc, cols(g)])
            with nc.Block("prepare0") as block:

                @block.sync
                def _(sp):
                    sp.dma_start(cm.ident[:, :], A["c_ident"]).then_inc(ctx_loaded, 16)
                    sp.dma_start(ctxs[:, :, :], A["ctx_512"].rearrange("b (i p) c -> p (b i) c", p=P))\
                        .then_inc(ctx_loaded, 16)
                    for z, name in enumerate(("L1_xattn_Wq", "L1_xattn_Wk")):
                        sp.dma_start(gw[:, z, :], A[name]).then_inc(ctx_loaded, 16)
                    off = 0
                    for name, n in (("L0_attn_bq", 2048), ("L0_attn_bk", 512), ("L0_attn_bv", 512), ("L0_attn_bo", C)):
                        sp.dma_start(bias1[:, off:off + n], A[name].unsqueeze(0)).then_inc(bias_loaded, 16)
                        off += n
                    sp.dma_start(X[:, :, :], A["x"].rearrange("b (i p) c -> p (b i) c", p=P)).then_inc(x_loaded, 16)
                    for g in (4, 0, 1, 2, 3, 5):
                        src = A["L0_attn_W" + ("q" if g < 4 else "kv"[g - 4])].rearrange("(k p) n -> p k n", p=P)
                        if g < 4:
                            src = src[:, :, 512 * g:512 * (g + 1)]
                        sp.dma_start(wqkv0[:, :, 512 * g:512 * (g + 1)], src).then_inc(w0_loaded[g], 16)
                        if g == 4:
                            sp.dma_start(rope[:, :, :, :], A["c_rope0"].rearrange("s (i p) d -> p s i d", p=P))\
                              .then_inc(rope_loaded, 16)
                            for dst, name in ((cm.identb, "c_identb"), (cm.maskb, "c_maskb"),
                                              (cm.headmask, "c_headmask")):
                                sp.dma_start(dst[:, :], A[name]).then_inc(rope_loaded, 16)
                    sp.dma_start(wo0, A["L0_attn_Wo"].rearrange("(h d) n -> d h n", d=HD)).then_inc(wo0_loaded, 16)

                @block.scalar
                def _(act):
                    act.preload_act_table_set("natural_log_exp_and_others")
                    for ht in range(2):
                        act.wait_ge(ctx_turned, ht + 1)
                        act.activation(ctxT[:, ht * 512:(ht + 1) * 512], bank[4 + ht][0:64, :], ACT.Copy)\
                           .then_inc(ctxT_ready, 1)
                    for z in range(2):
                        for ht in range(2):
                            act.wait_ge(gq_done, 2 * z + ht + 1)
                            act.activation(gqT[:, z, ht * 512:(ht + 1) * 512], bank[4 + ht if z == 0 else 6 + ht][0:64, :],
                                           ACT.Copy).then_inc(gq_ready, 1)
                    for g in EARLY:
                        high(act, g)
                    for c in range(NBIAS):
                        act.wait_ge(bias_spread, c + 1)
                        n = min(512, 3072 + C - 512 * c)
                        act.activation(brow[:, 512 * c:512 * c + n], bank[4 + c % 4][:, 0:n], ACT.Copy)\
                           .then_inc(bias_read, 1)

                @block.gpsimd
                def _(pool):
                    pool.memset(ones1[:, :], 1.0).then_inc(ones_ready, 1)
                    pool.memset(kstack[:, :, :], 0.0).then_inc(stack_clear, 1)
                    pool.memset(vstack[:, :, :, :], 0.0).then_inc(stack_clear, 1)

                @block.vector
                def _(dve):
                    own = Count(sem("prep_vector_own"))
                    dve.wait_ge(ctx_loaded, 4 * 16)
                    v = own.up(dve.tensor_copy(c_hi[:, :, :], ctxs[:, :, :]))
                    dve.wait_ge(own.sem, v)
                    dve.wait_ge(stack_clear, 2)
                    ks = kstack[:, :, :].rearrange("p t (h w) -> p (t h) w", w=32)
                    vs = vstack[:, :, :, :].rearrange("p t h w -> p (t h) w")
                    hi = c_hi[:, :, :].bitcast(F32).rearrange("p t (h d) -> p (t h) d", d=8)
                    cs = ctxs[:, :, :].rearrange("p t (h d) -> p (t h) d", d=8)
                    dve.tensor_copy(ks[:, :, 0:8], hi)
                    dve.tensor_tensor(ks[:, :, 8:16], cs, hi, ALU.subtract)
                    dve.tensor_copy(ks[:, :, 16:24], hi)
                    dve.memset(ks[:, :, 24:25], 1.0)
                    dve.tensor_copy(vs[:, :, 0:8], cs)
                    dve.memset(vs[:, :, 8:9], 1.0)
                    dve.wait_ge(w_turned, 1)
                    dve.tensor_copy(gwT[:, :, :], bank[6][0:64, 0:128].rearrange("p (k n) -> p k n", k=2))\
                        .then_inc(gw_ready, 1)
                    for b in range(B):
                        dve.wait_ge(similar, b + 1)
                        m = dve.tensor_scalar(sim[:, TPB * b:TPB * (b + 1), :].rearrange("p i m -> p (i m)"),
                                              bank[b][:, :], 1.0 / 16, None, ALU.mult)
                    for g in EARLY:
                        low(dve, g)
                    dve.wait_ge(rope_loaded, 4 * 16)

                @block.tensor
                def _(pe):
                    pe.wait_ge(ctx_loaded, 4 * 16)
                    for t in range(NT):
                        m = pe.transpose(bank[4 + t // 4][0:64, (t % 4) * P:(t % 4 + 1) * P], ctxs[:, t, :],
                                         cm.ident[:, :])
                        if t % 4 == 3:
                            m.then_inc(ctx_turned, 1)
                    for z in range(2):
                        m = pe.transpose(bank[6][0:64, z * 64:(z + 1) * 64], gw[:, z, :], cm.ident[0:64, 0:64])
                    m.then_inc(w_turned, 1)
                    pe.wait_ge(gw_ready, 1)
                    pe.wait_ge(ctxT_ready, 2)
                    for z in range(2):
                        for ht in range(2):
                            m = pe.matmul(bank[4 + ht if z == 0 else 6 + ht][0:64, :], gwT[:, z, :],
                                          ctxT[:, ht * 512:(ht + 1) * 512], start=True, stop=True)
                            m.then_inc(gq_done, 1)
                    pe.wait_ge(gq_ready, 4)
                    for b in range(B):
                        for i in range(TPB):
                            m = pe.matmul(bank[b][:, i * T:(i + 1) * T], gqT[:, 0, b * T + i * P:b * T + (i + 1) * P],
                                          gqT[:, 1, b * T:(b + 1) * T], start=True, stop=True, skip_group_check=True)
                        m.then_inc(similar, 1)
                    pe.wait_ge(bias_loaded, 4 * 16)
                    pe.wait_ge(ones_ready, 1)
                    for c in range(NBIAS):
                        if c >= 4:
                            pe.wait_ge(bias_read, c - 3)
                        n = min(512, 3072 + C - 512 * c)
                        pe.matmul(bank[4 + c % 4][:, 0:n], ones1[:, :], bias1[:, 512 * c:512 * c + n],
                                  start=True, stop=True).then_inc(bias_spread, 1)

            tmp0.close()
            w0.wo, w0.bo = wo0, brow[:, 3072:3072 + C]
            w0.bias = brow
            w0.cosw = lambda qk, i: rope[:, 0, i, :]
            w0.sinw = lambda qk, i: rope[:, 1, i, :]
            w0.prefetch = lambda sp: None
            w0.wait_x = lambda pe: pe.wait_ge(x_loaded, 16)
            w0.wait_split = wait_split
            w0.wait_o = lambda pe: pe.wait_ge(wo0_loaded, 16)
            attention_stage(nc, 0, cm, w0, A)
        release_semaphores(nc, cm)
        if stages >= 2:
            raw = [{n: moe.enter_context(nc.sbuf_tensor(f"raw_{n}{s}", [P, GCH if n == "d" else KC,
                                                                        C if n == "d" else GW], F32)) for n in "gud"}
                   for s in range(RAW)]
            raw_loaded = [sem(f"raw_loaded{s}") for s in range(RAW)]
            gate_w = moe.enter_context(nc.sbuf_tensor("gate_w", [P, KC, NE], F32))
            sel = moe.enter_context(nc.sbuf_tensor("sel", [3 * NE, NCH * P], BF16))
            small_loaded = sem("small_loaded")

            def prefetch0(sp):
                sp.dma_start(gate_w[:, :, :], A["L0_ffn_gate_w"].rearrange("(k p) e -> p k e", p=P))\
                  .then_inc(small_loaded, 16)
                sp.dma_start(sel[:, :], A["c_sel"]).then_inc(small_loaded, 16)
                for q in range(RAW):
                    moe_load(sp, A, q, raw, raw_loaded)

            cross_attention_stage(nc, cm, kstack, vstack, prefetch0, lambda pool: pad_shared(pool, raw, Count(sem("pad_own"))))
        w1_loaded = sem("w1_loaded")
        early_loaded = sem("early_loaded")
        if stages >= 3:
            def prefetch1(sp):
                early_loads(sp, A, early, gam, early_loaded)
                for r in range(4):
                    sp.dma_start(wA[:, 2560 * r:2560 * (r + 1)].rearrange("p (r c) -> p r c", c=C),
                                 A["L1_attn_w_qkv"][1280 * r:1280 * (r + 1), :].rearrange("(r p) c -> p r c", p=P))\
                        .then_inc(w1_loaded, 16)

            moe_stage(nc, cm, A, raw, raw_loaded, gate_w, sel, small_loaded, sim, kth, kstack, prefetch1)
            release_semaphores(nc, cm)
        moe.close()
        l0x.close()
        if stages >= 4:
            w1, keep1 = prepare_layer1(nc, cm, A, wA, sim, kth, w1_loaded, early, gam, early_loaded)
            attention_stage(nc, 1, cm, w1, A)
            release_semaphores(nc, cm)
            if stages >= 6:
                dense_stage(nc, cm, w1, A, out, stored)
            keep1.close()

        if stages < 6:
            with nc.Block("store") as block:
                @block.sync
                def _(sp):
                    sp.dma_start(out.rearrange("b (i p) c -> p (b i) c", p=P), X[:, :, :]).then_inc(stored, 16)
                    sp.wait_ge(stored, 16)


def constants():
    bf = np.dtype("bfloat16")
    k = {"c_ident": np.eye(P, dtype=np.float32), "c_identb": np.eye(P, dtype=np.float32).astype(bf),
         "c_maskb": np.triu(np.full((P, P), MASKED, np.float32), 1).astype(bf)}
    had = np.ones((1, 1), np.float32)
    while len(had) < P:
        had = np.block([[had, had], [had, -had]])
    k["c_hadamard"] = had.astype(np.float32)
    sel = np.zeros((3 * NE, NCH * P), np.float32)
    for z in range(3):
        sel[z * NE + np.arange(NCH * P) // FE, np.arange(NCH * P)] = 1
    k["c_sel"] = sel.astype(bf)
    k["c_headmask"] = np.repeat(np.eye(4, dtype=np.float32), 32, axis=0)
    for layer, base in ((0, 10000.0), (1, 1000000.0)):
        inv = (1.0 / np.float32(base) ** (np.arange(0, HD, 2, dtype=np.float32) / np.float32(HD))).astype(np.float32)
        f = (np.arange(T, dtype=np.float32)[:, None] * inv[None, :]).astype(np.float32)
        c, s = np.cos(f), np.sin(f)
        cc = np.repeat(c, 2, axis=1)
        ss = np.stack([-s, s], axis=-1).reshape(T, HD)
        k[f"c_rope{layer}"] = np.stack([cc, ss]).astype(np.float32)
    return k


_INS = ['x', 'ctx_512', 'L0_attn_Wq', 'L0_attn_bq', 'L0_attn_Wk', 'L0_attn_bk', 'L0_attn_Wv', 'L0_attn_bv',
        'L0_attn_Wo', 'L0_attn_bo', 'L0_ffn_gate_w', 'L0_ffn_wg', 'L0_ffn_wu', 'L0_ffn_wd', 'L0_ffn_sg',
        'L0_ffn_su', 'L0_ffn_sd', 'L1_attn_w_qkv', 'L1_attn_w_o', 'L1_attn_q_norm_w', 'L1_attn_q_norm_b',
        'L1_attn_k_norm_w', 'L1_attn_k_norm_b', 'L1_xattn_Wq', 'L1_xattn_Wk', 'L1_xattn_gamma_raw', 'L1_ffn_W1',
        'L1_ffn_W2', 'L1_ffn_W3']


def kernel(**inputs):
    import numpy as _np
    import concourse.bacc as _bacc
    from concourse import mybir as _mybir
    from concourse.bass_utils import run_bass_kernel_spmd as _run

    nc = _bacc.Bacc("TRN2", target_bir_lowering=False, num_devices=1)
    arrays, A = {}, {}
    for name in _INS:
        a = _np.ascontiguousarray(inputs[name])
        if name == "L1_xattn_gamma_raw":
            a = a.reshape(1)
        arrays[f"in_{name}"] = a
    for name, a in constants().items():
        arrays[f"in_{name}"] = a
    for name, a in arrays.items():
        A[name[3:]] = nc.dram_tensor(name, a.shape, _mybir.dt.from_np(a.dtype), kind="ExternalInput").ap()
    out = nc.dram_tensor("out", (B, T, C), F32, kind="ExternalOutput").ap()
    decoder(nc, A, out)
    r = _run(nc, [arrays], core_ids=[0])
    return r.results[0]["out"]
```
